# Optimizing a Trainium2 kernel written in Bass

```python
import numpy as np
import jax
import jax.numpy as jnp

def _softmax(x, axis=-1):
    return jax.nn.softmax(x, axis=axis)

def _gelu(x):
    return jax.nn.gelu(x, approximate=True)

def _silu(x):
    return jax.nn.silu(x)

def _sigmoid(x):
    return jax.nn.sigmoid(x)

def _layernorm(x, axis=-1, eps=1e-05):
    m = jnp.mean(x, axis=axis, keepdims=True)
    v = jnp.var(x, axis=axis, keepdims=True)
    return (x - m) / jnp.sqrt(v + eps)

def _scatter_add(tgt, idx, src, axis=0):
    return tgt.at[idx].add(src)

def _segment_sum(src, seg, n):
    return jax.ops.segment_sum(src, seg, n)
kernel_name = 'mk_sandwich_d2_jaxref_r8_67a172'

def setup_inputs(seed: int=0):
    np.random.seed(seed)
    _w = jnp.asarray

    def _L0_attn_setup():
        import jax, jax.numpy as jnp
        import numpy as np
        import math
        DIM = 128
        WINDOW = 16
        NUM_HEADS = 16
        HEAD_DIM = DIM // NUM_HEADS
        SCALE = math.sqrt(HEAD_DIM)
        LN_EPS = 1e-05

        def _gather_window(z, W):
            B, T, H, C = z.shape
            t = jnp.arange(T)[:, None]
            w = jnp.arange(W)[None, :]
            idx = t - 1 - w
            valid = idx >= 0
            idxc = jnp.clip(idx, 0, T - 1)
            nb = z[:, idxc]
            nb = jnp.where(valid[None, :, :, None, None], nb, jnp.zeros((), z.dtype))
            return nb.transpose(0, 1, 3, 2, 4)
        key = jax.random.key(seed)
        k0, k1, k2, k3 = jax.random.split(key, 4)
        B, T, D = (2, 512, DIM)
        x = jax.random.normal(k0, (B, T, D), dtype=jnp.float32)
        wq = jax.random.normal(k1, (D, D), dtype=jnp.float32) * 0.02
        wkv = jax.random.normal(k2, (2 * D, D), dtype=jnp.float32) * 0.02
        wo = jax.random.normal(k3, (D, D), dtype=jnp.float32) * 0.02
        gamma = jnp.ones((D,), dtype=jnp.float32)
        beta = jnp.zeros((D,), dtype=jnp.float32)
        return {'x': x, 'wq': wq, 'wkv': wkv, 'wo': wo, 'gamma': gamma, 'beta': beta}
    _L0_attn_in = _L0_attn_setup()

    def _L0_ffn_setup():
        import jax, jax.numpy as jnp
        import numpy as np
        H = 16
        E = 8
        EPS = 1e-05

        def _layernorm(x, g, b):
            mu = jnp.mean(x, axis=-1, keepdims=True)
            var = jnp.mean(jnp.square(x - mu), axis=-1, keepdims=True)
            return (x - mu) * jax.lax.rsqrt(var + EPS) * g + b
        key = jax.random.key(seed)
        T, B, C = (128, 8, 128)
        ks = jax.random.split(key, 12)
        s = 0.02
        return {'x': jax.random.normal(ks[0], (T, B, C), jnp.float32), 'in_proj_w': jax.random.normal(ks[1], (3 * C, C), jnp.float32) * s, 'in_proj_b': jnp.zeros((3 * C,), jnp.float32), 'out_w': jax.random.normal(ks[2], (C, C), jnp.float32) * s, 'out_b': jnp.zeros((C,), jnp.float32), 'ln1_g': jnp.ones((C,), jnp.float32), 'ln1_b': jnp.zeros((C,), jnp.float32), 'router_w': jax.random.normal(ks[3], (E, C), jnp.float32) * s, 'router_b': jnp.zeros((E,), jnp.float32), 'w1': jax.random.normal(ks[4], (E, C, C), jnp.float32) * s, 'b1': jnp.zeros((E, C), jnp.float32), 'w2': jax.random.normal(ks[5], (E, C, C), jnp.float32) * s, 'b2': jnp.zeros((E, C), jnp.float32), 'ln2_g': jnp.ones((C,), jnp.float32), 'ln2_b': jnp.zeros((C,), jnp.float32)}
    _L0_ffn_in = _L0_ffn_setup()

    def _L1_attn_setup():
        import jax, jax.numpy as jnp
        import numpy as np
        D_MODEL = 128
        D_STATE = 16
        D_CONV = 4
        LN_EPS = 1e-05

        def _layernorm(x, g, b):
            mu = jnp.mean(x, axis=-1, keepdims=True)
            var = jnp.mean(jnp.square(x - mu), axis=-1, keepdims=True)
            return (x - mu) * jax.lax.rsqrt(var + LN_EPS) * g + b

        def _causal_depthwise_conv(x, w, b):
            xc = jnp.transpose(x, (0, 2, 1))
            K = w.shape[-1]
            out = jax.lax.conv_general_dilated(xc, w, window_strides=(1,), padding=[(K - 1, 0)], dimension_numbers=('NCH', 'OIH', 'NCH'), feature_group_count=x.shape[-1])
            return jnp.transpose(out, (0, 2, 1)) + b

        def _ssm_scan(x, dt, Bm, Cm, A):
            Bsz, T, DI = x.shape
            DS = Bm.shape[-1]
            h0 = jnp.zeros((Bsz, DI, DS), jnp.float32)

            def step(h, inp):
                xt, dtt, bt, ct = inp
                decay = jnp.exp(jnp.minimum(dtt * A, 0.0))
                h = h * decay[..., None] + (dtt * xt)[..., None] * bt[:, None, :]
                y = jnp.einsum('bds,bs->bd', h, ct)
                return (h, y)
            xs = (jnp.swapaxes(x, 0, 1), jnp.swapaxes(dt, 0, 1), jnp.swapaxes(Bm, 0, 1), jnp.swapaxes(Cm, 0, 1))
            _, ys = jax.lax.scan(step, h0, xs)
            return jnp.swapaxes(ys, 0, 1)
        key = jax.random.key(seed)
        ks = jax.random.split(key, 12)
        B, T, D = (2, 256, D_MODEL)
        DI, DS, K = (D_MODEL, D_STATE, D_CONV)
        s = lambda k, shape, fan: jax.random.normal(k, shape, dtype=jnp.float32) * (1.0 / np.sqrt(fan))
        return {'x': jax.random.normal(ks[0], (B, T, D), dtype=jnp.float32), 'ln_g': jnp.ones((D,), jnp.float32), 'ln_b': jnp.zeros((D,), jnp.float32), 'W_in': s(ks[1], (D, 2 * DI), D), 'conv_w': s(ks[2], (DI, 1, K), K), 'conv_b': jnp.zeros((DI,), jnp.float32), 'dt_w': s(ks[3], (DI, DI), DI), 'dt_b': jnp.zeros((DI,), jnp.float32), 'B_w': s(ks[4], (DI, DS), DI), 'C_w': s(ks[5], (DI, DS), DI), 'log_A': jnp.log(jnp.linspace(1.0, 16.0, DI)).astype(jnp.float32), 'D_param': jnp.ones((DI,), jnp.float32), 'W_out': s(ks[6], (DI, D), DI)}
    _L1_attn_in = _L1_attn_setup()

    def _L1_ffn_setup():
        import jax, jax.numpy as jnp
        import numpy as np
        D_IN, D_HID = (128, 512)

        def _ternary(key, shape):
            return jax.random.randint(key, shape, -1, 2).astype(jnp.float32)

        def _tlin(x, w, s):
            return jnp.einsum('bsi,oi->bso', x, w) * s
        key = jax.random.key(seed)
        ks = jax.random.split(key, 12)
        inv = lambda fan: 1.0 / np.sqrt(fan).astype(np.float32)
        return {'x': jax.random.normal(ks[0], (4, 256, D_IN), dtype=jnp.float32), 'w1_w': _ternary(ks[1], (D_HID, D_IN)), 'w1_s': jax.random.uniform(ks[2], (D_HID,), dtype=jnp.float32) * inv(D_IN), 'w2_w': _ternary(ks[3], (D_HID, D_IN)), 'w2_s': jax.random.uniform(ks[4], (D_HID,), dtype=jnp.float32) * inv(D_IN), 'h1_w': _ternary(ks[5], (D_HID, D_HID)), 'h1_s': jax.random.uniform(ks[6], (D_HID,), dtype=jnp.float32) * inv(D_HID), 'h2_w': _ternary(ks[7], (D_HID, D_HID)), 'h2_s': jax.random.uniform(ks[8], (D_HID,), dtype=jnp.float32) * inv(D_HID), 'w3_w': _ternary(ks[9], (D_IN, D_HID)), 'w3_s': jax.random.uniform(ks[10], (D_IN,), dtype=jnp.float32) * inv(D_HID)}
    _L1_ffn_in = _L1_ffn_setup()
    _d = {'L0_attn_x': _L0_attn_in['x'], 'L0_attn_wq': _L0_attn_in['wq'], 'L0_attn_wkv': _L0_attn_in['wkv'], 'L0_attn_wo': _L0_attn_in['wo'], 'L0_attn_gamma': _L0_attn_in['gamma'], 'L0_attn_beta': _L0_attn_in['beta'], 'L0_ffn_in_proj_w': _L0_ffn_in['in_proj_w'], 'L0_ffn_in_proj_b': _L0_ffn_in['in_proj_b'], 'L0_ffn_out_w': _L0_ffn_in['out_w'], 'L0_ffn_out_b': _L0_ffn_in['out_b'], 'L0_ffn_ln1_g': _L0_ffn_in['ln1_g'], 'L0_ffn_ln1_b': _L0_ffn_in['ln1_b'], 'L0_ffn_router_w': _L0_ffn_in['router_w'], 'L0_ffn_router_b': _L0_ffn_in['router_b'], 'L0_ffn_w1': _L0_ffn_in['w1'], 'L0_ffn_b1': _L0_ffn_in['b1'], 'L0_ffn_w2': _L0_ffn_in['w2'], 'L0_ffn_b2': _L0_ffn_in['b2'], 'L0_ffn_ln2_g': _L0_ffn_in['ln2_g'], 'L0_ffn_ln2_b': _L0_ffn_in['ln2_b'], 'L1_attn_ln_g': _L1_attn_in['ln_g'], 'L1_attn_ln_b': _L1_attn_in['ln_b'], 'L1_attn_W_in': _L1_attn_in['W_in'], 'L1_attn_conv_w': _L1_attn_in['conv_w'], 'L1_attn_conv_b': _L1_attn_in['conv_b'], 'L1_attn_dt_w': _L1_attn_in['dt_w'], 'L1_attn_dt_b': _L1_attn_in['dt_b'], 'L1_attn_B_w': _L1_attn_in['B_w'], 'L1_attn_C_w': _L1_attn_in['C_w'], 'L1_attn_log_A': _L1_attn_in['log_A'], 'L1_attn_D_param': _L1_attn_in['D_param'], 'L1_attn_W_out': _L1_attn_in['W_out'], 'L1_ffn_w1_w': _L1_ffn_in['w1_w'], 'L1_ffn_w1_s': _L1_ffn_in['w1_s'], 'L1_ffn_w2_w': _L1_ffn_in['w2_w'], 'L1_ffn_w2_s': _L1_ffn_in['w2_s'], 'L1_ffn_h1_w': _L1_ffn_in['h1_w'], 'L1_ffn_h1_s': _L1_ffn_in['h1_s'], 'L1_ffn_h2_w': _L1_ffn_in['h2_w'], 'L1_ffn_h2_s': _L1_ffn_in['h2_s'], 'L1_ffn_w3_w': _L1_ffn_in['w3_w'], 'L1_ffn_w3_s': _L1_ffn_in['w3_s']}
    _x0 = _d['L0_attn_x']
    _d['L0_attn_x'] = jax.random.normal(jax.random.fold_in(jax.random.key(seed), 1), (16, 256, 128), dtype=_x0.dtype)
    del _x0
    return _d

def reference(L0_attn_x, L0_attn_wq, L0_attn_wkv, L0_attn_wo, L0_attn_gamma, L0_attn_beta, L0_ffn_in_proj_w, L0_ffn_in_proj_b, L0_ffn_out_w, L0_ffn_out_b, L0_ffn_ln1_g, L0_ffn_ln1_b, L0_ffn_router_w, L0_ffn_router_b, L0_ffn_w1, L0_ffn_b1, L0_ffn_w2, L0_ffn_b2, L0_ffn_ln2_g, L0_ffn_ln2_b, L1_attn_ln_g, L1_attn_ln_b, L1_attn_W_in, L1_attn_conv_w, L1_attn_conv_b, L1_attn_dt_w, L1_attn_dt_b, L1_attn_B_w, L1_attn_C_w, L1_attn_log_A, L1_attn_D_param, L1_attn_W_out, L1_ffn_w1_w, L1_ffn_w1_s, L1_ffn_w2_w, L1_ffn_w2_s, L1_ffn_h1_w, L1_ffn_h1_s, L1_ffn_h2_w, L1_ffn_h2_s, L1_ffn_w3_w, L1_ffn_w3_s):

    def _L0_attn_ref(x, wq, wkv, wo, gamma, beta):
        import jax, jax.numpy as jnp
        import numpy as np
        import math
        DIM = 128
        WINDOW = 16
        NUM_HEADS = 16
        HEAD_DIM = DIM // NUM_HEADS
        SCALE = math.sqrt(HEAD_DIM)
        LN_EPS = 1e-05

        def _gather_window(z, W):
            B, T, H, C = z.shape
            t = jnp.arange(T)[:, None]
            w = jnp.arange(W)[None, :]
            idx = t - 1 - w
            valid = idx >= 0
            idxc = jnp.clip(idx, 0, T - 1)
            nb = z[:, idxc]
            nb = jnp.where(valid[None, :, :, None, None], nb, jnp.zeros((), z.dtype))
            return nb.transpose(0, 1, 3, 2, 4)
        B, T, D = x.shape
        H, HD, W = (NUM_HEADS, HEAD_DIM, WINDOW)
        q = (x @ wq.T).reshape(B, T, H, HD)
        kv = (x @ wkv.T).reshape(B, T, H, 2 * HD)
        nb_kv = _gather_window(kv, W)
        nb_k, nb_v = (nb_kv[..., :HD], nb_kv[..., HD:])
        tau = jax.nn.sigmoid(jnp.einsum('bthd,bthwd->bthw', q, nb_k) / SCALE)
        msg = jnp.einsum('bthw,bthwd->bthd', tau, nb_v)
        y = x + msg.reshape(B, T, D) @ wo.T
        mu = jnp.mean(y, axis=-1, keepdims=True)
        var = jnp.mean((y - mu) ** 2, axis=-1, keepdims=True)
        out = (y - mu) * jax.lax.rsqrt(var + LN_EPS) * gamma + beta
        return out

    def _L0_ffn_ref(x, in_proj_w, in_proj_b, out_w, out_b, ln1_g, ln1_b, router_w, router_b, w1, b1, w2, b2, ln2_g, ln2_b):
        import jax, jax.numpy as jnp
        import numpy as np
        H = 16
        E = 8
        EPS = 1e-05

        def _layernorm(x, g, b):
            mu = jnp.mean(x, axis=-1, keepdims=True)
            var = jnp.mean(jnp.square(x - mu), axis=-1, keepdims=True)
            return (x - mu) * jax.lax.rsqrt(var + EPS) * g + b
        T, B, C = x.shape
        D = C // H
        qkv = x @ in_proj_w.T + in_proj_b
        q, k, v = jnp.split(qkv, 3, axis=-1)
        q = q.reshape(T, B, H, D)
        k = k.reshape(T, B, H, D)
        v = v.reshape(T, B, H, D)
        scale = 1.0 / np.sqrt(D).astype(np.float32)
        scores = jnp.einsum('tbhd,sbhd->bhts', q, k) * scale
        attn = jax.nn.softmax(scores, axis=-1)
        ctx = jnp.einsum('bhts,sbhd->tbhd', attn, v).reshape(T, B, C)
        attn_out = ctx @ out_w.T + out_b
        h = _layernorm(x + attn_out, ln1_g, ln1_b)
        flat = h.reshape(-1, C)
        logits = flat @ router_w.T + router_b
        probs = jax.nn.softmax(logits, axis=-1)
        _, top_i = jax.lax.top_k(probs, 2)
        assign = jnp.max(top_i, axis=-1)
        out = jnp.zeros_like(flat)
        for e in range(E):
            he = jax.nn.gelu(flat @ w1[e].T + b1[e], approximate=False)
            oe = he @ w2[e].T + b2[e]
            out = jnp.where((assign == e)[:, None], oe, out)
        moe_out = out.reshape(T, B, C)
        return _layernorm(h + moe_out, ln2_g, ln2_b)

    def _L1_attn_ref(x, ln_g, ln_b, W_in, conv_w, conv_b, dt_w, dt_b, B_w, C_w, log_A, D_param, W_out):
        import jax, jax.numpy as jnp
        import numpy as np
        D_MODEL = 128
        D_STATE = 16
        D_CONV = 4
        LN_EPS = 1e-05

        def _layernorm(x, g, b):
            mu = jnp.mean(x, axis=-1, keepdims=True)
            var = jnp.mean(jnp.square(x - mu), axis=-1, keepdims=True)
            return (x - mu) * jax.lax.rsqrt(var + LN_EPS) * g + b

        def _causal_depthwise_conv(x, w, b):
            xc = jnp.transpose(x, (0, 2, 1))
            K = w.shape[-1]
            out = jax.lax.conv_general_dilated(xc, w, window_strides=(1,), padding=[(K - 1, 0)], dimension_numbers=('NCH', 'OIH', 'NCH'), feature_group_count=x.shape[-1])
            return jnp.transpose(out, (0, 2, 1)) + b

        def _ssm_scan(x, dt, Bm, Cm, A):
            Bsz, T, DI = x.shape
            DS = Bm.shape[-1]
            h0 = jnp.zeros((Bsz, DI, DS), jnp.float32)

            def step(h, inp):
                xt, dtt, bt, ct = inp
                decay = jnp.exp(jnp.minimum(dtt * A, 0.0))
                h = h * decay[..., None] + (dtt * xt)[..., None] * bt[:, None, :]
                y = jnp.einsum('bds,bs->bd', h, ct)
                return (h, y)
            xs = (jnp.swapaxes(x, 0, 1), jnp.swapaxes(dt, 0, 1), jnp.swapaxes(Bm, 0, 1), jnp.swapaxes(Cm, 0, 1))
            _, ys = jax.lax.scan(step, h0, xs)
            return jnp.swapaxes(ys, 0, 1)
        residual = x
        xn = _layernorm(x, ln_g, ln_b)
        xz = xn @ W_in
        x_ssm, z = jnp.split(xz, 2, axis=-1)
        x_ssm = _causal_depthwise_conv(x_ssm, conv_w, conv_b)
        x_ssm = jax.nn.silu(x_ssm)
        dt = jax.nn.softplus(x_ssm @ dt_w + dt_b)
        Bm = x_ssm @ B_w
        Cm = x_ssm @ C_w
        A = -jnp.exp(log_A.astype(jnp.float32))
        y = _ssm_scan(x_ssm, dt, Bm, Cm, A)
        y = y + x_ssm * D_param
        y = y * jax.nn.silu(z)
        y = y @ W_out
        return residual + y

    def _L1_ffn_ref(x, w1_w, w1_s, w2_w, w2_s, h1_w, h1_s, h2_w, h2_s, w3_w, w3_s):
        import jax, jax.numpy as jnp
        import numpy as np
        D_IN, D_HID = (128, 512)

        def _ternary(key, shape):
            return jax.random.randint(key, shape, -1, 2).astype(jnp.float32)

        def _tlin(x, w, s):
            return jnp.einsum('bsi,oi->bso', x, w) * s
        h = jax.nn.silu(_tlin(x, w1_w, w1_s)) * _tlin(x, w2_w, w2_s)
        h = jax.nn.gelu(_tlin(h, h1_w, h1_s), approximate=False)
        h = jax.nn.gelu(_tlin(h, h2_w, h2_s), approximate=False)
        return _tlin(h, w3_w, w3_s)
    x = L0_attn_x
    x = x + _layernorm(_L0_attn_ref(_layernorm(x, axis=-1), L0_attn_wq, L0_attn_wkv, L0_attn_wo, L0_attn_gamma, L0_attn_beta), axis=-1)
    x = x + _layernorm(_L0_ffn_ref(_layernorm(x, axis=-1), L0_ffn_in_proj_w, L0_ffn_in_proj_b, L0_ffn_out_w, L0_ffn_out_b, L0_ffn_ln1_g, L0_ffn_ln1_b, L0_ffn_router_w, L0_ffn_router_b, L0_ffn_w1, L0_ffn_b1, L0_ffn_w2, L0_ffn_b2, L0_ffn_ln2_g, L0_ffn_ln2_b), axis=-1)
    x = x + _layernorm(_L1_attn_ref(_layernorm(x, axis=-1), L1_attn_ln_g, L1_attn_ln_b, L1_attn_W_in, L1_attn_conv_w, L1_attn_conv_b, L1_attn_dt_w, L1_attn_dt_b, L1_attn_B_w, L1_attn_C_w, L1_attn_log_A, L1_attn_D_param, L1_attn_W_out), axis=-1)
    x = x + _layernorm(_L1_ffn_ref(_layernorm(x, axis=-1), L1_ffn_w1_w, L1_ffn_w1_s, L1_ffn_w2_w, L1_ffn_w2_s, L1_ffn_h1_w, L1_ffn_h1_s, L1_ffn_h2_w, L1_ffn_h2_s, L1_ffn_w3_w, L1_ffn_w3_s), axis=-1)
    return x

_drawn_inputs = setup_inputs


def setup_inputs(seed=0):
    import zlib

    import numpy as np

    out = dict(_drawn_inputs(seed))
    spreads = {'L0_attn_gamma': (1.0, 0.2),
     'L0_attn_beta': (0.0, 0.1),
     'L0_ffn_in_proj_b': (0.0, 0.76),
     'L0_ffn_out_b': (0.0, 0.1),
     'L0_ffn_ln1_g': (1.0, 0.2),
     'L0_ffn_ln1_b': (0.0, 0.1),
     'L0_ffn_router_b': (0.0, 0.334),
     'L0_ffn_b1': (0.0, 0.8),
     'L0_ffn_b2': (0.0, 0.354),
     'L0_ffn_ln2_g': (1.0, 0.2),
     'L0_ffn_ln2_b': (0.0, 0.1),
     'L1_attn_ln_g': (1.0, 0.2),
     'L1_attn_ln_b': (0.0, 0.274),
     'L1_attn_conv_b': (0.0, 0.394),
     'L1_attn_dt_b': (0.0, 0.8),
     'L1_attn_D_param': (1.0, 0.6)}
    factors = {'L0_attn_wq': 8.0,
     'L0_ffn_in_proj_w': 8.0,
     'L0_ffn_out_w': 5.527,
     'L0_ffn_w1': 6.052,
     'L0_ffn_w2': 5.587,
     'L1_attn_log_A': 11.849}
    for name, (base, spread) in spreads.items():
        noise = np.random.default_rng([zlib.crc32(name.encode()), seed]).standard_normal(out[name].shape)
        drawn = base * np.exp(spread * noise) if base else spread * noise
        out[name] = jnp.asarray(drawn.astype(out[name].dtype))
    for name, factor in factors.items():
        out[name] = (out[name] * factor).astype(out[name].dtype)
    return out
```

```python
from contextlib import ExitStack

import concourse.bass as bass
from concourse import mybir

F32 = mybir.dt.float32
BF16 = mybir.dt.bfloat16
U32 = mybir.dt.uint32
ALU = mybir.AluOpType
ACT = mybir.ActivationFunctionType
AX = mybir.AxisListType

P = 128
D = 128
NB, NT = 16, 256
HD = 8
G = 4
BLK = 32
WIN = 16
SPAN = BLK + WIN
NBLK = NT // BLK
NE = 8
DS = 16
CH = 8
NCH = NT // CH
HID = 4
EPS = 1e-5
NEG = -1e12
ATT_SCALE = float(HD) ** -0.5
LANES = (0, 1)
ITER = NB // 2
ITER_MLP = NB // 4

PP = {}
for _name, _n in (("bq", 1), ("bk", 1), ("bv", 1), ("b1", NE), ("ln_g", 1), ("ln_b", 1), ("conv_w", 4), ("conv_b", 1),
                  ("dt_b", 1), ("log_A", 1), ("D_param", 1), ("w1_s", HID), ("w2_s", HID), ("h1_s", HID), ("h2_s", HID)):
    PP[_name] = sum(n for n, _ in PP.values()), _n
    PP[_name] = (_n, sum(n for k, (n, _) in PP.items() if k != _name))
NPP = sum(n for n, _ in PP.values())

OFF = [sum(NCH * (CH - k) for k in range(j)) for j in range(CH + 1)]
PAIR_BANKS = ((0, 2), (2, 5), (5, 8))


class Chain:

    def __init__(self, eng, sem):
        self.eng, self.sem, self.count = eng, sem, 0

    def clear(self):
        self.eng.sem_clear(self.sem)
        self.count = 0

    def link(self, ins):
        self.count += 1
        ins.then_inc(self.sem, 1)
        self.eng.wait_ge(self.sem, self.count)


class LayerNorm:

    def __init__(self, name, k, sb, sem):
        self.k = k
        self.st = [sb(f"{name}_st{l}", [P, k, 6]) for l in LANES]
        self.mv = [sb(f"{name}_mv{l}", [P, k, 2]) for l in LANES]
        self.ve = [sb(f"{name}_ve{l}", [P, k]) for l in LANES]
        self.rs = [sb(f"{name}_rs{l}", [P, k]) for l in LANES]
        self.mv_ready = sem(f"{name}_mv_ready")
        self.rstd_ready = sem(f"{name}_rstd_ready")

    def stats(self, dve, chain, src, l):
        for b in range(self.k):
            last = dve.bn_stats(self.st[l][:, b, :], src(b))
        chain.link(last)
        for b in range(self.k):
            last = dve.bn_aggr(self.mv[l][:, b, :], self.st[l][:, b, :])
        last.then_inc(self.mv_ready, 1)

    def rstd(self, pool, chain, eps, half, l, n):
        pool.wait_ge(self.mv_ready, n)
        chain.link(pool.tensor_tensor(self.ve[l][:, :], self.mv[l][:, :, 1], eps[:, 0:self.k], ALU.add))
        pool.tensor_tensor(self.rs[l][:, :], self.ve[l][:, :], half[:, 0:self.k], ALU.pow).then_inc(self.rstd_ready, 1)

    def apply(self, dve, out, src, l, n, scale=None):
        rs = self.rs if scale is None else scale
        dve.wait_ge(self.rstd_ready, n)
        for b in range(self.k):
            last = dve.tensor_scalar(out(b), src(b), self.mv[l][:, b, 0:1], rs[l][:, b:b + 1],
                                     ALU.subtract, ALU.mult)
        return last


def build(nc, a, out, stage=4):
    with ExitStack() as ctx:
        def sb(name, shape, dt=F32):
            return ctx.enter_context(nc.sbuf_tensor(name, shape, dt))

        def sem(name):
            return ctx.enter_context(nc.semaphore(name))

        ps = ctx.enter_context(nc.psum_tensor("ps", [P, 8, 512], F32))

        x = sb("x", [P, 2 * NB, D])
        ident = sb("ident", [P, P])
        headmask = sb("headmask", [P, G])
        vmask = sb("vmask", [P, 4 * D])
        rep = sb("rep", [P, P], BF16)
        eps = sb("eps", [P, 4])
        half = sb("half", [P, 4])
        pp = sb("pp", [P, NPP])
        wa = sb("wa", [P, 4, D])
        wf = sb("wf", [P, 4, D])
        w_router = sb("w_router", [P, NE])
        w_e1 = sb("w_e1", [P, NE, D])
        w_e2 = sb("w_e2", [P, NE, D])
        b_e2 = sb("b_e2", [NE, D])
        rows = sb("rows", [P, 7, 2, D])
        router_b = sb("router_b", [P, 2, NE])
        iota = sb("iota", [P, NE])
        negsel = sb("negsel", [NE, NE, P], BF16)
        band = sb("band", [P, NBLK * SPAN], BF16)
        same = sb("same", [P, NBLK * BLK], BF16)
        w_in = sb("w_in", [P, 2 * D])
        w_dt = sb("w_dt", [P, D])
        w_b = sb("w_b", [P, DS])
        w_c = sb("w_c", [P, DS])
        w_bR = sb("w_bR", [P, DS, 16])
        w_cR = sb("w_cR", [P, 8, DS])
        w_out = sb("w_out", [P, D])
        bmask = sb("bmask", [P, 2, DS, 16])
        cmask = sb("cmask", [P, NT])
        first = sb("first", [P, NT])
        ones = sb("ones", [P, P])
        expA = sb("expA", [P, 1])
        negA = sb("negA", [P, 1])
        w_m1 = sb("w_m1", [P, HID * D])
        w_m2 = sb("w_m2", [P, HID * D])
        w_h1 = sb("w_h1", [P, HID, HID * D])
        w_h2 = sb("w_h2", [P, HID, HID * D])
        w_m3 = sb("w_m3", [P, HID, D])
        w3_s = sb("w3_s", [P, HID, D])

        fill_done, cast_ready, expA_ready, negA_ready, zero_ready = (sem(n) for n in (
            "fill_done", "cast_ready", "expA_ready", "negA_ready", "zero_ready"))
        w_loaded = {k: sem("w_loaded_" + k) for k in "abcd"}
        x_loaded = [sem(f"x_loaded{l}") for l in LANES]
        pool_chain, dve_chain, act_chain = sem("pool_chain"), sem("dve_chain"), sem("act_chain")

        loads = {
            "a": [(ident[:, :], "c_ident"), (headmask[:, :], "c_headmask"), (vmask[:, :], "c_vmask"),
                  (wa[:, :, :], "wa"), (rows[:, :, :, :], "rows"), (pp[:, :], "pp")],
            "b": [(wf[:, :, :], "wf"), (w_router[:, :], "w_router"), (w_e1[:, :, :], "w_e1"), (w_e2[:, :, :], "w_e2"),
                  (b_e2[:, :], "b_e2"), (router_b[:, :, :], "router_b"), (iota[:, :], "c_iota")],
            "c": [(w_in[:, :], "w_in"), (w_dt[:, :], "w_dt"), (w_b[:, :], "w_b"), (w_c[:, :], "w_c"),
                  (w_bR[:, :, :], "w_bR"), (w_cR[:, :, :], "w_cR"), (w_out[:, :], "w_out"),
                  (bmask[:, :, :, :], "c_bmask"), (cmask[:, :], "c_cmask"), (first[:, :], "c_first")],
            "d": [(w_m1[:, :], "w_m1"), (w_m2[:, :], "w_m2"), (w_h1[:, :, :], "w_h1"), (w_h2[:, :, :], "w_h2"),
                  (w_m3[:, :, :], "w_m3"), (w3_s[:, :, :], "w3_s")],
        }
        W_ALL = {k: 16 * len(v) for k, v in loads.items()}
        W_ALL["a"] += 16 * 4

        def vec(name, c=0):
            return pp[:, PP[name][1] + c:PP[name][1] + c + 1]

        def tok(name, k=2):
            return [sb(f"{name}{l}", [P, k, D]) for l in LANES]

        def chan(name):
            return [sb(f"{name}{l}", [P, NT]) for l in LANES]

        def flat3(t):
            return t.rearrange("p a b -> p (a b)")

        outer = ctx
        ctx = ExitStack()
        stage_f = [sb("stage_rep", [P, P]), sb("stage_band", [P, NBLK * SPAN]), sb("stage_same", [P, NBLK * BLK]),
                   sb("stage_negsel", [NE, NE, P])]
        xB = sb("xB", [P, 2 * NB, D])
        t_xn, t_xb, t_y, t_zn, t_zg, t_z, t_o = (tok("t_" + n) for n in ("xn", "xb", "y", "zn", "zg", "z", "o"))
        xnT, qT, msgT = (chan(n) for n in ("xnT", "qT", "msgT"))
        xnR = [sb(f"xnR{l}", [P, NBLK, 4, BLK]) for l in LANES]
        hbd = [sb(f"hbd{l}", [P, NBLK, 4, BLK]) for l in LANES]
        vbd = [sb(f"vbd{l}", [P, NBLK, D]) for l in LANES]
        tau = [sb(f"tau{l}", [P, G, NBLK * SPAN]) for l in LANES]
        sm = [sb(f"sm{l}", [P, G * NBLK, BLK]) for l in LANES]
        ex = [sb(f"ex{l}", [P, G * NBLK, BLK]) for l in LANES]
        pT = [sb(f"pT{l}", [P, G, NBLK * BLK]) for l in LANES]
        mx, den, rden = ([sb(f"{n}{l}", [P, G * NBLK]) for l in LANES] for n in ("mx", "den", "rden"))
        hT = chan("hT")
        lg, le = ([sb(f"{n}{l}", [P, 2, NE]) for l in LANES] for n in ("lg", "le"))
        lmx = [sb(f"lmx{l}", [P, 2]) for l in LANES]
        m8 = [sb(f"m8{l}", [P, 2, 8]) for l in LANES]
        ix = [sb(f"ix{l}", [P, 2, 8], U32) for l in LANES]
        pick = [sb(f"pick{l}", [P, 2]) for l in LANES]
        hot = [sb(f"hot{l}", [P, 2, NE]) for l in LANES]
        hotT = [sb(f"hotT{l}", [NE, NT]) for l in LANES]
        hotTb = [sb(f"hotTb{l}", [NE, NT], BF16) for l in LANES]
        he = [[sb(f"he{l}{c}", [P, NT]) for c in range(2)] for l in LANES]
        a_ln1, a_ln2, a_ln3, b_ln0, b_ln1, b_ln2, b_ln3 = (
            LayerNorm(n, 2, sb, lambda m: outer.enter_context(nc.semaphore(m)))
            for n in ("a_ln1", "a_ln2", "a_ln3", "b_ln0", "b_ln1", "b_ln2", "b_ln3"))
        ctx.close()

        ctx = ExitStack()
        c_xn, c_xq, c_r, c_o = (tok("c_" + n) for n in ("xn", "xq", "r", "o"))
        c_xT, zs, cv, xs, zb, sp_, dt, u, cdt, ya, yi = (
            chan("c_" + n) for n in ("xT", "zs", "cv", "xs", "zb", "sp", "dt", "u", "cdt", "ya", "yi"))
        xpad = [sb(f"xpad{l}", [P, 3 + NT]) for l in LANES]
        dec = [sb(f"dec{l}", [P, 2, NCH, CH]) for l in LANES]
        bcT = [sb(f"bcT{l}", [DS, 2, NCH, CH]) for l in LANES]
        prod = [sb(f"prod{l}", [DS, OFF[CH]]) for l in LANES]
        wall = [sb(f"wall{l}", [P, OFF[CH]]) for l in LANES]
        term = [sb(f"term{l}", [P, OFF[CH]]) for l in LANES]
        wend = [sb(f"wend{l}", [P, NCH, CH]) for l in LANES]
        wendT = [sb(f"wendT{l}", [P, 2, D]) for l in LANES]
        bbd = [sb(f"bbd{l}", [P, 2, DS * 16]) for l in LANES]
        cbd = [sb(f"cbd{l}", [P, NT]) for l in LANES]
        d0 = [sb(f"d0{l}", [P, DS, NCH]) for l in LANES]
        hs = [sb(f"hs{l}", [P, DS, NCH]) for l in LANES]
        hc = [sb(f"hc{l}", [P, NCH, DS]) for l in LANES]
        hcT = [sb(f"hcT{l}", [P, 4, D]) for l in LANES]
        c_v2, c_r2 = ([sb(f"{n}{l}", [P, 2]) for l in LANES] for n in ("c_v2", "c_r2"))
        new = lambda m: outer.enter_context(nc.semaphore(m))
        c_ln1, c_ln2 = (LayerNorm(n, 2, sb, new) for n in ("c_ln1", "c_ln2"))
        ctx.close()
        ctx = ExitStack()
        d_xn, d_y, d_o = (tok("d_" + n, 4) for n in ("xn", "y", "o"))
        d_xT = [sb(f"d_xT{l}", [P, 4 * P]) for l in LANES]
        gate = [[sb(f"gate{l}{c}", [P, 4 * P]) for c in range(2)] for l in LANES]
        h0 = [sb(f"h0{l}", [P, HID, 4 * P]) for l in LANES]
        h1 = [sb(f"h1{l}", [P, HID, 4 * P]) for l in LANES]
        d_ln1, d_ln2 = (LayerNorm(n, 4, sb, new) for n in ("d_ln1", "d_ln2"))
        ctx.close()
        ctx = outer

        SEMS = """a_xn a_t_ps a_xnT a_qk_ps a_v_ps a_qT a_hbd a_vbd a_s_ps a_tau a_m_ps a_msgT a_y_ps a_zn a_z
            a_o a_x a_stored
            b_xn b_xb b_t_ps b_xnT b_qk_ps b_v_ps b_kT b_hbd b_vbd b_s_ps b_sm b_ex b_rden b_p b_pT b_m_ps b_msgT
            b_y_ps b_zn b_h b_ht_ps b_hT b_l_ps b_lg b_le b_hot b_hott_ps b_hotT b_moe_ps b_on b_z b_o b_x b_stored
            c_r2 c_xn_ c_t_ps c_xT_ c_in_ps c_xpad c_zs_ c_cv_ c_xs_ c_dt_ps c_b_ps c_c_ps c_zb_ c_sp_ c_dt_ c_dec c_decm
            c_bcT c_prod c_g0_ps c_g1_ps c_term c_cbd c_bbd c_wall c_wend c_wt_ps c_wendT c_st_ps c_d0 c_hs c_hc c_hct_ps c_hcT
            c_yi_ps c_y c_out_ps c_o_ c_x
            d_xn_ d_t_ps d_xT_ d_y_ps d_o_ d_x d_stored""".split()
        S = {n: sem(n) for n in SEMS}
        he_ps, he_ready, e_done = ([sem(f"{n}{l}") for l in LANES] for n in ("he_ps", "he_ready", "e_done"))
        m_gu_ps, m_gate, m_h0, m_h1_ps, m_h1, m_h2_ps, m_h2 = (
            [sem(f"{n}{l}") for l in LANES] for n in ("m_gu_ps", "m_gate", "m_h0", "m_h1_ps", "m_h1", "m_h2_ps", "m_h2"))

        x_in = a["x"].rearrange("b (h p) d -> (b h) p d", p=P)
        out_t = out.rearrange("b (h p) d -> (b h) p d", p=P)
        x1 = nc.dram_tensor("x1", (NB, NT, D), F32, kind="Internal").ap()
        x2 = nc.dram_tensor("x2", (NB, NT, D), F32, kind="Internal").ap()
        by_seq = lambda t: t.rearrange("b (h p) d -> (b h) p d", p=P)
        by_step = lambda t: t.rearrange("b (k s) d -> k s b d", s=8)

        def xblk(t, i, c):
            return t[:, bass.ds(i + c, 1), :].rearrange("p o d -> p (o d)")

        def heads(g):
            return slice(BLK * g, BLK * g + BLK)

        def bank(l, b, lo=0, hi=512):
            return ps[:, 4 * l + b, lo:hi]

        block = ctx.enter_context(nc.Block())

        @block.sync
        def _(sp):
            def load(per, first, issue):
                for l in LANES:
                    issue(0, l)
                with sp.Fori(1, ITER) as i:
                    for l in LANES:
                        sp.wait_ge(x_loaded[l], i * (16 * per) + first)
                        issue(i, l)

            def load_seq(src):
                def issue(i, l):
                    sp.dma_start(x[:, bass.ds(i * 4 + 2 * l, 2), :],
                                 by_seq(src)[bass.ds(i * 4 + 2 * l, 2)].rearrange("b p d -> p b d")
                                 ).then_inc(x_loaded[l], 16)
                return issue

            def load_step(src):
                def issue(i, l):
                    for b in range(2):
                        sp.dma_start(xblk(xB, i * 4, 2 * l + b),
                                     by_step(src)[bass.ds(i * 4 + 2 * l + b, 1)].rearrange("o s b d -> (o s) b d")
                                     ).then_inc(x_loaded[l], 16)
                return issue

            load(1, 0, load_seq(a["x"]))
            dst = out if stage == 1 else x1
            with sp.Fori(0, ITER) as i:
                for l in LANES:
                    sp.wait_ge(S["a_x"], i * 2 + l + 1)
                    sp.dma_start(by_seq(dst)[bass.ds(i * 4 + 2 * l, 2)].rearrange("b p d -> p b d"),
                                 x[:, bass.ds(i * 4 + 2 * l, 2), :]).then_inc(S["a_stored"], 16)
            sp.wait_ge(S["a_stored"], 16 * NB)
            if stage < 4:
                for k in "abcd":
                    sp.wait_ge(w_loaded[k], W_ALL[k])
            if stage == 1:
                return
            load(2, 16 * ITER, load_step(x1))
            dst = out if stage == 2 else x2
            with sp.Fori(0, ITER) as i:
                for l in LANES:
                    sp.wait_ge(S["b_x"], i * 2 + l + 1)
                    for b in range(2):
                        sp.dma_start(by_step(dst)[bass.ds(i * 4 + 2 * l + b, 1)].rearrange("o s b d -> (o s) b d"),
                                     xB[:, bass.ds(i * 4 + 2 * l + b, 1), :].rearrange("p o d -> p (o d)")
                                     ).then_inc(S["b_stored"], 16)
            sp.wait_ge(S["b_stored"], 32 * NB)
            if stage == 2:
                return
            load(1, 48 * ITER, load_seq(x2))
            if stage == 3:
                sp.wait_ge(S["c_x"], NB)
                sp.dma_start(by_seq(out).rearrange("b p d -> p b d"), x[:, :, :]).then_inc(S["d_stored"], 16)
                sp.wait_ge(S["d_stored"], 16)
                return
            with sp.Fori(0, ITER_MLP) as i:
                for l in LANES:
                    sp.wait_ge(S["d_x"], i * 2 + l + 1)
                    sp.dma_start(out_t[bass.ds(i * 8 + 4 * l, 4)].rearrange("b p d -> p b d"),
                                 x[:, bass.ds(i * 8 + 4 * l, 4), :]).then_inc(S["d_stored"], 16)
            sp.wait_ge(S["d_stored"], 16 * 2 * ITER_MLP)

        @block.gpsimd
        def _(pool):
            chain = Chain(pool, pool_chain)
            pool.memset(eps[:, :], EPS).then_inc(fill_done, 1)
            pool.memset(half[:, :], -0.5).then_inc(fill_done, 1)
            pool.memset(ones[:, :], 1.0).then_inc(fill_done, 1)
            pool.wait_ge(fill_done, 3)
            pool.wait_ge(w_loaded["a"], W_ALL["a"])

            def scale_shift(l, n, ready, src, tmp, dst, g, b, done):
                pool.wait_ge(ready, n)
                chain.link(pool.tensor_tensor(tmp[l][:, :, :], src[l][:, :, :], rows[:, g, :, :], ALU.mult))
                pool.tensor_tensor(dst[l][:, :, :], tmp[l][:, :, :], rows[:, b, :, :], ALU.add).then_inc(done, 1)

            def copy(dst, src, one):
                return pool.tensor_tensor(dst, src, one, ALU.mult)

            with pool.Fori(0, ITER) as i:
                chain.clear()
                for l in LANES:
                    a_ln1.rstd(pool, chain, eps, half, l, i * 2 + l + 1)
                for l in LANES:
                    a_ln2.rstd(pool, chain, eps, half, l, i * 2 + l + 1)
                for l in LANES:
                    scale_shift(l, i * 2 + l + 1, S["a_zn"], t_zn, t_zg, t_z, 0, 1, S["a_z"])
                for l in LANES:
                    a_ln3.rstd(pool, chain, eps, half, l, i * 2 + l + 1)
                for l in LANES:
                    pool.wait_ge(S["a_o"], i * 2 + l + 1)
                    xt = x[:, bass.ds(i * 4 + 2 * l, 2), :]
                    pool.tensor_tensor(xt, xt, t_o[l][:, :, :], ALU.add).then_inc(S["a_x"], 1)
            if stage == 1:
                return
            with pool.Fori(0, ITER) as i:
                chain.clear()
                for l in LANES:
                    b_ln0.rstd(pool, chain, eps, half, l, i * 2 + l + 1)
                for l in LANES:
                    pool.wait_ge(S["b_xn"], i * 2 + l + 1)
                    pool.tensor_tensor(t_xb[l][:, :, :], t_xn[l][:, :, :], rows[:, 2, :, :], ALU.add).then_inc(S["b_xb"], 1)
                for l in LANES:
                    pool.wait_ge(S["b_rden"], i * 2 + l + 1)
                    pool.tensor_tensor(sm[l][:, :, :], ex[l][:, :, :],
                                       rden[l][:, :].unsqueeze(2).to_broadcast([P, G * NBLK, BLK]),
                                       ALU.mult).then_inc(S["b_p"], 1)
                for l in LANES:
                    b_ln1.rstd(pool, chain, eps, half, l, i * 2 + l + 1)
                for l in LANES:
                    scale_shift(l, i * 2 + l + 1, S["b_zn"], t_zn, t_zg, t_z, 3, 4, S["b_h"])
                for l in LANES:
                    b_ln2.rstd(pool, chain, eps, half, l, i * 2 + l + 1)
                for l in LANES:
                    scale_shift(l, i * 2 + l + 1, S["b_on"], t_zn, t_zg, t_xn, 5, 6, S["b_z"])
                for l in LANES:
                    b_ln3.rstd(pool, chain, eps, half, l, i * 2 + l + 1)
                for l in LANES:
                    pool.wait_ge(S["b_o"], i * 2 + l + 1)
                    xt = xB[:, bass.ds(i * 4 + 2 * l, 2), :]
                    pool.tensor_tensor(xt, xt, t_o[l][:, :, :], ALU.add).then_inc(S["b_x"], 1)
            if stage == 2:
                return
            pool.wait_ge(S["b_stored"], 32 * NB)
            for l in LANES:
                pool.memset(xpad[l][:, 0:3], 0.0)
                pool.memset(d0[l][:, :, 0:1], 0.0)
                pool.memset(hc[l][:, 0:1, :], 0.0).then_inc(zero_ready, 1)
            with pool.Fori(0, ITER) as i:
                chain.clear()
                for l in LANES:
                    n = i * 2 + l + 1
                    c_ln1.rstd(pool, chain, eps, half, l, n)
                    pool.wait_ge(c_ln1.rstd_ready, n)
                    chain.link(pool.tensor_tensor(c_v2[l][:, :], c_ln1.mv[l][:, :, 1], c_ln1.rs[l][:, :], ALU.mult))
                    chain.link(pool.tensor_tensor(c_v2[l][:, :], c_v2[l][:, :], c_ln1.rs[l][:, :], ALU.mult))
                    chain.link(pool.tensor_tensor(c_v2[l][:, :], c_v2[l][:, :], eps[:, 0:2], ALU.add))
                    chain.link(pool.tensor_tensor(c_v2[l][:, :], c_v2[l][:, :], half[:, 0:2], ALU.pow))
                    pool.tensor_tensor(c_r2[l][:, :], c_v2[l][:, :], c_ln1.rs[l][:, :], ALU.mult).then_inc(S["c_r2"], 1)
                for l in LANES:
                    n = i * 2 + l + 1
                    pool.wait_ge(S["c_bcT"], n)
                    for j in range(CH):
                        last = pool.tensor_tensor(
                            prod[l][:, OFF[j]:OFF[j + 1]].rearrange("p (c t) -> p c t", t=CH - j),
                            bcT[l][:, 1, :, j:CH], bcT[l][:, 0, :, 0:CH - j], ALU.mult)
                    last.then_inc(S["c_prod"], 1)
                for l in LANES:
                    n = i * 2 + l + 1
                    pool.wait_ge(S["c_decm"], n)
                    copy(d0[l][:, :, 1:NCH], dec[l][:, 1, 1:NCH, CH - 1].unsqueeze(1).to_broadcast([P, DS, NCH - 1]),
                         ones[:, 0:1].unsqueeze(2).to_broadcast([P, DS, NCH - 1])).then_inc(S["c_d0"], 1)
                    pool.wait_ge(S["c_wall"], n)
                    for j in range(CH):
                        w = wall[l][:, OFF[j]:OFF[j + 1]].rearrange("p (c t) -> p c t", t=CH - j)
                        last = copy(wend[l][:, :, CH - 1 - j], w[:, :, CH - 1 - j], ones[:, 0:NCH])
                    last.then_inc(S["c_wend"], 1)
                for l in LANES:
                    c_ln2.rstd(pool, chain, eps, half, l, i * 2 + l + 1)
                for l in LANES:
                    pool.wait_ge(S["c_o_"], i * 2 + l + 1)
                    xt = x[:, bass.ds(i * 4 + 2 * l, 2), :]
                    pool.tensor_tensor(xt, xt, c_o[l][:, :, :], ALU.add).then_inc(S["c_x"], 1)
            if stage == 3:
                return
            with pool.Fori(0, ITER_MLP) as i:
                chain.clear()
                for l in LANES:
                    d_ln1.rstd(pool, chain, eps, half, l, i * 2 + l + 1)
                for l in LANES:
                    d_ln2.rstd(pool, chain, eps, half, l, i * 2 + l + 1)
                for l in LANES:
                    pool.wait_ge(S["d_o_"], i * 2 + l + 1)
                    xt = x[:, bass.ds(i * 8 + 4 * l, 4), :]
                    pool.tensor_tensor(xt, xt, d_o[l][:, :, :], ALU.add).then_inc(S["d_x"], 1)

        @block.scalar
        def _(act):
            chain = Chain(act, act_chain)
            for t, name in zip(stage_f, ("c_rep", "c_band", "c_same", "c_negsel")):
                dst = t[:, :, :] if name == "c_negsel" else t[:, :]
                act.dma_start(dst, a[name]).then_inc(w_loaded["a"], 16)
            for part in "abcd":
                for dst, name in loads[part]:
                    act.dma_start(dst, a[name]).then_inc(w_loaded[part], 16)

            def transposed(l, n, t_ps, done):
                act.wait_ge(t_ps, n)
                act.activation(xnT[l][:, :], bank(l, 0, 0, NT), ACT.Copy)
                src = bank(l, 0, 0, NT).rearrange("p (j s) -> p j s", s=BLK).unsqueeze(2).to_broadcast([P, NBLK, 4, BLK])
                act.activation(xnR[l][:, :, :, :], src, ACT.Copy).then_inc(done, 1)

            with act.Fori(0, ITER) as i:
                for l in LANES:
                    transposed(l, i * 2 + l + 1, S["a_t_ps"], S["a_xnT"])
                for l in LANES:
                    act.wait_ge(S["a_qk_ps"], i * 2 + l + 1)
                    act.activation(qT[l][:, :], bank(l, 0, 0, NT), ACT.Copy).then_inc(S["a_qT"], 1)
                for l in LANES:
                    act.wait_ge(S["a_s_ps"], i * 2 + l + 1)
                    act.activation(tau[l][:, :, :], ps[:, 4 * l:4 * l + 4, 0:NBLK * SPAN], ACT.Sigmoid,
                                   scale=ATT_SCALE).then_inc(S["a_tau"], 1)
                for l in LANES:
                    act.wait_ge(S["a_m_ps"], i * 2 + l + 1)
                    act.activation(msgT[l][:, :], bank(l, 0, 0, NT), ACT.Copy).then_inc(S["a_msgT"], 1)
            if stage == 1:
                return
            act.wait_ge(w_loaded["a"], W_ALL["a"])
            act.wait_ge(w_loaded["b"], W_ALL["b"])
            with act.Fori(0, ITER) as i:
                for l in LANES:
                    transposed(l, i * 2 + l + 1, S["b_t_ps"], S["b_xnT"])
                for l in LANES:
                    act.wait_ge(S["b_qk_ps"], i * 2 + l + 1)
                    act.activation(qT[l][:, :], bank(l, 1, 0, NT), ACT.Identity, bias=vec("bk")).then_inc(S["b_kT"], 1)
                for l in LANES:
                    act.wait_ge(S["b_sm"], i * 2 + l + 1)
                    act.activation(ex[l][:, :, :], sm[l][:, :, :], ACT.Exp, scale=ATT_SCALE).then_inc(S["b_ex"], 1)
                for l in LANES:
                    act.wait_ge(S["b_m_ps"], i * 2 + l + 1)
                    act.activation(msgT[l][:, :], bank(l, 0, 0, NT), ACT.Identity, bias=vec("bv")).then_inc(S["b_msgT"], 1)
                for l in LANES:
                    act.wait_ge(S["b_ht_ps"], i * 2 + l + 1)
                    act.activation(hT[l][:, :], bank(l, 0, 0, NT), ACT.Copy).then_inc(S["b_hT"], 1)
                for l in LANES:
                    act.wait_ge(S["b_lg"], i * 2 + l + 1)
                    act.activation(le[l][:, :, :], lg[l][:, :, :], ACT.Exp).then_inc(S["b_le"], 1)
                for l in LANES:
                    act.wait_ge(S["b_hott_ps"], i * 2 + l + 1)
                    act.activation(hotT[l][:, :], ps[0:NE, 4 * l + 1, 0:NT], ACT.Copy)
                    act.activation(hotTb[l][:, :], ps[0:NE, 4 * l + 1, 0:NT], ACT.Copy).then_inc(S["b_hotT"], 1)
                for e in range(NE):
                    for l in LANES:
                        act.wait_ge(he_ps[l], i * NE + e + 1)
                        if e >= 2:
                            act.wait_ge(e_done[l], i * NE + e - 1)
                        act.activation(he[l][e % 2][:, :], bank(l, 3 * (e % 2), 0, NT), ACT.Gelu,
                                       bias=vec("b1", e)).then_inc(he_ready[l], 1)
            if stage == 2:
                return
            act.wait_ge(S["b_stored"], 32 * NB)
            act.wait_ge(w_loaded["c"], W_ALL["c"])
            act.wait_ge(zero_ready, 2)
            act.activation(expA[:, :], vec("log_A"), ACT.Exp).then_inc(expA_ready, 1)
            act.wait_ge(negA_ready, 1)
            with act.Fori(0, ITER) as i:
                chain.clear()
                for l in LANES:
                    act.wait_ge(S["c_t_ps"], i * 2 + l + 1)
                    act.activation(c_xT[l][:, :], bank(l, 0, 0, NT), ACT.Identity, bias=vec("ln_b"),
                                   scale=vec("ln_g")).then_inc(S["c_xT_"], 1)
                for l in LANES:
                    act.wait_ge(S["c_in_ps"], i * 2 + l + 1)
                    act.activation(xpad[l][:, 3:3 + NT], bank(l, 1, 0, NT), ACT.Copy).then_inc(S["c_xpad"], 1)
                    act.activation(zs[l][:, :], bank(l, 2, 0, NT), ACT.Silu).then_inc(S["c_zs_"], 1)
                for l in LANES:
                    act.wait_ge(S["c_cv_"], i * 2 + l + 1)
                    act.activation(xs[l][:, :], cv[l][:, :], ACT.Silu).then_inc(S["c_xs_"], 1)
                for l in LANES:
                    act.wait_ge(S["c_b_ps"], i * 2 + l + 1)
                    act.activation(bcT[l][:, :, :, :].rearrange("p a c t -> p (a c t)"), ps[0:DS, 4 * l + 3, :],
                                   ACT.Copy).then_inc(S["c_bcT"], 1)
                for l in LANES:
                    act.wait_ge(S["c_zb_"], i * 2 + l + 1)
                    chain.link(act.activation(sp_[l][:, :], zb[l][:, :], ACT.Abs))
                    chain.link(act.activation(sp_[l][:, :], sp_[l][:, :], ACT.Exp, scale=-1.0))
                    act.activation(sp_[l][:, :], sp_[l][:, :], ACT.Ln, bias=1.0).then_inc(S["c_sp_"], 1)
                for l in LANES:
                    act.wait_ge(S["c_dt_"], i * 2 + l + 1)
                    act.activation(dec[l][:, 0, :, :].rearrange("p c t -> p (c t)"), dt[l][:, :], ACT.Exp, scale=negA[:, :])
                    act.activation(dec[l][:, 1, :, :].rearrange("p c t -> p (c t)"), cdt[l][:, :], ACT.Exp,
                                   scale=negA[:, :]).then_inc(S["c_dec"], 1)
                for l in LANES:
                    act.wait_ge(S["c_wt_ps"], i * 2 + l + 1)
                    act.activation(flat3(wendT[l][:, :, :]), bank(l, 0, 0, NT), ACT.Copy).then_inc(S["c_wendT"], 1)
                for l in LANES:
                    act.wait_ge(S["c_hs"], i * 2 + l + 1)
                    act.activation(hc[l][:, 1:NCH, :], hs[l][:, :, 0:NCH - 1].rearrange("p n c -> p c n"),
                                   ACT.Copy).then_inc(S["c_hc"], 1)
                for l in LANES:
                    act.wait_ge(S["c_hct_ps"], i * 2 + l + 1)
                    act.activation(flat3(hcT[l][:, :, :]), bank(l, 1), ACT.Copy).then_inc(S["c_hcT"], 1)
            if stage == 3:
                return
            act.wait_ge(w_loaded["d"], W_ALL["d"])
            with act.Fori(0, ITER_MLP) as i:
                for l in LANES:
                    act.wait_ge(S["d_t_ps"], i * 2 + l + 1)
                    act.activation(d_xT[l][:, :], bank(l, 0), ACT.Copy).then_inc(S["d_xT_"], 1)
                for l in LANES:
                    for m in range(HID):
                        act.wait_ge(m_gu_ps[l], i * HID + m + 1)
                        if m >= 2:
                            act.wait_ge(m_h0[l], i * HID + m - 1)
                        act.activation(gate[l][m % 2][:, :], bank(l, 2 * (m % 2)), ACT.Silu,
                                       scale=vec("w1_s", m)).then_inc(m_gate[l], 1)
                for l in LANES:
                    for m in range(HID):
                        act.wait_ge(m_h1_ps[l], i * HID + m + 1)
                        act.activation(h1[l][:, m, :], bank(l, m), ACT.Gelu, scale=vec("h1_s", m)).then_inc(m_h1[l], 1)
                for l in LANES:
                    for m in range(HID):
                        act.wait_ge(m_h2_ps[l], i * HID + m + 1)
                        act.activation(h0[l][:, m, :], bank(l, m), ACT.Gelu, scale=vec("h2_s", m)).then_inc(m_h2[l], 1)

        @block.vector
        def _(dve):
            chain = Chain(dve, dve_chain)
            dve.wait_ge(w_loaded["a"], W_ALL["a"])
            for dst, src in zip((rep[:, :], band[:, :], same[:, :], negsel[:, :, :]),
                                (stage_f[0][:, :], stage_f[1][:, :], stage_f[2][:, :], stage_f[3][:, :, :])):
                dve.tensor_copy(dst, src).then_inc(cast_ready, 1)

            def four_heads(l, src, bias):
                src = src.rearrange("p (j s) -> p j s", s=BLK)
                for h in range(4):
                    if bias is None:
                        last = dve.tensor_scalar(hbd[l][:, :, h, :], src, headmask[:, h:h + 1], None, ALU.mult)
                    else:
                        last = dve.tensor_scalar(hbd[l][:, :, h, :], src, bias, headmask[:, h:h + 1], ALU.add, ALU.mult)
                return last

            def values(l):
                for c in range(2):
                    last = dve.tensor_tensor(flat3(vbd[l][:, 4 * c:4 * c + 4, :]), bank(l, 2 + c), vmask[:, :], ALU.mult)
                return last

            def blocks(t):
                return t.rearrange("p (b d) -> p b d", d=D)

            with dve.Fori(0, ITER) as i:
                chain.clear()
                for l in LANES:
                    dve.wait_ge(x_loaded[l], i * 16 + 16)
                    a_ln1.stats(dve, chain, lambda b: xblk(x, i * 4, 2 * l + b), l)
                for l in LANES:
                    a_ln1.apply(dve, lambda b: t_xn[l][:, b, :], lambda b: xblk(x, i * 4, 2 * l + b), l,
                                i * 2 + l + 1).then_inc(S["a_xn"], 1)
                for l in LANES:
                    n = i * 2 + l + 1
                    dve.wait_ge(S["a_qk_ps"], n)
                    four_heads(l, bank(l, 1, 0, NT), None).then_inc(S["a_hbd"], 1)
                    dve.wait_ge(S["a_v_ps"], n)
                    values(l).then_inc(S["a_vbd"], 1)
                for l in LANES:
                    dve.wait_ge(S["a_y_ps"], i * 2 + l + 1)
                    chain.link(dve.tensor_tensor(t_y[l][:, :, :], blocks(bank(l, 1, 0, NT)), t_xn[l][:, :, :], ALU.add))
                    a_ln2.stats(dve, chain, lambda b: t_y[l][:, b, :], l)
                for l in LANES:
                    a_ln2.apply(dve, lambda b: t_zn[l][:, b, :], lambda b: t_y[l][:, b, :], l,
                                i * 2 + l + 1).then_inc(S["a_zn"], 1)
                for l in LANES:
                    dve.wait_ge(S["a_z"], i * 2 + l + 1)
                    a_ln3.stats(dve, chain, lambda b: t_z[l][:, b, :], l)
                for l in LANES:
                    a_ln3.apply(dve, lambda b: t_o[l][:, b, :], lambda b: t_z[l][:, b, :], l,
                                i * 2 + l + 1).then_inc(S["a_o"], 1)
            if stage == 1:
                return
            dve.wait_ge(S["a_x"], NB)
            dve.wait_ge(w_loaded["b"], W_ALL["b"])
            with dve.Fori(0, ITER) as i:
                chain.clear()
                for l in LANES:
                    dve.wait_ge(x_loaded[l], i * 32 + (16 * ITER + 32))
                    b_ln0.stats(dve, chain, lambda b: xblk(xB, i * 4, 2 * l + b), l)
                for l in LANES:
                    b_ln0.apply(dve, lambda b: t_xn[l][:, b, :], lambda b: xblk(xB, i * 4, 2 * l + b), l,
                                i * 2 + l + 1).then_inc(S["b_xn"], 1)
                for l in LANES:
                    n = i * 2 + l + 1
                    dve.wait_ge(S["b_qk_ps"], n)
                    four_heads(l, bank(l, 0, 0, NT), vec("bq")).then_inc(S["b_hbd"], 1)
                    dve.wait_ge(S["b_v_ps"], n)
                    values(l).then_inc(S["b_vbd"], 1)
                for l in LANES:
                    dve.wait_ge(S["b_s_ps"], i * 2 + l + 1)
                    sc = ps[:, 4 * l:4 * l + 4, 0:NT].rearrange("p g (j s) -> p g j s", s=BLK)
                    m4 = mx[l][:, :].rearrange("p (g j) -> p g j", j=NBLK)
                    chain.link(dve.tensor_reduce(m4, sc, AX.X, ALU.max))
                    dve.tensor_tensor(sm[l][:, :, :].rearrange("p (g j) s -> p g j s", j=NBLK), sc,
                                      m4.unsqueeze(3).to_broadcast([P, G, NBLK, BLK]), ALU.subtract).then_inc(S["b_sm"], 1)
                for l in LANES:
                    dve.wait_ge(S["b_ex"], i * 2 + l + 1)
                    chain.link(dve.tensor_reduce(den[l][:, :], ex[l][:, :, :], AX.X, ALU.add))
                    dve.reciprocal(rden[l][:, :], den[l][:, :]).then_inc(S["b_rden"], 1)
                for l in LANES:
                    dve.wait_ge(S["b_p"], i * 2 + l + 1)
                    dve.transpose(flat3(pT[l][:, :, :]), flat3(sm[l][:, :, :])).then_inc(S["b_pT"], 1)
                for l in LANES:
                    n = i * 2 + l + 1
                    dve.wait_ge(S["b_xb"], n)
                    dve.wait_ge(S["b_y_ps"], n)
                    chain.link(dve.tensor_tensor(t_y[l][:, :, :], blocks(bank(l, 1, 0, NT)), t_xb[l][:, :, :], ALU.add))
                    b_ln1.stats(dve, chain, lambda b: t_y[l][:, b, :], l)
                for l in LANES:
                    b_ln1.apply(dve, lambda b: t_zn[l][:, b, :], lambda b: t_y[l][:, b, :], l,
                                i * 2 + l + 1).then_inc(S["b_zn"], 1)
                for l in LANES:
                    dve.wait_ge(S["b_l_ps"], i * 2 + l + 1)
                    chain.link(dve.tensor_tensor(lg[l][:, :, :], bank(l, 1, 0, 2 * NE).rearrange("p (b e) -> p b e", e=NE),
                                                 router_b[:, :, :], ALU.add))
                    chain.link(dve.tensor_reduce(lmx[l][:, :], lg[l][:, :, :], AX.X, ALU.max))
                    dve.tensor_tensor(lg[l][:, :, :], lg[l][:, :, :], lmx[l][:, :].unsqueeze(2).to_broadcast([P, 2, NE]),
                                      ALU.subtract).then_inc(S["b_lg"], 1)
                for l in LANES:
                    dve.wait_ge(S["b_le"], i * 2 + l + 1)
                    dve.tensor_copy(lg[l][:, :, :], le[l][:, :, :])
                    for b in range(2):
                        last = dve.max(m8[l][:, b, :], le[l][:, b, :])
                    chain.link(last)
                    for b in range(2):
                        last = dve.max_index(ix[l][:, b, :], m8[l][:, b, :], le[l][:, b, :])
                    chain.link(last)
                    chain.link(dve.tensor_tensor(pick[l][:, :], ix[l][:, :, 0], ix[l][:, :, 1], ALU.max))
                    for b in range(2):
                        last = dve.tensor_scalar(hot[l][:, b, :], iota[:, :], pick[l][:, b:b + 1], None, ALU.is_equal)
                    last.then_inc(S["b_hot"], 1)
                for l in LANES:
                    dve.wait_ge(S["b_moe_ps"], i * 2 + l + 1)
                    chain.link(dve.tensor_tensor(t_y[l][:, :, :], blocks(bank(l, 2, 0, NT)), t_z[l][:, :, :], ALU.add))
                    b_ln2.stats(dve, chain, lambda b: t_y[l][:, b, :], l)
                for l in LANES:
                    b_ln2.apply(dve, lambda b: t_zn[l][:, b, :], lambda b: t_y[l][:, b, :], l,
                                i * 2 + l + 1).then_inc(S["b_on"], 1)
                for l in LANES:
                    dve.wait_ge(S["b_z"], i * 2 + l + 1)
                    b_ln3.stats(dve, chain, lambda b: t_xn[l][:, b, :], l)
                for l in LANES:
                    b_ln3.apply(dve, lambda b: t_o[l][:, b, :], lambda b: t_xn[l][:, b, :], l,
                                i * 2 + l + 1).then_inc(S["b_o"], 1)
            if stage == 2:
                return
            dve.wait_ge(S["b_stored"], 32 * NB)
            dve.wait_ge(w_loaded["c"], W_ALL["c"])
            dve.wait_ge(zero_ready, 2)
            dve.wait_ge(expA_ready, 1)
            dve.tensor_scalar(negA[:, :], expA[:, :], -1.0, None, ALU.mult).then_inc(negA_ready, 1)
            with dve.Fori(0, ITER) as i:
                chain.clear()
                for l in LANES:
                    dve.wait_ge(x_loaded[l], i * 16 + (48 * ITER + 16))
                    c_ln1.stats(dve, chain, lambda b: xblk(x, i * 4, 2 * l + b), l)
                for l in LANES:
                    n = i * 2 + l + 1
                    c_ln1.apply(dve, lambda b: c_xn[l][:, b, :], lambda b: xblk(x, i * 4, 2 * l + b), l, n)
                    dve.wait_ge(S["c_r2"], n)
                    c_ln1.apply(dve, lambda b: c_xq[l][:, b, :], lambda b: xblk(x, i * 4, 2 * l + b), l, n,
                                scale=c_r2).then_inc(S["c_xn_"], 1)
                for l in LANES:
                    dve.wait_ge(S["c_xpad"], i * 2 + l + 1)
                    chain.link(dve.tensor_scalar(cv[l][:, :], xpad[l][:, 3:3 + NT], vec("conv_w", 3), vec("conv_b"),
                                                 ALU.mult, ALU.add))
                    for k in (2, 1, 0):
                        ins = dve.scalar_tensor_tensor(out=cv[l][:, :], in0=xpad[l][:, k:k + NT], scalar=vec("conv_w", k),
                                                       in1=cv[l][:, :], op0=ALU.mult, op1=ALU.add)
                        if k:
                            chain.link(ins)
                    ins.then_inc(S["c_cv_"], 1)
                for l in LANES:
                    dve.wait_ge(S["c_dt_ps"], i * 2 + l + 1)
                    dve.tensor_scalar(zb[l][:, :], bank(l, 1, 0, NT), vec("dt_b"), None, ALU.add).then_inc(S["c_zb_"], 1)
                for l in LANES:
                    dve.wait_ge(S["c_c_ps"], i * 2 + l + 1)
                    dve.tensor_tensor(flat3(bbd[l][:, :, :]), bank(l, 0), bmask[:, :, :, :].rearrange("p k n c -> p (k n c)"),
                                      ALU.mult).then_inc(S["c_bbd"], 1)
                    dve.tensor_tensor(cbd[l][:, :], bank(l, 2, 0, NT), cmask[:, :], ALU.mult).then_inc(S["c_cbd"], 1)
                for l in LANES:
                    dve.wait_ge(S["c_sp_"], i * 2 + l + 1)
                    chain.link(dve.scalar_tensor_tensor(out=dt[l][:, :], in0=zb[l][:, :], scalar=0.0, in1=sp_[l][:, :],
                                                        op0=ALU.max, op1=ALU.add))
                    dve.tensor_tensor_scan(cdt[l][:, :], first[:, :], dt[l][:, :], 0.0, ALU.mult, ALU.add
                                           ).then_inc(S["c_dt_"], 1)
                    dve.tensor_tensor(wall[l][:, 0:NT], dt[l][:, :], xs[l][:, :], ALU.mult)
                for l in LANES:
                    dve.wait_ge(S["c_dec"], i * 2 + l + 1)
                    chain.link(dve.tensor_scalar(dec[l][:, :, :, :].rearrange("p a c t -> p (a c t)"),
                                                 dec[l][:, :, :, :].rearrange("p a c t -> p (a c t)"), 1.0, None, ALU.min))
                    dve.sem_inc(S["c_decm"], 1)
                    for j in range(1, CH):
                        w0 = wall[l][:, OFF[j - 1]:OFF[j]].rearrange("p (c t) -> p c t", t=CH - j + 1)
                        w1 = wall[l][:, OFF[j]:OFF[j + 1]].rearrange("p (c t) -> p c t", t=CH - j)
                        ins = dve.tensor_tensor(w1, dec[l][:, 0, :, j:CH], w0[:, :, 0:CH - j], ALU.mult)
                        if j < CH - 1:
                            chain.link(ins)
                    ins.then_inc(S["c_wall"], 1)
                for l in LANES:
                    n = i * 2 + l + 1
                    dve.wait_ge(S["c_wall"], n)
                    dve.wait_ge(S["c_g1_ps"], n)
                    for b, (j0, j1) in zip((3, 1, 2), PAIR_BANKS):
                        ins = dve.tensor_tensor(term[l][:, OFF[j0]:OFF[j1]], wall[l][:, OFF[j0]:OFF[j1]],
                                                bank(l, b, 0, OFF[j1] - OFF[j0]), ALU.mult)
                    ins.then_inc(S["c_term"], 1)
                    dve.wait_ge(S["c_term"], n)
                    y = term[l][:, 0:NT].rearrange("p (c t) -> p c t", t=CH)
                    for j in range(1, CH):
                        chain.link(dve.tensor_tensor(y[:, :, j:CH], y[:, :, j:CH],
                                                     term[l][:, OFF[j]:OFF[j + 1]].rearrange("p (c t) -> p c t", t=CH - j),
                                                     ALU.add))
                for l in LANES:
                    n = i * 2 + l + 1
                    dve.wait_ge(S["c_d0"], n)
                    dve.wait_ge(S["c_st_ps"], n)
                    dve.tensor_tensor_scan(flat3(hs[l][:, :, :]), flat3(d0[l][:, :, :]), bank(l, 0), 0.0,
                                           ALU.mult, ALU.add).then_inc(S["c_hs"], 1)
                for l in LANES:
                    n = i * 2 + l + 1
                    dve.wait_ge(S["c_yi_ps"], n)
                    chain.link(dve.tensor_tensor(yi[l][:, :], bank(l, 2, 0, NT),
                                                 dec[l][:, 1, :, :].rearrange("p c t -> p (c t)"), ALU.mult))
                    chain.link(dve.tensor_tensor(yi[l][:, :], yi[l][:, :], term[l][:, 0:NT], ALU.add))
                    chain.link(dve.scalar_tensor_tensor(out=yi[l][:, :], in0=xs[l][:, :], scalar=vec("D_param"),
                                                        in1=yi[l][:, :], op0=ALU.mult, op1=ALU.add))
                    dve.wait_ge(S["c_zs_"], n)
                    dve.tensor_tensor(ya[l][:, :], yi[l][:, :], zs[l][:, :], ALU.mult).then_inc(S["c_y"], 1)
                for l in LANES:
                    dve.wait_ge(S["c_out_ps"], i * 2 + l + 1)
                    chain.link(dve.tensor_tensor(c_r[l][:, :, :], blocks(bank(l, 3, 0, NT)), c_xn[l][:, :, :], ALU.add))
                    c_ln2.stats(dve, chain, lambda b: c_r[l][:, b, :], l)
                for l in LANES:
                    c_ln2.apply(dve, lambda b: c_o[l][:, b, :], lambda b: c_r[l][:, b, :], l,
                                i * 2 + l + 1).then_inc(S["c_o_"], 1)
            if stage == 3:
                return
            dve.wait_ge(w_loaded["d"], W_ALL["d"])
            dve.wait_ge(S["c_x"], NB)
            with dve.Fori(0, ITER_MLP) as i:
                chain.clear()
                for l in LANES:
                    d_ln1.stats(dve, chain, lambda b: xblk(x, i * 8, 4 * l + b), l)
                for l in LANES:
                    d_ln1.apply(dve, lambda b: d_xn[l][:, b, :], lambda b: xblk(x, i * 8, 4 * l + b), l,
                                i * 2 + l + 1).then_inc(S["d_xn_"], 1)
                for l in LANES:
                    for m in range(HID):
                        dve.wait_ge(m_gate[l], i * HID + m + 1)
                        dve.scalar_tensor_tensor(out=h0[l][:, m, :], in0=bank(l, 2 * (m % 2) + 1), scalar=vec("w2_s", m),
                                                 in1=gate[l][m % 2][:, :], op0=ALU.mult, op1=ALU.mult).then_inc(m_h0[l], 1)
                for l in LANES:
                    dve.wait_ge(S["d_y_ps"], i * 2 + l + 1)
                    chain.link(dve.tensor_tensor(flat3(d_y[l][:, :, :]), bank(l, 0), flat3(w3_s[:, :, :]), ALU.mult))
                    d_ln2.stats(dve, chain, lambda b: d_y[l][:, b, :], l)
                for l in LANES:
                    d_ln2.apply(dve, lambda b: d_o[l][:, b, :], lambda b: d_y[l][:, b, :], l,
                                i * 2 + l + 1).then_inc(S["d_o_"], 1)

        @block.tensor
        def _(pe):
            pe.wait_ge(w_loaded["a"], W_ALL["a"])
            pe.wait_ge(cast_ready, 4)

            def turn(l, b, src, k, ready, n, done):
                pe.wait_ge(ready, n)
                for c in range(k):
                    last = pe.transpose(bank(l, b, P * c, P * c + P), src[l][:, c, :], ident[:, :])
                last.then_inc(done, 1)

            def project(l, w, qk_ps, v_ps):
                pe.matmul(bank(l, 0, 0, NT), w[:, 0, :], xnT[l][:, :], start=True, stop=True)
                pe.matmul(bank(l, 1, 0, NT), w[:, 1, :], xnT[l][:, :], start=True, stop=True).then_inc(qk_ps, 1)
                for j in range(NBLK):
                    last = pe.matmul(bank(l, 2 + j // 4, P * (j % 4), P * (j % 4) + P), flat3(xnR[l][:, j, :, :]),
                                     w[:, 2, :], start=True, stop=True)
                last.then_inc(v_ps, 1)

            def out_tokens(l, b, src, w, done):
                for c in range(2):
                    last = pe.matmul(bank(l, b, P * c, P * c + P), src[l][:, P * c:P * c + P], w, start=True, stop=True)
                last.then_inc(done, 1)

            with pe.Fori(0, ITER) as i:
                for l in LANES:
                    turn(l, 0, t_xn, 2, S["a_xn"], i * 2 + l + 1, S["a_t_ps"])
                for l in LANES:
                    pe.wait_ge(S["a_xnT"], i * 2 + l + 1)
                    project(l, wa, S["a_qk_ps"], S["a_v_ps"])
                for l in LANES:
                    n = i * 2 + l + 1
                    pe.wait_ge(S["a_qT"], n)
                    pe.wait_ge(S["a_hbd"], n)
                    pe.wait_ge(S["a_vbd"], n)
                    for g in range(G):
                        pe.matmul(bank(l, g, 0, NBLK * SPAN), rep[heads(g), :], band[heads(g), :], start=True, stop=True)
                        for j in range(NBLK):
                            w = SPAN if j < NBLK - 1 else BLK
                            last = pe.matmul(bank(l, g, SPAN * j, SPAN * j + w), flat3(hbd[l][heads(g), j, :, :]),
                                             qT[l][heads(g), BLK * j:BLK * j + w], start=False, stop=True,
                                             skip_group_check=True)
                    last.then_inc(S["a_s_ps"], 1)
                for l in LANES:
                    pe.wait_ge(S["a_tau"], i * 2 + l + 1)
                    for g in range(G):
                        for j in range(NBLK):
                            w = SPAN if j < NBLK - 1 else BLK
                            last = pe.matmul(ps[heads(g), 4 * l, BLK * j:BLK * j + w], vbd[l][:, j, heads(g)],
                                             tau[l][:, g, SPAN * j:SPAN * j + w], start=(j == 0),
                                             stop=True, skip_group_check=True)
                    last.then_inc(S["a_m_ps"], 1)
                for l in LANES:
                    pe.wait_ge(S["a_msgT"], i * 2 + l + 1)
                    out_tokens(l, 1, msgT, wa[:, 3, :], S["a_y_ps"])
            if stage == 1:
                return
            pe.wait_ge(w_loaded["b"], W_ALL["b"])
            with pe.Fori(0, ITER) as i:
                for l in LANES:
                    turn(l, 0, t_xn, 2, S["b_xn"], i * 2 + l + 1, S["b_t_ps"])
                for l in LANES:
                    pe.wait_ge(S["b_xnT"], i * 2 + l + 1)
                    project(l, wf, S["b_qk_ps"], S["b_v_ps"])
                for l in LANES:
                    n = i * 2 + l + 1
                    pe.wait_ge(S["b_kT"], n)
                    pe.wait_ge(S["b_hbd"], n)
                    pe.wait_ge(S["b_vbd"], n)
                    for g in range(G):
                        pe.matmul(bank(l, g, 0, NT), rep[heads(g), :], same[heads(g), :], start=True, stop=True)
                        for j in range(NBLK):
                            last = pe.matmul(bank(l, g, BLK * j, BLK * j + BLK), flat3(hbd[l][heads(g), j, :, :]),
                                             qT[l][heads(g), BLK * j:BLK * j + BLK], start=False, stop=True,
                                             skip_group_check=True)
                    last.then_inc(S["b_s_ps"], 1)
                for l in LANES:
                    pe.wait_ge(S["b_pT"], i * 2 + l + 1)
                    for g in range(G):
                        for j in range(NBLK):
                            last = pe.matmul(ps[heads(g), 4 * l, BLK * j:BLK * j + BLK], vbd[l][:, j, heads(g)],
                                             pT[l][:, g, BLK * j:BLK * j + BLK], start=True, stop=True)
                    last.then_inc(S["b_m_ps"], 1)
                for l in LANES:
                    pe.wait_ge(S["b_msgT"], i * 2 + l + 1)
                    out_tokens(l, 1, msgT, wf[:, 3, :], S["b_y_ps"])
                for l in LANES:
                    turn(l, 0, t_z, 2, S["b_h"], i * 2 + l + 1, S["b_ht_ps"])
                for l in LANES:
                    pe.wait_ge(S["b_hT"], i * 2 + l + 1)
                    for c in range(2):
                        last = pe.matmul(bank(l, 1, NE * c, NE * c + NE), hT[l][:, P * c:P * c + P], w_router[:, :],
                                         start=True, stop=True)
                    last.then_inc(S["b_l_ps"], 1)
                for l in LANES:
                    pe.wait_ge(S["b_hot"], i * 2 + l + 1)
                    for c in range(2):
                        last = pe.transpose(ps[0:NE, 4 * l + 1, P * c:P * c + P], hot[l][:, c, :], ident[:, :])
                    last.then_inc(S["b_hott_ps"], 1)
                for l in LANES:
                    pe.wait_ge(S["b_hotT"], i * 2 + l + 1)
                    for c in range(2):
                        pe.matmul(bank(l, 2, P * c, P * c + P), hotT[l][:, P * c:P * c + P], b_e2[:, :],
                                  start=(c == 0), stop=True, skip_group_check=True)
                for e in range(NE + 1):
                    for l in LANES:
                        if e < NE:
                            if e >= 2:
                                pe.wait_ge(he_ready[l], i * NE + e - 1)
                            bk = bank(l, 3 * (e % 2), 0, NT)
                            pe.matmul(bk, negsel[:, e, :], hotTb[l][:, :], start=True, stop=False)
                            pe.matmul(bk, w_e1[:, e, :], hT[l][:, :], start=False, stop=True).then_inc(he_ps[l], 1)
                    for l in LANES:
                        if e > 0:
                            pe.wait_ge(he_ready[l], i * NE + e)
                            for c in range(2):
                                last = pe.matmul(bank(l, 2, P * c, P * c + P), he[l][(e - 1) % 2][:, P * c:P * c + P],
                                                 w_e2[:, e - 1, :], start=False, stop=True, skip_group_check=True)
                            last.then_inc(e_done[l], 1)
                            if e == NE:
                                pe.wait_ge(e_done[l], i * NE + NE)
                                pe.sem_inc(S["b_moe_ps"], 1)
            if stage == 2:
                return
            pe.wait_ge(w_loaded["c"], W_ALL["c"])
            with pe.Fori(0, ITER) as i:
                for l in LANES:
                    turn(l, 0, c_xq, 2, S["c_xn_"], i * 2 + l + 1, S["c_t_ps"])
                for l in LANES:
                    pe.wait_ge(S["c_xT_"], i * 2 + l + 1)
                    pe.matmul(bank(l, 1, 0, NT), w_in[:, 0:D], c_xT[l][:, :], start=True, stop=True)
                    pe.matmul(bank(l, 2, 0, NT), w_in[:, D:2 * D], c_xT[l][:, :], start=True, stop=True
                              ).then_inc(S["c_in_ps"], 1)
                for l in LANES:
                    n = i * 2 + l + 1
                    pe.wait_ge(S["c_zs_"], n)
                    pe.wait_ge(S["c_xs_"], n)
                    pe.matmul(bank(l, 1, 0, NT), w_dt[:, :], xs[l][:, :], start=True, stop=True).then_inc(S["c_dt_ps"], 1)
                    pe.matmul(ps[0:DS, 4 * l + 3, 0:NT], w_b[:, :], xs[l][:, :], start=True, stop=True)
                    pe.matmul(ps[0:DS, 4 * l + 3, NT:2 * NT], w_c[:, :], xs[l][:, :], start=True, stop=True
                              ).then_inc(S["c_b_ps"], 1)
                    for c in range(2):
                        pe.matmul(bank(l, 0, NT * c, NT * c + NT), xs[l][:, P * c:P * c + P], flat3(w_bR[:, :, :]),
                                  start=True, stop=True)
                    pe.matmul(bank(l, 2, 0, NT), flat3(w_cR[:, :, :]), xs[l][:, :], start=True, stop=True
                              ).then_inc(S["c_c_ps"], 1)
                for l in LANES:
                    n = i * 2 + l + 1
                    pe.wait_ge(S["c_prod"], n)
                    pe.wait_ge(S["c_zb_"], n)
                    pe.wait_ge(S["c_cbd"], n)
                    for b, (j0, j1) in zip((3, 1, 2), PAIR_BANKS):
                        last = pe.matmul(bank(l, b, 0, OFF[j1] - OFF[j0]), ones[0:DS, :], prod[l][:, OFF[j0]:OFF[j1]],
                                         start=True, stop=True)
                    last.then_inc(S["c_g1_ps"], 1)
                for l in LANES:
                    n = i * 2 + l + 1
                    pe.wait_ge(S["c_wend"], n)
                    for c in range(2):
                        last = pe.transpose(bank(l, 0, P * c, P * c + P),
                                            wend[l][:, 16 * c:16 * c + 16, :].rearrange("p c t -> p (c t)"), ident[:, :])
                    last.then_inc(S["c_wt_ps"], 1)
                for l in LANES:
                    pe.wait_ge(S["c_wendT"], i * 2 + l + 1)
                    for c in range(2):
                        o = bank(l, 0).rearrange("p (n c) -> p n c", c=NCH)[:, :, 16 * c:16 * c + 16]
                        last = pe.matmul(o, wendT[l][:, c, :], bbd[l][:, c, :].rearrange("p (n c) -> p n c", c=16),
                                         start=True, stop=True)
                    last.then_inc(S["c_st_ps"], 1)
                for l in LANES:
                    n = i * 2 + l + 1
                    pe.wait_ge(S["c_term"], n)
                    pe.wait_ge(S["c_hc"], n)
                    for c in range(4):
                        last = pe.transpose(bank(l, 1, P * c, P * c + P),
                                            hc[l][:, 8 * c:8 * c + 8, :].rearrange("p c n -> p (c n)"), ident[:, :])
                    last.then_inc(S["c_hct_ps"], 1)
                for l in LANES:
                    pe.wait_ge(S["c_hcT"], i * 2 + l + 1)
                    for c in range(4):
                        last = pe.matmul(bank(l, 2, 64 * c, 64 * c + 64), hcT[l][:, c, :], cbd[l][:, 64 * c:64 * c + 64],
                                         start=True, stop=True)
                    last.then_inc(S["c_yi_ps"], 1)
                for l in LANES:
                    pe.wait_ge(S["c_y"], i * 2 + l + 1)
                    out_tokens(l, 3, ya, w_out[:, :], S["c_out_ps"])
            if stage == 3:
                return
            pe.wait_ge(w_loaded["d"], W_ALL["d"])
            with pe.Fori(0, ITER_MLP) as i:
                for l in LANES:
                    turn(l, 0, d_xn, 4, S["d_xn_"], i * 2 + l + 1, S["d_t_ps"])
                for l in LANES:
                    pe.wait_ge(S["d_xT_"], i * 2 + l + 1)
                    for m in range(HID):
                        if m >= 2:
                            pe.wait_ge(m_h0[l], i * HID + m - 1)
                        pe.matmul(bank(l, 2 * (m % 2)), w_m1[:, P * m:P * m + P], d_xT[l][:, :], start=True, stop=True)
                        pe.matmul(bank(l, 2 * (m % 2) + 1), w_m2[:, P * m:P * m + P], d_xT[l][:, :], start=True, stop=True
                                  ).then_inc(m_gu_ps[l], 1)
                for w, src, ready, done in ((w_h1, h0, m_h0, m_h1_ps), (w_h2, h1, m_h1, m_h2_ps)):
                    for l in LANES:
                        pe.wait_ge(ready[l], i * HID + HID)
                        for m in range(HID):
                            for k in range(HID):
                                last = pe.matmul(bank(l, m), w[:, k, P * m:P * m + P], src[l][:, k, :],
                                                 start=(k == 0), stop=(k == HID - 1))
                            last.then_inc(done[l], 1)
                for l in LANES:
                    pe.wait_ge(m_h2[l], i * HID + HID)
                    for c in range(4):
                        for k in range(HID):
                            last = pe.matmul(bank(l, 0, P * c, P * c + P), h0[l][:, k, P * c:P * c + P], w_m3[:, k, :],
                                             start=(k == 0), stop=(k == HID - 1))
                    last.then_inc(S["d_y_ps"], 1)


def lay_out(inp):
    import numpy as np
    f = np.float32
    v = {k: np.asarray(t) for k, t in inp.items()}
    p, col = np.arange(P), np.arange(D)
    r = {"x": v["L0_attn_x"]}
    wkv = v["L0_attn_wkv"].reshape(16, 2, HD, D)
    r["wa"] = np.stack([v["L0_attn_wq"].T, wkv[:, 0].reshape(D, D).T, wkv[:, 1].reshape(D, D).T, v["L0_attn_wo"].T], 1)
    wi = v["L0_ffn_in_proj_w"]
    r["wf"] = np.stack([wi[0:D].T, wi[D:2 * D].T, wi[2 * D:].T, v["L0_ffn_out_w"].T], 1)
    r["w_router"] = v["L0_ffn_router_w"].T
    r["w_e1"] = v["L0_ffn_w1"].transpose(2, 0, 1)
    r["w_e2"] = v["L0_ffn_w2"].transpose(2, 0, 1)
    r["b_e2"] = v["L0_ffn_b2"]
    r["rows"] = np.broadcast_to(np.stack([v[n] for n in (
        "L0_attn_gamma", "L0_attn_beta", "L0_ffn_out_b", "L0_ffn_ln1_g", "L0_ffn_ln1_b", "L0_ffn_ln2_g",
        "L0_ffn_ln2_b")])[None, :, None, :], (P, 7, 2, D))
    r["router_b"] = np.broadcast_to(v["L0_ffn_router_b"][None, None, :], (P, 2, NE))
    bi = v["L0_ffn_in_proj_b"].reshape(3, D)
    blk = lambda t: t.reshape(HID, P).T
    cols = {"bq": bi[0][:, None], "bk": bi[1][:, None], "bv": bi[2][:, None], "b1": v["L0_ffn_b1"].T,
            "ln_g": v["L1_attn_ln_g"][:, None], "ln_b": v["L1_attn_ln_b"][:, None], "conv_w": v["L1_attn_conv_w"][:, 0, :],
            "conv_b": v["L1_attn_conv_b"][:, None], "dt_b": v["L1_attn_dt_b"][:, None],
            "log_A": v["L1_attn_log_A"][:, None], "D_param": v["L1_attn_D_param"][:, None],
            "w1_s": blk(v["L1_ffn_w1_s"]), "w2_s": blk(v["L1_ffn_w2_s"]), "h1_s": blk(v["L1_ffn_h1_s"]),
            "h2_s": blk(v["L1_ffn_h2_s"])}
    r["pp"] = np.concatenate([cols[n] for n in PP], 1)
    r["w_in"], r["w_dt"], r["w_b"], r["w_c"], r["w_out"] = (
        v["L1_attn_" + n] for n in ("W_in", "dt_w", "B_w", "C_w", "W_out"))
    r["w_bR"] = np.broadcast_to(v["L1_attn_B_w"][:, :, None], (D, DS, 16))
    r["w_cR"] = np.broadcast_to(v["L1_attn_C_w"][:, None, :], (D, 8, DS))
    r["w_m1"], r["w_m2"] = v["L1_ffn_w1_w"].T, v["L1_ffn_w2_w"].T
    for n, k in (("w_h1", "h1_w"), ("w_h2", "h2_w"), ("w_m3", "w3_w")):
        t = v["L1_ffn_" + k].T
        r[n] = t.reshape(HID, P, t.shape[1]).transpose(1, 0, 2)
    r["w3_s"] = np.broadcast_to(v["L1_ffn_w3_s"][None, None, :], (P, HID, D))
    r["c_ident"] = np.eye(P, dtype=f)
    r["c_headmask"] = (p[:, None] // HD % 4 == np.arange(4)[None, :]).astype(f)
    r["c_vmask"] = np.tile((p[:, None] // BLK == col[None, :] // HD % 4).astype(f), (1, 4))
    r["c_rep"] = (p[:, None] % BLK == p[None, :] % BLK).astype(f)
    gap = np.arange(SPAN)[None, :] - (p % BLK)[:, None]
    r["c_band"] = np.tile(np.where((gap >= 1) & (gap <= WIN), 0.0, NEG).astype(f), (1, NBLK))
    own = (p % BLK)[:, None] // NB == np.arange(BLK)[None, :] // NB
    r["c_same"] = np.tile(np.where(own, 0.0, NEG).astype(f), (1, NBLK))
    e = np.arange(NE)
    r["c_negsel"] = np.where(e[:, None, None] == e[None, :, None], 0.0, NEG).astype(f) * np.ones((1, 1, P), f)
    r["c_iota"] = np.broadcast_to(e.astype(f), (P, NE))
    r["c_bmask"] = np.broadcast_to((p[:, None] // CH == np.arange(16)[None, :]).astype(f)[:, None, None, :], (P, 2, DS, 16))
    r["c_cmask"] = (p[:, None] // DS == np.arange(NT)[None, :] % 64 // CH).astype(f)
    r["c_first"] = np.broadcast_to((np.arange(NT) % CH != 0).astype(f), (P, NT))
    return {k: np.ascontiguousarray(t) for k, t in r.items()}


def kernel(**inputs):
    import concourse.bacc as _bacc
    from concourse import mybir as _mybir
    from concourse.bass_utils import run_bass_kernel_spmd as _run

    nc = _bacc.Bacc("TRN2", target_bir_lowering=False, num_devices=1)
    arrays, args = {}, {}
    for name, v in lay_out(inputs).items():
        arrays[f"in_{name}"] = v
        args[name] = nc.dram_tensor(f"in_{name}", v.shape, _mybir.dt.from_np(v.dtype), kind="ExternalInput").ap()
    out = nc.dram_tensor("out_x", (NB, NT, D), F32, kind="ExternalOutput").ap()
    build(nc, args, out)
    r = _run(nc, [arrays], core_ids=[0])
    return r.results[0]["out_x"]
```

```python
from contextlib import ExitStack

import concourse.bass as bass
from concourse import mybir

F32 = mybir.dt.float32
BF16 = mybir.dt.bfloat16
F32R = mybir.dt.float32r
U32 = mybir.dt.uint32
ALU = mybir.AluOpType
ACT = mybir.ActivationFunctionType
AX = mybir.AxisListType

P = 128
D = 128
NB, NT = 16, 256
HD = 8
G = 4
BLK = 32
WIN = 16
SPAN = BLK + WIN
NBLK = NT // BLK
NE = 8
DS = 16
CH = 8
NCH = NT // CH
HID = 4
EPS = 1e-5
NEG = -1e12
ATT_SCALE = float(HD) ** -0.5
LANES = (0, 1)
ITER = NB // 2
ITER_MLP = NB // 4

PP = {}
for _name, _n in (("bq", 1), ("bk", 1), ("bv", 1), ("b1", NE), ("ln_g", 1), ("ln_b", 1), ("conv_w", 4), ("conv_b", 1),
                  ("dt_b", 1), ("log_A", 1), ("D_param", 1), ("w1_s", HID), ("w2_s", HID), ("h1_s", HID), ("h2_s", HID)):
    PP[_name] = sum(n for n, _ in PP.values()), _n
    PP[_name] = (_n, sum(n for k, (n, _) in PP.items() if k != _name))
NPP = sum(n for n, _ in PP.values())

OFF = [sum(NCH * (CH - k) for k in range(j)) for j in range(CH + 1)]
PAIR_BANKS = ((0, 2), (2, 5), (5, 8))


class Chain:

    def __init__(self, eng, sem):
        self.eng, self.sem, self.count = eng, sem, 0

    def clear(self):
        self.eng.sem_clear(self.sem)
        self.count = 0

    def link(self, ins):
        self.count += 1
        ins.then_inc(self.sem, 1)
        self.eng.wait_ge(self.sem, self.count)


def pipelined(eng, step, ahead, behind, tiles):
    def one(n):
        step(n, n % 2, lambda k: 0 <= n + k < tiles)

    lo, hi = behind, tiles - ahead
    turns = (hi - lo) // 2
    for n in range(-ahead, lo):
        one(n)
    with eng.Fori(0, turns) as i:
        for k in range(2):
            step(i * 2 + (lo + k), (lo + k) % 2, lambda d: True)
    for n in range(lo + 2 * turns, tiles + behind):
        one(n)


class LayerNorm:

    def __init__(self, name, k, sb, sem):
        self.k = k
        self.st = [sb(f"{name}_st{l}", [P, k, 6]) for l in LANES]
        self.mv = [sb(f"{name}_mv{l}", [P, k, 2]) for l in LANES]
        self.ve = [sb(f"{name}_ve{l}", [P, k]) for l in LANES]
        self.rs = [sb(f"{name}_rs{l}", [P, k]) for l in LANES]
        self.mv_ready = sem(f"{name}_mv_ready")
        self.rstd_ready = sem(f"{name}_rstd_ready")

    def stats(self, dve, chain, src, l):
        for b in range(self.k):
            last = dve.bn_stats(self.st[l][:, b, :], src(b))
        chain.link(last)
        for b in range(self.k):
            last = dve.bn_aggr(self.mv[l][:, b, :], self.st[l][:, b, :])
        last.then_inc(self.mv_ready, 1)

    def rstd(self, pool, chain, eps, half, l, n):
        pool.wait_ge(self.mv_ready, n)
        chain.link(pool.tensor_tensor(self.ve[l][:, :], self.mv[l][:, :, 1], eps[:, 0:self.k], ALU.add))
        pool.tensor_tensor(self.rs[l][:, :], self.ve[l][:, :], half[:, 0:self.k], ALU.pow).then_inc(self.rstd_ready, 1)

    def apply(self, dve, out, src, l, n, scale=None):
        rs = self.rs if scale is None else scale
        dve.wait_ge(self.rstd_ready, n)
        for b in range(self.k):
            last = dve.tensor_scalar(out(b), src(b), self.mv[l][:, b, 0:1], rs[l][:, b:b + 1],
                                     ALU.subtract, ALU.mult)
        return last


def build(nc, a, out, stage=4):
    with ExitStack() as ctx:
        def sb(name, shape, dt=F32):
            return ctx.enter_context(nc.sbuf_tensor(name, shape, dt))

        def sem(name):
            return ctx.enter_context(nc.semaphore(name))

        ps = ctx.enter_context(nc.psum_tensor("ps", [P, 8, 512], F32))

        x = sb("x", [P, 2 * NB, D])
        ident = sb("ident", [P, P])
        headmask = sb("headmask", [P, G])
        vmask = sb("vmask", [P, BLK])
        rep = sb("rep", [P, P], BF16)
        eps = sb("eps", [P, 4])
        half = sb("half", [P, 4])
        pp = sb("pp", [P, NPP])
        wa = sb("wa", [P, 4, D])
        wf = sb("wf", [P, 4, D])
        w_router = sb("w_router", [P, NE])
        w_e1 = sb("w_e1", [P, NE, D])
        w_e2 = sb("w_e2", [P, NE, D])
        b_e2 = sb("b_e2", [NE, D])
        rows = sb("rows", [P, 7, 2, D])
        router_b = sb("router_b", [P, 2, NE])
        iota = sb("iota", [P, NE])
        negsel = sb("negsel", [NE, NE, P], BF16)
        band = sb("band", [P, NBLK * SPAN], BF16)
        same = sb("same", [P, NBLK * BLK], BF16)
        w_in = sb("w_in", [P, 2 * D])
        w_dt = sb("w_dt", [P, D])
        w_b = sb("w_b", [P, DS])
        w_c = sb("w_c", [P, DS])
        w_bR = sb("w_bR", [P, DS, 16])
        w_cR = sb("w_cR", [P, 8, DS])
        w_out = sb("w_out", [P, D])
        bmask = sb("bmask", [P, 2, DS, 16])
        cmask = sb("cmask", [P, NT])
        first = sb("first", [P, NT])
        ones = sb("ones", [P, P])
        expA = sb("expA", [P, 1])
        negA = sb("negA", [P, 1])
        w_m1 = sb("w_m1", [P, HID * D])
        w_m2 = sb("w_m2", [P, HID * D])
        w_h1 = sb("w_h1", [P, HID, HID * D])
        w_h2 = sb("w_h2", [P, HID, HID * D])
        w_m3 = sb("w_m3", [P, HID, D])
        w3_s = sb("w3_s", [P, HID, D])

        fill_done, cast_ready, expA_ready, negA_ready, zero_ready = (sem(n) for n in (
            "fill_done", "cast_ready", "expA_ready", "negA_ready", "zero_ready"))
        w_loaded = {k: sem("w_loaded_" + k) for k in "abcd"}
        x_loaded = [sem(f"x_loaded{l}") for l in LANES]
        pool_chain, dve_chain, act_chain = sem("pool_chain"), sem("dve_chain"), sem("act_chain")

        loads = {
            "a": [(ident[:, :], "c_ident"), (headmask[:, :], "c_headmask"), (vmask[:, :], "c_vmask"),
                  (wa[:, :, :], "wa"), (rows[:, :, :, :], "rows"), (pp[:, :], "pp")],
            "b": [(wf[:, :, :], "wf"), (w_router[:, :], "w_router"), (w_e1[:, :, :], "w_e1"), (w_e2[:, :, :], "w_e2"),
                  (b_e2[:, :], "b_e2"), (router_b[:, :, :], "router_b"), (iota[:, :], "c_iota")],
            "c": [(w_in[:, :], "w_in"), (w_dt[:, :], "w_dt"), (w_b[:, :], "w_b"), (w_c[:, :], "w_c"),
                  (w_bR[:, :, :], "w_bR"), (w_cR[:, :, :], "w_cR"), (w_out[:, :], "w_out"),
                  (bmask[:, :, :, :], "c_bmask"), (cmask[:, :], "c_cmask"), (first[:, :], "c_first")],
            "d": [(w_m1[:, :], "w_m1"), (w_m2[:, :], "w_m2"), (w_h1[:, :, :], "w_h1"), (w_h2[:, :, :], "w_h2"),
                  (w_m3[:, :, :], "w_m3"), (w3_s[:, :, :], "w3_s")],
        }
        W_ALL = {k: 16 * len(v) for k, v in loads.items()}
        W_ALL["a"] += 16 * 4

        def vec(name, c=0):
            return pp[:, PP[name][1] + c:PP[name][1] + c + 1]

        def tok(name, k=2):
            return [sb(f"{name}{l}", [P, k, D]) for l in LANES]

        def chan(name):
            return [sb(f"{name}{l}", [P, NT]) for l in LANES]

        def flat3(t):
            return t.rearrange("p a b -> p (a b)")

        outer = ctx
        ctx = ExitStack()
        stage_f = [sb("stage_rep", [P, P]), sb("stage_band", [P, NBLK * SPAN]), sb("stage_same", [P, NBLK * BLK]),
                   sb("stage_negsel", [NE, NE, P])]
        xB = sb("xB", [P, 2 * NB, D])
        t_xn, t_xb, t_y, t_zn, t_zg, t_z, t_o, t_h, t_on, t_og, t_yo = (
            tok("t_" + n) for n in ("xn", "xb", "y", "zn", "zg", "z", "o", "h", "on", "og", "yo"))
        xh, xl = ([sb(f"{n}{l}", [P, NT], F32R) for l in LANES] for n in ("xh", "xl"))
        wa_h, wa_l, wf_h, wf_l = (sb(n, [P, 3, D], F32R) for n in ("wa_h", "wa_l", "wf_h", "wf_l"))
        msgT = chan("msgT")
        qk, rest = ([sb(f"{n}{l}", [P, 2, NT]) for l in LANES] for n in ("qk", "rest"))
        parts = [sb(f"parts{l}", [P, 3, 2, NT], BF16) for l in LANES]
        hbd = [sb(f"hbd{l}", [P, 3, NBLK, 4, BLK], BF16) for l in LANES]
        vT = [sb(f"vT{l}", [P, NT]) for l in LANES]
        vbd = [sb(f"vbd{l}", [P, NBLK, D]) for l in LANES]
        with ExitStack() as only_a:
            tau = [only_a.enter_context(nc.sbuf_tensor(f"tau{l}", [P, G, NBLK * SPAN], F32)) for l in LANES]
        sm = [sb(f"sm{l}", [P, G * NBLK, BLK]) for l in LANES]
        ex = [sb(f"ex{l}", [P, G * NBLK, BLK]) for l in LANES]
        pT = [sb(f"pT{l}", [P, G, NBLK * BLK]) for l in LANES]
        mx, den, rden = ([sb(f"{n}{l}", [P, G * NBLK]) for l in LANES] for n in ("mx", "den", "rden"))
        hT = chan("hT")
        lg, le = ([sb(f"{n}{l}", [P, 2, NE]) for l in LANES] for n in ("lg", "le"))
        lmx = [sb(f"lmx{l}", [P, 2]) for l in LANES]
        m8 = [sb(f"m8{l}", [P, 2, 8]) for l in LANES]
        ix = [sb(f"ix{l}", [P, 2, 8], U32) for l in LANES]
        pick = [sb(f"pick{l}", [P, 2]) for l in LANES]
        hot = [sb(f"hot{l}", [P, 2, NE]) for l in LANES]
        hotT = [sb(f"hotT{l}", [NE, NT]) for l in LANES]
        hotTb = [sb(f"hotTb{l}", [NE, NT], BF16) for l in LANES]
        he = [sb(f"he{c}", [P, NT]) for c in range(2)]
        a_ln1, a_ln2, a_ln3, b_ln0, b_ln1, b_ln2, b_ln3 = (
            LayerNorm(n, 2, sb, lambda m: outer.enter_context(nc.semaphore(m)))
            for n in ("a_ln1", "a_ln2", "a_ln3", "b_ln0", "b_ln1", "b_ln2", "b_ln3"))
        ctx.close()

        ctx = ExitStack()
        c_xn, c_xq, c_r, c_o = (tok("c_" + n) for n in ("xn", "xq", "r", "o"))
        c_xT, zs, cv, xs, zb, sp_, dt, u, cdt, ya, yi = (
            chan("c_" + n) for n in ("xT", "zs", "cv", "xs", "zb", "sp", "dt", "u", "cdt", "ya", "yi"))
        xpad = [sb(f"xpad{l}", [P, 3 + NT]) for l in LANES]
        dec = [sb(f"dec{l}", [P, 2, NCH, CH]) for l in LANES]
        bcT = [sb(f"bcT{l}", [DS, 2, NCH, CH]) for l in LANES]
        prod = [sb(f"prod{l}", [DS, OFF[CH]]) for l in LANES]
        wall = [sb(f"wall{l}", [P, OFF[CH]]) for l in LANES]
        term = [sb(f"term{l}", [P, OFF[CH]]) for l in LANES]
        wend = [sb(f"wend{l}", [P, NCH, CH]) for l in LANES]
        wendT = [sb(f"wendT{l}", [P, 2, D]) for l in LANES]
        bbd = [sb(f"bbd{l}", [P, 2, DS * 16]) for l in LANES]
        cbd = [sb(f"cbd{l}", [P, NT]) for l in LANES]
        d0 = [sb(f"d0{l}", [P, DS, NCH]) for l in LANES]
        hs = [sb(f"hs{l}", [P, DS, NCH]) for l in LANES]
        hc = [sb(f"hc{l}", [P, NCH, DS]) for l in LANES]
        hcT = [sb(f"hcT{l}", [P, 4, D]) for l in LANES]
        c_v2, c_r2 = ([sb(f"{n}{l}", [P, 2]) for l in LANES] for n in ("c_v2", "c_r2"))
        new = lambda m: outer.enter_context(nc.semaphore(m))
        c_ln1, c_ln2 = (LayerNorm(n, 2, sb, new) for n in ("c_ln1", "c_ln2"))
        ctx.close()
        ctx = ExitStack()
        d_xn, d_y, d_o = (tok("d_" + n, 4) for n in ("xn", "y", "o"))
        d_xT = [sb(f"d_xT{l}", [P, 4 * P]) for l in LANES]
        gate = [[sb(f"gate{l}{c}", [P, 4 * P]) for c in range(2)] for l in LANES]
        h0 = [sb(f"h0{l}", [P, HID, 4 * P]) for l in LANES]
        h1 = [sb(f"h1{l}", [P, HID, 4 * P]) for l in LANES]
        d_ln1, d_ln2 = (LayerNorm(n, 4, sb, new) for n in ("d_ln1", "d_ln2"))
        ctx.close()
        ctx = outer

        SEMS = """a_xn a_xb a_t_ps a_xh a_xl b_xh b_xl a_qk_ps a_v_ps a_qT a_hbd a_vbd a_s_ps a_tau a_m_ps a_msgT a_y_ps
            a_y a_zn a_z a_o a_x a_stored b_xn b_xb b_t_ps b_qk_ps b_v_ps b_kT b_hbd b_vbd b_s_ps b_sm b_ex b_rden
            b_p b_pT b_m_ps b_msgT b_y_ps b_zn b_h b_ht_ps b_hT b_l_ps b_lg b_le b_hot b_hott_ps b_hotT b_on
            b_z b_o b_x b_stored c_r2 c_xn_ c_t_ps c_xT_ c_in_ps c_xpad c_zs_ c_cv_ c_xs_ c_dt_ps c_b_ps c_c_ps c_zb_
            c_sp_ c_dt_ c_dec c_decm c_bcT c_prod c_g1_ps c_term c_cbd c_bbd c_wall c_wend c_wt_ps c_wendT c_st_ps
            c_d0 c_hs c_hc c_hct_ps c_hcT c_yi_ps c_y c_out_ps c_o_ c_x d_xn_ d_t_ps d_xT_ d_y_ps d_o_ d_x d_stored""".split()
        S = {n: sem(n) for n in SEMS}
        he_ps, he_ready, e_done = (sem(n) for n in ("he_ps", "he_ready", "e_done"))
        b_sum_read, split_done = sem("b_sum_read"), sem("split_done")
        LATE, HE, ACC = 4, 5, 7
        m_gu_ps, m_gate, m_h0, m_h1_ps, m_h1, m_h2_ps, m_h2 = (
            [sem(f"{n}{l}") for l in LANES] for n in ("m_gu_ps", "m_gate", "m_h0", "m_h1_ps", "m_h1", "m_h2_ps", "m_h2"))

        x_in = a["x"].rearrange("b (h p) d -> (b h) p d", p=P)
        out_t = out.rearrange("b (h p) d -> (b h) p d", p=P)
        x1 = nc.dram_tensor("x1", (NB, NT, D), F32, kind="Internal").ap()
        x2 = nc.dram_tensor("x2", (NB, NT, D), F32, kind="Internal").ap()
        by_seq = lambda t: t.rearrange("b (h p) d -> (b h) p d", p=P)
        by_step = lambda t: t.rearrange("b (k s) d -> k s b d", s=8)

        def xblk(t, i, c):
            return t[:, bass.ds(i + c, 1), :].rearrange("p o d -> p (o d)")

        def heads(g):
            return slice(BLK * g, BLK * g + BLK)

        def bank(l, b, lo=0, hi=512):
            return ps[:, 4 * l + b, lo:hi]

        block = ctx.enter_context(nc.Block())

        @block.sync
        def _(sp):
            def load(per, first, issue):
                for l in LANES:
                    issue(0, l)
                with sp.Fori(1, ITER) as i:
                    for l in LANES:
                        sp.wait_ge(x_loaded[l], i * (16 * per) + first)
                        issue(i, l)

            def load_seq(src):
                def issue(i, l):
                    sp.dma_start(x[:, bass.ds(i * 4 + 2 * l, 2), :],
                                 by_seq(src)[bass.ds(i * 4 + 2 * l, 2)].rearrange("b p d -> p b d")
                                 ).then_inc(x_loaded[l], 16)
                return issue

            def load_step(src):
                def issue(i, l):
                    for b in range(2):
                        sp.dma_start(xblk(xB, i * 4, 2 * l + b),
                                     by_step(src)[bass.ds(i * 4 + 2 * l + b, 1)].rearrange("o s b d -> (o s) b d")
                                     ).then_inc(x_loaded[l], 16)
                return issue

            load(1, 0, load_seq(a["x"]))
            dst = out if stage == 1 else x1
            with sp.Fori(0, ITER) as i:
                for l in LANES:
                    sp.wait_ge(S["a_x"], i * 2 + l + 1)
                    sp.dma_start(by_seq(dst)[bass.ds(i * 4 + 2 * l, 2)].rearrange("b p d -> p b d"),
                                 x[:, bass.ds(i * 4 + 2 * l, 2), :]).then_inc(S["a_stored"], 16)
            sp.wait_ge(S["a_stored"], 16 * NB)
            if stage < 4:
                for k in "abcd":
                    sp.wait_ge(w_loaded[k], W_ALL[k])
            if stage == 1:
                return
            load(2, 16 * ITER, load_step(x1))
            dst = out if stage == 2 else x2
            with sp.Fori(0, ITER) as i:
                for l in LANES:
                    sp.wait_ge(S["b_x"], i * 2 + l + 1)
                    for b in range(2):
                        sp.dma_start(by_step(dst)[bass.ds(i * 4 + 2 * l + b, 1)].rearrange("o s b d -> (o s) b d"),
                                     xB[:, bass.ds(i * 4 + 2 * l + b, 1), :].rearrange("p o d -> p (o d)")
                                     ).then_inc(S["b_stored"], 16)
            sp.wait_ge(S["b_stored"], 32 * NB)
            if stage == 2:
                return
            load(1, 48 * ITER, load_seq(x2))
            if stage == 3:
                sp.wait_ge(S["c_x"], NB)
                sp.dma_start(by_seq(out).rearrange("b p d -> p b d"), x[:, :, :]).then_inc(S["d_stored"], 16)
                sp.wait_ge(S["d_stored"], 16)
                return
            with sp.Fori(0, ITER_MLP) as i:
                for l in LANES:
                    sp.wait_ge(S["d_x"], i * 2 + l + 1)
                    sp.dma_start(out_t[bass.ds(i * 8 + 4 * l, 4)].rearrange("b p d -> p b d"),
                                 x[:, bass.ds(i * 8 + 4 * l, 4), :]).then_inc(S["d_stored"], 16)
            sp.wait_ge(S["d_stored"], 16 * 2 * ITER_MLP)

        @block.gpsimd
        def _(pool):
            chain = Chain(pool, pool_chain)
            pool.memset(eps[:, :], EPS).then_inc(fill_done, 1)
            pool.memset(half[:, :], -0.5).then_inc(fill_done, 1)
            pool.memset(ones[:, :], 1.0).then_inc(fill_done, 1)
            pool.wait_ge(fill_done, 3)
            pool.wait_ge(w_loaded["a"], W_ALL["a"])

            def scale_shift(l, n, ready, src, tmp, dst, g, b, done):
                pool.wait_ge(ready, n)
                chain.link(pool.tensor_tensor(tmp[l][:, :, :], src[l][:, :, :], rows[:, g, :, :], ALU.mult))
                pool.tensor_tensor(dst[l][:, :, :], tmp[l][:, :, :], rows[:, b, :, :], ALU.add).then_inc(done, 1)

            def copy(dst, src, one):
                return pool.tensor_tensor(dst, src, one, ALU.mult)

            def step_a(n, l, have):
                chain.clear()
                if have(-1):
                    a_ln2.rstd(pool, chain, eps, half, 1 - l, n)
                if have(2):
                    a_ln1.rstd(pool, chain, eps, half, l, n + 3)
                if have(1):
                    pool.wait_ge(S["a_xn"], n + 2)
                    if have(-1):
                        pool.wait_ge(S["a_y"], n)
                    copy(t_xb[1 - l][:, :, :], t_xn[1 - l][:, :, :], ones[:, :].unsqueeze(1).to_broadcast([P, 2, D])
                         ).then_inc(S["a_xb"], 1)
                if have(-1):
                    scale_shift(1 - l, n, S["a_zn"], t_zn, t_zg, t_z, 0, 1, S["a_z"])
                    a_ln3.rstd(pool, chain, eps, half, 1 - l, n)
                    pool.wait_ge(S["a_o"], n)
                    xt = x[:, bass.ds(n * 2 - 2, 2), :]
                    pool.tensor_tensor(xt, xt, t_o[1 - l][:, :, :], ALU.add).then_inc(S["a_x"], 1)

            pipelined(pool, step_a, 2, 1, NB)
            if stage == 1:
                return

            def step_b(n, l, have):
                chain.clear()
                o = 1 - l
                if have(-1):
                    b_ln2.rstd(pool, chain, eps, half, o, n)
                    scale_shift(o, n, S["b_on"], t_on, t_og, t_z, 5, 6, S["b_z"])
                if have(1):
                    b_ln1.rstd(pool, chain, eps, half, o, n + 2)
                    scale_shift(o, n + 2, S["b_zn"], t_zn, t_zg, t_h, 3, 4, S["b_h"])
                if have(4):
                    b_ln0.rstd(pool, chain, eps, half, l, n + 5)
                if have(3):
                    pool.wait_ge(S["b_xn"], n + 4)
                    pool.tensor_tensor(t_xb[o][:, :, :], t_xn[o][:, :, :], rows[:, 2, :, :], ALU.add).then_inc(S["b_xb"], 1)
                if have(-1):
                    b_ln3.rstd(pool, chain, eps, half, o, n)
                    pool.wait_ge(S["b_o"], n)
                    xt = xB[:, bass.ds(n * 2 - 2, 2), :]
                    pool.tensor_tensor(xt, xt, t_o[o][:, :, :], ALU.add).then_inc(S["b_x"], 1)
                if have(2):
                    pool.wait_ge(S["b_rden"], n + 3)
                    pool.tensor_tensor(sm[l][:, :, :], ex[l][:, :, :],
                                       rden[l][:, :].unsqueeze(2).to_broadcast([P, G * NBLK, BLK]),
                                       ALU.mult).then_inc(S["b_p"], 1)

            pool.wait_ge(S["a_x"], NB)
            pipelined(pool, step_b, 4, 1, NB)
            if stage == 2:
                return
            pool.wait_ge(S["b_stored"], 32 * NB)
            for l in LANES:
                pool.memset(xpad[l][:, 0:3], 0.0)
                pool.memset(d0[l][:, :, 0:1], 0.0)
                pool.memset(hc[l][:, 0:1, :], 0.0).then_inc(zero_ready, 1)
            with pool.Fori(0, ITER) as i:
                chain.clear()
                for l in LANES:
                    n = i * 2 + l + 1
                    c_ln1.rstd(pool, chain, eps, half, l, n)
                    pool.wait_ge(c_ln1.rstd_ready, n)
                    chain.link(pool.tensor_tensor(c_v2[l][:, :], c_ln1.mv[l][:, :, 1], c_ln1.rs[l][:, :], ALU.mult))
                    chain.link(pool.tensor_tensor(c_v2[l][:, :], c_v2[l][:, :], c_ln1.rs[l][:, :], ALU.mult))
                    chain.link(pool.tensor_tensor(c_v2[l][:, :], c_v2[l][:, :], eps[:, 0:2], ALU.add))
                    chain.link(pool.tensor_tensor(c_v2[l][:, :], c_v2[l][:, :], half[:, 0:2], ALU.pow))
                    pool.tensor_tensor(c_r2[l][:, :], c_v2[l][:, :], c_ln1.rs[l][:, :], ALU.mult).then_inc(S["c_r2"], 1)
                for l in LANES:
                    n = i * 2 + l + 1
                    pool.wait_ge(S["c_bcT"], n)
                    for j in range(CH):
                        last = pool.tensor_tensor(
                            prod[l][:, OFF[j]:OFF[j + 1]].rearrange("p (c t) -> p c t", t=CH - j),
                            bcT[l][:, 1, :, j:CH], bcT[l][:, 0, :, 0:CH - j], ALU.mult)
                    last.then_inc(S["c_prod"], 1)
                for l in LANES:
                    n = i * 2 + l + 1
                    pool.wait_ge(S["c_decm"], n)
                    copy(d0[l][:, :, 1:NCH], dec[l][:, 1, 1:NCH, CH - 1].unsqueeze(1).to_broadcast([P, DS, NCH - 1]),
                         ones[:, 0:1].unsqueeze(2).to_broadcast([P, DS, NCH - 1])).then_inc(S["c_d0"], 1)
                    pool.wait_ge(S["c_wall"], n)
                    for j in range(CH):
                        w = wall[l][:, OFF[j]:OFF[j + 1]].rearrange("p (c t) -> p c t", t=CH - j)
                        last = copy(wend[l][:, :, CH - 1 - j], w[:, :, CH - 1 - j], ones[:, 0:NCH])
                    last.then_inc(S["c_wend"], 1)
                for l in LANES:
                    c_ln2.rstd(pool, chain, eps, half, l, i * 2 + l + 1)
                for l in LANES:
                    pool.wait_ge(S["c_o_"], i * 2 + l + 1)
                    xt = x[:, bass.ds(i * 4 + 2 * l, 2), :]
                    pool.tensor_tensor(xt, xt, c_o[l][:, :, :], ALU.add).then_inc(S["c_x"], 1)
            if stage == 3:
                return
            with pool.Fori(0, ITER_MLP) as i:
                chain.clear()
                for l in LANES:
                    d_ln1.rstd(pool, chain, eps, half, l, i * 2 + l + 1)
                for l in LANES:
                    d_ln2.rstd(pool, chain, eps, half, l, i * 2 + l + 1)
                for l in LANES:
                    pool.wait_ge(S["d_o_"], i * 2 + l + 1)
                    xt = x[:, bass.ds(i * 8 + 4 * l, 4), :]
                    pool.tensor_tensor(xt, xt, d_o[l][:, :, :], ALU.add).then_inc(S["d_x"], 1)

        @block.scalar
        def _(act):
            chain = Chain(act, act_chain)
            for t, name in zip(stage_f, ("c_rep", "c_band", "c_same", "c_negsel")):
                dst = t[:, :, :] if name == "c_negsel" else t[:, :]
                act.dma_start(dst, a[name]).then_inc(w_loaded["a"], 16)
            for part in "abcd":
                for dst, name in loads[part]:
                    act.dma_start(dst, a[name]).then_inc(w_loaded[part], 16)

            def transposed(l, b, n, t_ps, done):
                act.wait_ge(t_ps, n)
                act.activation(xh[l][:, :], ps[:, b, 0:NT], ACT.Copy).then_inc(done, 1)

            def step_a(n, l, have):
                if have(1):
                    act.wait_ge(S["a_qk_ps"], n + 2)
                    act.activation(qk[1 - l][:, :, :], ps[:, 4 * (1 - l):4 * (1 - l) + 2, 0:NT], ACT.Copy
                                   ).then_inc(S["a_qT"], 1)
                if have(0):
                    act.wait_ge(S["a_s_ps"], n + 1)
                    act.activation(tau[l][:, :, :], ps[:, 4 * l:4 * l + 4, 0:NBLK * SPAN], ACT.Sigmoid,
                                   scale=ATT_SCALE).then_inc(S["a_tau"], 1)
                if have(2):
                    transposed(l, 4 * (1 - l) + 3, n + 3, S["a_t_ps"], S["a_xh"])
                if have(0):
                    act.wait_ge(S["a_m_ps"], n + 1)
                    act.activation(msgT[l][:, :], bank(l, 0, 0, NT), ACT.Copy).then_inc(S["a_msgT"], 1)

            pipelined(act, step_a, 2, 1, NB)
            if stage == 1:
                return

            def gelu(n, l, e):
                act.wait_ge(he_ps, n * NE + (e + 1))
                if e >= 2:
                    act.wait_ge(e_done, n * NE + (e - 1))
                act.activation(he[e % 2][:, :], ps[:, HE + e % 2, 0:NT], ACT.Gelu,
                               bias=vec("b1", e)).then_inc(he_ready, 1)

            def step_b(n, l, have):
                if have(0):
                    act.wait_ge(S["b_hott_ps"], n + 1)
                    act.activation(hotT[l][:, :], ps[0:NE, LATE, 0:NT], ACT.Copy)
                    act.activation(hotTb[l][:, :], ps[0:NE, LATE, 0:NT], ACT.Copy).then_inc(S["b_hotT"], 1)
                if have(1):
                    act.wait_ge(S["b_m_ps"], n + 2)
                    act.activation(msgT[1 - l][:, :], ps[:, LATE, 0:NT], ACT.Identity, bias=vec("bv")
                                   ).then_inc(S["b_msgT"], 1)
                if have(3):
                    transposed(1 - l, 3, n + 4, S["b_t_ps"], S["b_xh"])
                if have(3):
                    act.wait_ge(S["b_qk_ps"], n + 4)
                    act.activation(qk[1 - l][:, 0, :], ps[:, 0, 0:NT], ACT.Identity, bias=vec("bq"))
                    act.activation(qk[1 - l][:, 1, :], ps[:, 1, 0:NT], ACT.Identity, bias=vec("bk")
                                   ).then_inc(S["b_kT"], 1)
                if have(0):
                    for e in range(0, 4):
                        gelu(n, l, e)
                if have(1):
                    act.wait_ge(S["b_ht_ps"], n + 2)
                    act.activation(hT[1 - l][:, :], ps[:, LATE, 0:NT], ACT.Copy).then_inc(S["b_hT"], 1)
                if have(0):
                    for e in range(4, NE):
                        gelu(n, l, e)
                if have(2):
                    act.wait_ge(S["b_sm"], n + 3)
                    act.activation(ex[l][:, :, :], sm[l][:, :, :], ACT.Exp, scale=ATT_SCALE).then_inc(S["b_ex"], 1)
                if have(1):
                    act.wait_ge(S["b_lg"], n + 2)
                    act.activation(le[1 - l][:, :, :], lg[1 - l][:, :, :], ACT.Exp).then_inc(S["b_le"], 1)

            act.wait_ge(w_loaded["a"], W_ALL["a"])
            act.wait_ge(w_loaded["b"], W_ALL["b"])
            act.wait_ge(S["a_x"], NB)
            pipelined(act, step_b, 4, 1, NB)
            if stage == 2:
                return
            act.wait_ge(S["b_stored"], 32 * NB)
            act.wait_ge(w_loaded["c"], W_ALL["c"])
            act.wait_ge(zero_ready, 2)
            act.activation(expA[:, :], vec("log_A"), ACT.Exp).then_inc(expA_ready, 1)
            act.wait_ge(negA_ready, 1)
            with act.Fori(0, ITER) as i:
                chain.clear()
                for l in LANES:
                    act.wait_ge(S["c_t_ps"], i * 2 + l + 1)
                    act.activation(c_xT[l][:, :], bank(l, 0, 0, NT), ACT.Identity, bias=vec("ln_b"),
                                   scale=vec("ln_g")).then_inc(S["c_xT_"], 1)
                for l in LANES:
                    act.wait_ge(S["c_in_ps"], i * 2 + l + 1)
                    act.activation(xpad[l][:, 3:3 + NT], bank(l, 1, 0, NT), ACT.Copy).then_inc(S["c_xpad"], 1)
                    act.activation(zs[l][:, :], bank(l, 2, 0, NT), ACT.Silu).then_inc(S["c_zs_"], 1)
                for l in LANES:
                    act.wait_ge(S["c_cv_"], i * 2 + l + 1)
                    act.activation(xs[l][:, :], cv[l][:, :], ACT.Silu).then_inc(S["c_xs_"], 1)
                for l in LANES:
                    act.wait_ge(S["c_b_ps"], i * 2 + l + 1)
                    act.activation(bcT[l][:, :, :, :].rearrange("p a c t -> p (a c t)"), ps[0:DS, 4 * l + 3, :],
                                   ACT.Copy).then_inc(S["c_bcT"], 1)
                for l in LANES:
                    act.wait_ge(S["c_zb_"], i * 2 + l + 1)
                    chain.link(act.activation(sp_[l][:, :], zb[l][:, :], ACT.Abs))
                    chain.link(act.activation(sp_[l][:, :], sp_[l][:, :], ACT.Exp, scale=-1.0))
                    act.activation(sp_[l][:, :], sp_[l][:, :], ACT.Ln, bias=1.0).then_inc(S["c_sp_"], 1)
                for l in LANES:
                    act.wait_ge(S["c_dt_"], i * 2 + l + 1)
                    act.activation(dec[l][:, 0, :, :].rearrange("p c t -> p (c t)"), dt[l][:, :], ACT.Exp, scale=negA[:, :])
                    act.activation(dec[l][:, 1, :, :].rearrange("p c t -> p (c t)"), cdt[l][:, :], ACT.Exp,
                                   scale=negA[:, :]).then_inc(S["c_dec"], 1)
                for l in LANES:
                    act.wait_ge(S["c_wt_ps"], i * 2 + l + 1)
                    act.activation(flat3(wendT[l][:, :, :]), bank(l, 0, 0, NT), ACT.Copy).then_inc(S["c_wendT"], 1)
                for l in LANES:
                    act.wait_ge(S["c_hs"], i * 2 + l + 1)
                    act.activation(hc[l][:, 1:NCH, :], hs[l][:, :, 0:NCH - 1].rearrange("p n c -> p c n"),
                                   ACT.Copy).then_inc(S["c_hc"], 1)
                for l in LANES:
                    act.wait_ge(S["c_hct_ps"], i * 2 + l + 1)
                    act.activation(flat3(hcT[l][:, :, :]), bank(l, 1), ACT.Copy).then_inc(S["c_hcT"], 1)
            if stage == 3:
                return
            act.wait_ge(w_loaded["d"], W_ALL["d"])
            with act.Fori(0, ITER_MLP) as i:
                for l in LANES:
                    act.wait_ge(S["d_t_ps"], i * 2 + l + 1)
                    act.activation(d_xT[l][:, :], bank(l, 0), ACT.Copy).then_inc(S["d_xT_"], 1)
                for l in LANES:
                    for m in range(HID):
                        act.wait_ge(m_gu_ps[l], i * HID + m + 1)
                        if m >= 2:
                            act.wait_ge(m_h0[l], i * HID + m - 1)
                        act.activation(gate[l][m % 2][:, :], bank(l, 2 * (m % 2)), ACT.Silu,
                                       scale=vec("w1_s", m)).then_inc(m_gate[l], 1)
                for l in LANES:
                    for m in range(HID):
                        act.wait_ge(m_h1_ps[l], i * HID + m + 1)
                        act.activation(h1[l][:, m, :], bank(l, m), ACT.Gelu, scale=vec("h1_s", m)).then_inc(m_h1[l], 1)
                for l in LANES:
                    for m in range(HID):
                        act.wait_ge(m_h2_ps[l], i * HID + m + 1)
                        act.activation(h0[l][:, m, :], bank(l, m), ACT.Gelu, scale=vec("h2_s", m)).then_inc(m_h2[l], 1)

        @block.vector
        def _(dve):
            chain = Chain(dve, dve_chain)
            dve.wait_ge(w_loaded["a"], W_ALL["a"])
            for dst, src in zip((rep[:, :], band[:, :], same[:, :], negsel[:, :, :]),
                                (stage_f[0][:, :], stage_f[1][:, :], stage_f[2][:, :], stage_f[3][:, :, :])):
                dve.tensor_copy(dst, src).then_inc(cast_ready, 1)

            def split(dst_h, dst_l, src, done, before):
                dve.tensor_copy(dst_h, src).then_inc(done, 1)
                dve.wait_ge(done, before + 1)
                dve.tensor_tensor(dst_l, src, dst_h.bitcast(F32), ALU.subtract).then_inc(done, 1)

            def low_part(l, b, n, high, done):
                dve.wait_ge(high, n)
                dve.tensor_tensor(xl[l][:, :], ps[:, b, 0:NT], xh[l][:, :].bitcast(F32), ALU.subtract).then_inc(done, 1)

            def four_heads(l, which, done):
                f, r, p = qk[l][:, :, :], rest[l][:, :, :], parts[l]
                chain.link(dve.tensor_copy(p[:, 0, :, :], f))
                chain.link(dve.tensor_tensor(r, f, p[:, 0, :, :], ALU.subtract))
                chain.link(dve.tensor_copy(p[:, 1, :, :], r))
                chain.link(dve.tensor_tensor(p[:, 2, :, :], r, p[:, 1, :, :], ALU.subtract))
                src = p[:, :, which, :].rearrange("p k (j s) -> p k j s", s=BLK)
                for h in range(4):
                    last = dve.tensor_scalar(hbd[l][:, :, :, h, :], src, headmask[:, h:h + 1], None, ALU.mult)
                last.then_inc(done, 1)

            def values(l, b, done):
                chain.link(dve.transpose(vT[l][:, :], ps[:, b + 2, 0:NT]))
                dve.tensor_tensor(flat3(vbd[l][:, :, :]).rearrange("p (k h c) -> p k h c", h=4, c=HD),
                                  vT[l][:, :].rearrange("p (k c) -> p k c", c=HD).unsqueeze(2).to_broadcast([P, 4 * NBLK, 4, HD]),
                                  vmask[:, :].rearrange("p (h c) -> p h c", c=HD).unsqueeze(1).to_broadcast([P, 4 * NBLK, 4, HD]),
                                  ALU.mult).then_inc(done, 1)

            def blocks(t):
                return t.rearrange("p (b d) -> p b d", d=D)

            def step_a(n, l, have):
                chain.clear()
                o = 1 - l
                if have(-1):
                    dve.wait_ge(S["a_y_ps"], n)
                    dve.wait_ge(S["a_xb"], n)
                    dve.tensor_tensor(t_y[o][:, :, :], blocks(bank(o, 3, 0, NT)), t_xb[o][:, :, :], ALU.add
                                      ).then_inc(S["a_y"], 1)
                    dve.wait_ge(S["a_y"], n)
                    a_ln2.stats(dve, chain, lambda b: t_y[o][:, b, :], o)
                if have(2):
                    if isinstance(n, int):
                        dve.wait_ge(x_loaded[l], 16 * ((n + 2) // 2 + 1))
                    else:
                        dve.wait_ge(x_loaded[l], n * 8 + (32 - 8 * l))
                    a_ln1.stats(dve, chain, lambda b: xblk(x, n * 2, 4 + b), l)
                    if have(0):
                        dve.wait_ge(S["a_xb"], n + 1)
                    a_ln1.apply(dve, lambda b: t_xn[l][:, b, :], lambda b: xblk(x, n * 2, 4 + b), l,
                                n + 3).then_inc(S["a_xn"], 1)
                if have(-1):
                    a_ln2.apply(dve, lambda b: t_zn[o][:, b, :], lambda b: t_y[o][:, b, :], o, n).then_inc(S["a_zn"], 1)
                if have(1):
                    dve.wait_ge(S["a_qT"], n + 2)
                    four_heads(o, 1, S["a_hbd"])
                    dve.wait_ge(S["a_v_ps"], n + 2)
                    values(o, 4 * o, S["a_vbd"])
                if have(-1):
                    dve.wait_ge(S["a_z"], n)
                    a_ln3.stats(dve, chain, lambda b: t_z[o][:, b, :], o)
                    a_ln3.apply(dve, lambda b: t_o[o][:, b, :], lambda b: t_z[o][:, b, :], o, n).then_inc(S["a_o"], 1)
                if have(2):
                    low_part(l, 4 * o + 3, n + 3, S["a_xh"], S["a_xl"])

            split(wa_h[:, :, :], wa_l[:, :, :], wa[:, 0:3, :], split_done, 0)
            dve.wait_ge(w_loaded["b"], W_ALL["b"])
            split(wf_h[:, :, :], wf_l[:, :, :], wf[:, 0:3, :], split_done, 2)
            pipelined(dve, step_a, 2, 1, NB)
            if stage == 1:
                return

            def step_b(n, l, have):
                chain.clear()
                o = 1 - l
                if have(2):
                    dve.wait_ge(S["b_s_ps"], n + 3)
                    sc = ps[:, 0:4, 0:NT].rearrange("p g (j s) -> p g j s", s=BLK)
                    m4 = mx[l][:, :].rearrange("p (g j) -> p g j", j=NBLK)
                    chain.link(dve.tensor_reduce(m4, sc, AX.X, ALU.max))
                    dve.tensor_tensor(sm[l][:, :, :].rearrange("p (g j) s -> p g j s", j=NBLK), sc,
                                      m4.unsqueeze(3).to_broadcast([P, G, NBLK, BLK]), ALU.subtract).then_inc(S["b_sm"], 1)
                if have(-1):
                    dve.wait_ge(e_done, n * NE)
                    chain.link(dve.tensor_tensor(t_yo[o][:, :, :], blocks(ps[:, ACC, 0:NT]), t_h[o][:, :, :], ALU.add))
                    dve.sem_inc(b_sum_read, 1)
                    b_ln2.stats(dve, chain, lambda b: t_yo[o][:, b, :], o)
                if have(3):
                    low_part(o, 3, n + 4, S["b_xh"], S["b_xl"])
                if have(-1):
                    b_ln2.apply(dve, lambda b: t_on[o][:, b, :], lambda b: t_yo[o][:, b, :], o, n).then_inc(S["b_on"], 1)
                if have(1):
                    dve.wait_ge(S["b_y_ps"], n + 2)
                    chain.link(dve.tensor_tensor(t_y[o][:, :, :], blocks(ps[:, LATE, 0:NT]), t_xb[o][:, :, :], ALU.add))
                    b_ln1.stats(dve, chain, lambda b: t_y[o][:, b, :], o)
                if have(3):
                    dve.wait_ge(S["b_kT"], n + 4)
                    four_heads(o, 0, S["b_hbd"])
                if have(1):
                    b_ln1.apply(dve, lambda b: t_zn[o][:, b, :], lambda b: t_y[o][:, b, :], o, n + 2).then_inc(S["b_zn"], 1)
                if have(3):
                    dve.wait_ge(S["b_v_ps"], n + 4)
                    values(o, 0, S["b_vbd"])
                if have(4):
                    if isinstance(n, int):
                        dve.wait_ge(x_loaded[l], 16 * ITER + 32 * ((n + 4) // 2 + 1))
                    else:
                        dve.wait_ge(x_loaded[l], n * 16 + (16 * ITER + 96 - 16 * l))
                    b_ln0.stats(dve, chain, lambda b: xblk(xB, n * 2, 8 + b), l)
                if have(-1):
                    dve.wait_ge(S["b_z"], n)
                    b_ln3.stats(dve, chain, lambda b: t_z[o][:, b, :], o)
                if have(4):
                    if have(2):
                        dve.wait_ge(S["b_xb"], n + 3)
                    b_ln0.apply(dve, lambda b: t_xn[l][:, b, :], lambda b: xblk(xB, n * 2, 8 + b), l,
                                n + 5).then_inc(S["b_xn"], 1)
                if have(-1):
                    b_ln3.apply(dve, lambda b: t_o[o][:, b, :], lambda b: t_z[o][:, b, :], o, n).then_inc(S["b_o"], 1)
                if have(1):
                    dve.wait_ge(S["b_l_ps"], n + 2)
                    chain.link(dve.tensor_tensor(lg[o][:, :, :], ps[:, LATE, 0:2 * NE].rearrange("p (b e) -> p b e", e=NE),
                                                 router_b[:, :, :], ALU.add))
                    chain.link(dve.tensor_reduce(lmx[o][:, :], lg[o][:, :, :], AX.X, ALU.max))
                    dve.tensor_tensor(lg[o][:, :, :], lg[o][:, :, :], lmx[o][:, :].unsqueeze(2).to_broadcast([P, 2, NE]),
                                      ALU.subtract).then_inc(S["b_lg"], 1)
                if have(2):
                    dve.wait_ge(S["b_ex"], n + 3)
                    chain.link(dve.tensor_reduce(den[l][:, :], ex[l][:, :, :], AX.X, ALU.add))
                    dve.reciprocal(rden[l][:, :], den[l][:, :]).then_inc(S["b_rden"], 1)
                if have(1):
                    dve.wait_ge(S["b_le"], n + 2)
                    dve.tensor_copy(lg[o][:, :, :], le[o][:, :, :])
                    for b in range(2):
                        last = dve.max(m8[o][:, b, :], le[o][:, b, :])
                    chain.link(last)
                    for b in range(2):
                        last = dve.max_index(ix[o][:, b, :], m8[o][:, b, :], le[o][:, b, :])
                    chain.link(last)
                    chain.link(dve.tensor_tensor(pick[o][:, :], ix[o][:, :, 0], ix[o][:, :, 1], ALU.max))
                    for b in range(2):
                        last = dve.tensor_scalar(hot[o][:, b, :], iota[:, :], pick[o][:, b:b + 1], None, ALU.is_equal)
                    last.then_inc(S["b_hot"], 1)
                if have(2):
                    dve.wait_ge(S["b_p"], n + 3)
                    dve.transpose(flat3(pT[l][:, :, :]), flat3(sm[l][:, :, :])).then_inc(S["b_pT"], 1)

            dve.wait_ge(S["a_x"], NB)
            pipelined(dve, step_b, 4, 1, NB)
            if stage == 2:
                return
            dve.wait_ge(S["b_stored"], 32 * NB)
            dve.wait_ge(w_loaded["c"], W_ALL["c"])
            dve.wait_ge(zero_ready, 2)
            dve.wait_ge(expA_ready, 1)
            dve.tensor_scalar(negA[:, :], expA[:, :], -1.0, None, ALU.mult).then_inc(negA_ready, 1)
            with dve.Fori(0, ITER) as i:
                chain.clear()
                for l in LANES:
                    dve.wait_ge(x_loaded[l], i * 16 + (48 * ITER + 16))
                    c_ln1.stats(dve, chain, lambda b: xblk(x, i * 4, 2 * l + b), l)
                for l in LANES:
                    n = i * 2 + l + 1
                    c_ln1.apply(dve, lambda b: c_xn[l][:, b, :], lambda b: xblk(x, i * 4, 2 * l + b), l, n)
                    dve.wait_ge(S["c_r2"], n)
                    c_ln1.apply(dve, lambda b: c_xq[l][:, b, :], lambda b: xblk(x, i * 4, 2 * l + b), l, n,
                                scale=c_r2).then_inc(S["c_xn_"], 1)
                for l in LANES:
                    dve.wait_ge(S["c_xpad"], i * 2 + l + 1)
                    chain.link(dve.tensor_scalar(cv[l][:, :], xpad[l][:, 3:3 + NT], vec("conv_w", 3), vec("conv_b"),
                                                 ALU.mult, ALU.add))
                    for k in (2, 1, 0):
                        ins = dve.scalar_tensor_tensor(out=cv[l][:, :], in0=xpad[l][:, k:k + NT], scalar=vec("conv_w", k),
                                                       in1=cv[l][:, :], op0=ALU.mult, op1=ALU.add)
                        if k:
                            chain.link(ins)
                    ins.then_inc(S["c_cv_"], 1)
                for l in LANES:
                    dve.wait_ge(S["c_dt_ps"], i * 2 + l + 1)
                    dve.tensor_scalar(zb[l][:, :], bank(l, 1, 0, NT), vec("dt_b"), None, ALU.add).then_inc(S["c_zb_"], 1)
                for l in LANES:
                    dve.wait_ge(S["c_c_ps"], i * 2 + l + 1)
                    dve.tensor_tensor(flat3(bbd[l][:, :, :]), bank(l, 0), bmask[:, :, :, :].rearrange("p k n c -> p (k n c)"),
                                      ALU.mult).then_inc(S["c_bbd"], 1)
                    dve.tensor_tensor(cbd[l][:, :], bank(l, 2, 0, NT), cmask[:, :], ALU.mult).then_inc(S["c_cbd"], 1)
                for l in LANES:
                    dve.wait_ge(S["c_sp_"], i * 2 + l + 1)
                    chain.link(dve.scalar_tensor_tensor(out=dt[l][:, :], in0=zb[l][:, :], scalar=0.0, in1=sp_[l][:, :],
                                                        op0=ALU.max, op1=ALU.add))
                    dve.tensor_tensor_scan(cdt[l][:, :], first[:, :], dt[l][:, :], 0.0, ALU.mult, ALU.add
                                           ).then_inc(S["c_dt_"], 1)
                    dve.tensor_tensor(wall[l][:, 0:NT], dt[l][:, :], xs[l][:, :], ALU.mult)
                for l in LANES:
                    dve.wait_ge(S["c_dec"], i * 2 + l + 1)
                    chain.link(dve.tensor_scalar(dec[l][:, :, :, :].rearrange("p a c t -> p (a c t)"),
                                                 dec[l][:, :, :, :].rearrange("p a c t -> p (a c t)"), 1.0, None, ALU.min))
                    dve.sem_inc(S["c_decm"], 1)
                    for j in range(1, CH):
                        w0 = wall[l][:, OFF[j - 1]:OFF[j]].rearrange("p (c t) -> p c t", t=CH - j + 1)
                        w1 = wall[l][:, OFF[j]:OFF[j + 1]].rearrange("p (c t) -> p c t", t=CH - j)
                        ins = dve.tensor_tensor(w1, dec[l][:, 0, :, j:CH], w0[:, :, 0:CH - j], ALU.mult)
                        if j < CH - 1:
                            chain.link(ins)
                    ins.then_inc(S["c_wall"], 1)
                for l in LANES:
                    n = i * 2 + l + 1
                    dve.wait_ge(S["c_wall"], n)
                    dve.wait_ge(S["c_g1_ps"], n)
                    for b, (j0, j1) in zip((3, 1, 2), PAIR_BANKS):
                        ins = dve.tensor_tensor(term[l][:, OFF[j0]:OFF[j1]], wall[l][:, OFF[j0]:OFF[j1]],
                                                bank(l, b, 0, OFF[j1] - OFF[j0]), ALU.mult)
                    ins.then_inc(S["c_term"], 1)
                    dve.wait_ge(S["c_term"], n)
                    y = term[l][:, 0:NT].rearrange("p (c t) -> p c t", t=CH)
                    for j in range(1, CH):
                        chain.link(dve.tensor_tensor(y[:, :, j:CH], y[:, :, j:CH],
                                                     term[l][:, OFF[j]:OFF[j + 1]].rearrange("p (c t) -> p c t", t=CH - j),
                                                     ALU.add))
                for l in LANES:
                    n = i * 2 + l + 1
                    dve.wait_ge(S["c_d0"], n)
                    dve.wait_ge(S["c_st_ps"], n)
                    dve.tensor_tensor_scan(flat3(hs[l][:, :, :]), flat3(d0[l][:, :, :]), bank(l, 0), 0.0,
                                           ALU.mult, ALU.add).then_inc(S["c_hs"], 1)
                for l in LANES:
                    n = i * 2 + l + 1
                    dve.wait_ge(S["c_yi_ps"], n)
                    chain.link(dve.tensor_tensor(yi[l][:, :], bank(l, 2, 0, NT),
                                                 dec[l][:, 1, :, :].rearrange("p c t -> p (c t)"), ALU.mult))
                    chain.link(dve.tensor_tensor(yi[l][:, :], yi[l][:, :], term[l][:, 0:NT], ALU.add))
                    chain.link(dve.scalar_tensor_tensor(out=yi[l][:, :], in0=xs[l][:, :], scalar=vec("D_param"),
                                                        in1=yi[l][:, :], op0=ALU.mult, op1=ALU.add))
                    dve.wait_ge(S["c_zs_"], n)
                    dve.tensor_tensor(ya[l][:, :], yi[l][:, :], zs[l][:, :], ALU.mult).then_inc(S["c_y"], 1)
                for l in LANES:
                    dve.wait_ge(S["c_out_ps"], i * 2 + l + 1)
                    chain.link(dve.tensor_tensor(c_r[l][:, :, :], blocks(bank(l, 3, 0, NT)), c_xn[l][:, :, :], ALU.add))
                    c_ln2.stats(dve, chain, lambda b: c_r[l][:, b, :], l)
                for l in LANES:
                    c_ln2.apply(dve, lambda b: c_o[l][:, b, :], lambda b: c_r[l][:, b, :], l,
                                i * 2 + l + 1).then_inc(S["c_o_"], 1)
            if stage == 3:
                return
            dve.wait_ge(w_loaded["d"], W_ALL["d"])
            dve.wait_ge(S["c_x"], NB)
            with dve.Fori(0, ITER_MLP) as i:
                chain.clear()
                for l in LANES:
                    d_ln1.stats(dve, chain, lambda b: xblk(x, i * 8, 4 * l + b), l)
                for l in LANES:
                    d_ln1.apply(dve, lambda b: d_xn[l][:, b, :], lambda b: xblk(x, i * 8, 4 * l + b), l,
                                i * 2 + l + 1).then_inc(S["d_xn_"], 1)
                for l in LANES:
                    for m in range(HID):
                        dve.wait_ge(m_gate[l], i * HID + m + 1)
                        dve.scalar_tensor_tensor(out=h0[l][:, m, :], in0=bank(l, 2 * (m % 2) + 1), scalar=vec("w2_s", m),
                                                 in1=gate[l][m % 2][:, :], op0=ALU.mult, op1=ALU.mult).then_inc(m_h0[l], 1)
                for l in LANES:
                    dve.wait_ge(S["d_y_ps"], i * 2 + l + 1)
                    chain.link(dve.tensor_tensor(flat3(d_y[l][:, :, :]), bank(l, 0), flat3(w3_s[:, :, :]), ALU.mult))
                    d_ln2.stats(dve, chain, lambda b: d_y[l][:, b, :], l)
                for l in LANES:
                    d_ln2.apply(dve, lambda b: d_o[l][:, b, :], lambda b: d_y[l][:, b, :], l,
                                i * 2 + l + 1).then_inc(S["d_o_"], 1)

        @block.tensor
        def _(pe):
            pe.wait_ge(w_loaded["a"], W_ALL["a"])
            pe.wait_ge(cast_ready, 4)

            def turn(b, src, k, ready, n, done):
                pe.wait_ge(ready, n)
                for c in range(k):
                    last = pe.transpose(ps[:, b, P * c:P * c + P], src[:, c, :], ident[:, :])
                last.then_inc(done, 1)

            def product(dst, a_h, a_l, b_h, b_l, start):
                pe.matmul(dst, a_h, b_h, start=start, stop=True, skip_group_check=True)
                pe.matmul(dst, a_l, b_h, start=False, stop=True, skip_group_check=True)
                return pe.matmul(dst, a_h, b_l, start=False, stop=True, skip_group_check=True)

            def project(l, b, w_h, w_l, qk_ps, v_ps):
                for k, done in ((0, None), (1, qk_ps), (2, v_ps)):
                    last = product(ps[:, b + k, 0:NT], w_h[:, k, :], w_l[:, k, :], xh[l][:, :], xl[l][:, :], True)
                    if done is not None:
                        last.then_inc(done, 1)

            def score(l, dst, g, j, w, moving):
                for k, m in ((0, 0), (0, 1), (1, 0), (1, 1), (0, 2), (2, 0)):
                    last = pe.matmul(dst, hbd[l][heads(g), k, j, :, :].rearrange("p h s -> p (h s)"),
                                     parts[l][heads(g), m, moving, BLK * j:BLK * j + w], start=False, stop=True,
                                     skip_group_check=True)
                return last

            def out_tokens(b, src, w, done):
                for c in range(2):
                    last = pe.matmul(ps[:, b, P * c:P * c + P], src[:, P * c:P * c + P], w, start=True, stop=True)
                last.then_inc(done, 1)

            def step_a(n, l, have):
                o = 1 - l
                if have(1):
                    pe.wait_ge(S["a_xl"], n + 2)
                    project(o, 4 * o, wa_h, wa_l, S["a_qk_ps"], S["a_v_ps"])
                if have(0):
                    pe.wait_ge(S["a_qT"], n + 1)
                    pe.wait_ge(S["a_hbd"], n + 1)
                    pe.wait_ge(S["a_vbd"], n + 1)
                    for g in range(G):
                        pe.matmul(bank(l, g, 0, NBLK * SPAN), rep[heads(g), :], band[heads(g), :], start=True, stop=True)
                    for j in range(NBLK):
                        w = SPAN if j < NBLK - 1 else BLK
                        for g in range(G):
                            last = score(l, bank(l, g, SPAN * j, SPAN * j + w), g, j, w, 0)
                    last.then_inc(S["a_s_ps"], 1)
                if have(2):
                    if have(-1):
                        pe.wait_ge(S["a_y"], n)
                    turn(4 * o + 3, t_xn[l], 2, S["a_xn"], n + 3, S["a_t_ps"])
                if have(0):
                    pe.wait_ge(S["a_tau"], n + 1)
                    for j in range(NBLK):
                        w = SPAN if j < NBLK - 1 else BLK
                        for g in range(G):
                            last = pe.matmul(ps[heads(g), 4 * l, BLK * j:BLK * j + w], vbd[l][:, j, heads(g)],
                                             tau[l][:, g, SPAN * j:SPAN * j + w], start=(j == 0),
                                             stop=True, skip_group_check=True)
                    last.then_inc(S["a_m_ps"], 1)
                    pe.wait_ge(S["a_msgT"], n + 1)
                    out_tokens(4 * l + 3, msgT[l], wa[:, 3, :], S["a_y_ps"])

            pe.wait_ge(split_done, 4)
            pipelined(pe, step_a, 2, 1, NB)
            if stage == 1:
                return

            def expert(n, l, e):
                if e < NE:
                    if e >= 2:
                        pe.wait_ge(he_ready, n * NE + (e - 1))
                    bk = ps[:, HE + e % 2, 0:NT]
                    pe.matmul(bk, negsel[:, e, :], hotTb[l][:, :], start=True, stop=False)
                    pe.matmul(bk, w_e1[:, e, :], hT[l][:, :], start=False, stop=True).then_inc(he_ps, 1)
                if e > 0:
                    pe.wait_ge(he_ready, n * NE + e)
                    for c in range(2):
                        last = pe.matmul(ps[:, ACC, P * c:P * c + P], he[(e - 1) % 2][:, P * c:P * c + P],
                                         w_e2[:, e - 1, :], start=False, stop=True, skip_group_check=True)
                    last.then_inc(e_done, 1)

            def step_b(n, l, have):
                o = 1 - l
                if have(0):
                    pe.wait_ge(S["b_hot"], n + 1)
                    for c in range(2):
                        last = pe.transpose(ps[0:NE, LATE, P * c:P * c + P], hot[l][:, c, :], ident[:, :])
                    last.then_inc(S["b_hott_ps"], 1)
                if have(1):
                    pe.wait_ge(S["b_pT"], n + 2)
                    if have(0):
                        pe.wait_ge(S["b_hotT"], n + 1)
                    for j in range(NBLK):
                        for g in range(G):
                            last = pe.matmul(ps[heads(g), LATE, BLK * j:BLK * j + BLK], vbd[o][:, j, heads(g)],
                                             pT[o][:, g, BLK * j:BLK * j + BLK], start=True, stop=True)
                    last.then_inc(S["b_m_ps"], 1)
                if have(3):
                    if have(2):
                        pe.wait_ge(S["b_sm"], n + 3)
                    turn(3, t_xn[o], 2, S["b_xn"], n + 4, S["b_t_ps"])
                if have(1):
                    pe.wait_ge(S["b_msgT"], n + 2)
                    out_tokens(LATE, msgT[o], wf[:, 3, :], S["b_y_ps"])
                if have(3):
                    pe.wait_ge(S["b_xl"], n + 4)
                    project(o, 0, wf_h, wf_l, S["b_qk_ps"], S["b_v_ps"])
                if have(0):
                    pe.wait_ge(S["b_hotT"], n + 1)
                    if have(-1):
                        pe.wait_ge(b_sum_read, n)
                    for c in range(2):
                        pe.matmul(ps[:, ACC, P * c:P * c + P], hotT[l][:, P * c:P * c + P], b_e2[:, :],
                                  start=(c == 0), stop=True, skip_group_check=True)
                    for e in range(0, 4):
                        expert(n, l, e)
                if have(1):
                    turn(LATE, t_h[o], 2, S["b_h"], n + 2, S["b_ht_ps"])
                if have(0):
                    expert(n, l, 4)
                    expert(n, l, 5)
                if have(1):
                    pe.wait_ge(S["b_hT"], n + 2)
                    for c in range(2):
                        last = pe.matmul(ps[:, LATE, NE * c:NE * c + NE], hT[o][:, P * c:P * c + P], w_router[:, :],
                                         start=True, stop=True)
                    last.then_inc(S["b_l_ps"], 1)
                if have(0):
                    for e in (6, 7, 8):
                        expert(n, l, e)
                if have(3):
                    pe.wait_ge(S["b_kT"], n + 4)
                    pe.wait_ge(S["b_hbd"], n + 4)
                    pe.wait_ge(S["b_vbd"], n + 4)
                    for g in range(G):
                        pe.matmul(ps[:, g, 0:NT], rep[heads(g), :], same[heads(g), :], start=True, stop=True)
                    for j in range(NBLK):
                        for g in range(G):
                            last = score(o, ps[:, g, BLK * j:BLK * j + BLK], g, j, BLK, 1)
                    last.then_inc(S["b_s_ps"], 1)

            pe.wait_ge(w_loaded["b"], W_ALL["b"])
            pe.wait_ge(S["a_x"], NB)
            pipelined(pe, step_b, 4, 1, NB)
            if stage == 2:
                return
            pe.wait_ge(w_loaded["c"], W_ALL["c"])
            with pe.Fori(0, ITER) as i:
                for l in LANES:
                    turn(4 * l, c_xq[l], 2, S["c_xn_"], i * 2 + l + 1, S["c_t_ps"])
                for l in LANES:
                    pe.wait_ge(S["c_xT_"], i * 2 + l + 1)
                    pe.matmul(bank(l, 1, 0, NT), w_in[:, 0:D], c_xT[l][:, :], start=True, stop=True)
                    pe.matmul(bank(l, 2, 0, NT), w_in[:, D:2 * D], c_xT[l][:, :], start=True, stop=True
                              ).then_inc(S["c_in_ps"], 1)
                for l in LANES:
                    n = i * 2 + l + 1
                    pe.wait_ge(S["c_zs_"], n)
                    pe.wait_ge(S["c_xs_"], n)
                    pe.matmul(bank(l, 1, 0, NT), w_dt[:, :], xs[l][:, :], start=True, stop=True).then_inc(S["c_dt_ps"], 1)
                    pe.matmul(ps[0:DS, 4 * l + 3, 0:NT], w_b[:, :], xs[l][:, :], start=True, stop=True)
                    pe.matmul(ps[0:DS, 4 * l + 3, NT:2 * NT], w_c[:, :], xs[l][:, :], start=True, stop=True
                              ).then_inc(S["c_b_ps"], 1)
                    for c in range(2):
                        pe.matmul(bank(l, 0, NT * c, NT * c + NT), xs[l][:, P * c:P * c + P], flat3(w_bR[:, :, :]),
                                  start=True, stop=True)
                    pe.matmul(bank(l, 2, 0, NT), flat3(w_cR[:, :, :]), xs[l][:, :], start=True, stop=True
                              ).then_inc(S["c_c_ps"], 1)
                for l in LANES:
                    n = i * 2 + l + 1
                    pe.wait_ge(S["c_prod"], n)
                    pe.wait_ge(S["c_zb_"], n)
                    pe.wait_ge(S["c_cbd"], n)
                    for b, (j0, j1) in zip((3, 1, 2), PAIR_BANKS):
                        last = pe.matmul(bank(l, b, 0, OFF[j1] - OFF[j0]), ones[0:DS, :], prod[l][:, OFF[j0]:OFF[j1]],
                                         start=True, stop=True)
                    last.then_inc(S["c_g1_ps"], 1)
                for l in LANES:
                    n = i * 2 + l + 1
                    pe.wait_ge(S["c_wend"], n)
                    for c in range(2):
                        last = pe.transpose(bank(l, 0, P * c, P * c + P),
                                            wend[l][:, 16 * c:16 * c + 16, :].rearrange("p c t -> p (c t)"), ident[:, :])
                    last.then_inc(S["c_wt_ps"], 1)
                for l in LANES:
                    pe.wait_ge(S["c_wendT"], i * 2 + l + 1)
                    for c in range(2):
                        o = bank(l, 0).rearrange("p (n c) -> p n c", c=NCH)[:, :, 16 * c:16 * c + 16]
                        last = pe.matmul(o, wendT[l][:, c, :], bbd[l][:, c, :].rearrange("p (n c) -> p n c", c=16),
                                         start=True, stop=True)
                    last.then_inc(S["c_st_ps"], 1)
                for l in LANES:
                    n = i * 2 + l + 1
                    pe.wait_ge(S["c_term"], n)
                    pe.wait_ge(S["c_hc"], n)
                    for c in range(4):
                        last = pe.transpose(bank(l, 1, P * c, P * c + P),
                                            hc[l][:, 8 * c:8 * c + 8, :].rearrange("p c n -> p (c n)"), ident[:, :])
                    last.then_inc(S["c_hct_ps"], 1)
                for l in LANES:
                    pe.wait_ge(S["c_hcT"], i * 2 + l + 1)
                    for c in range(4):
                        last = pe.matmul(bank(l, 2, 64 * c, 64 * c + 64), hcT[l][:, c, :], cbd[l][:, 64 * c:64 * c + 64],
                                         start=True, stop=True)
                    last.then_inc(S["c_yi_ps"], 1)
                for l in LANES:
                    pe.wait_ge(S["c_y"], i * 2 + l + 1)
                    out_tokens(4 * l + 3, ya[l], w_out[:, :], S["c_out_ps"])
            if stage == 3:
                return
            pe.wait_ge(w_loaded["d"], W_ALL["d"])
            with pe.Fori(0, ITER_MLP) as i:
                for l in LANES:
                    turn(4 * l, d_xn[l], 4, S["d_xn_"], i * 2 + l + 1, S["d_t_ps"])
                for l in LANES:
                    pe.wait_ge(S["d_xT_"], i * 2 + l + 1)
                    for m in range(HID):
                        if m >= 2:
                            pe.wait_ge(m_h0[l], i * HID + m - 1)
                        pe.matmul(bank(l, 2 * (m % 2)), w_m1[:, P * m:P * m + P], d_xT[l][:, :], start=True, stop=True)
                        pe.matmul(bank(l, 2 * (m % 2) + 1), w_m2[:, P * m:P * m + P], d_xT[l][:, :], start=True, stop=True
                                  ).then_inc(m_gu_ps[l], 1)
                for w, src, ready, done in ((w_h1, h0, m_h0, m_h1_ps), (w_h2, h1, m_h1, m_h2_ps)):
                    for l in LANES:
                        pe.wait_ge(ready[l], i * HID + HID)
                        for m in range(HID):
                            for k in range(HID):
                                last = pe.matmul(bank(l, m), w[:, k, P * m:P * m + P], src[l][:, k, :],
                                                 start=(k == 0), stop=(k == HID - 1))
                            last.then_inc(done[l], 1)
                for l in LANES:
                    pe.wait_ge(m_h2[l], i * HID + HID)
                    for c in range(4):
                        for k in range(HID):
                            last = pe.matmul(bank(l, 0, P * c, P * c + P), h0[l][:, k, P * c:P * c + P], w_m3[:, k, :],
                                             start=(k == 0), stop=(k == HID - 1))
                    last.then_inc(S["d_y_ps"], 1)


def lay_out(inp):
    import numpy as np
    f = np.float32
    v = {k: np.asarray(t) for k, t in inp.items()}
    p = np.arange(P)
    r = {"x": v["L0_attn_x"]}
    wkv = v["L0_attn_wkv"].reshape(16, 2, HD, D)
    by_head = lambda t: t.reshape(D, G, 4, HD).transpose(0, 2, 1, 3).reshape(D, D)
    r["wa"] = np.stack([v["L0_attn_wq"].T, wkv[:, 0].reshape(D, D).T, by_head(wkv[:, 1].reshape(D, D).T),
                        v["L0_attn_wo"].T], 1)
    wi = v["L0_ffn_in_proj_w"]
    r["wf"] = np.stack([wi[0:D].T, wi[D:2 * D].T, by_head(wi[2 * D:].T), v["L0_ffn_out_w"].T], 1)
    r["w_router"] = v["L0_ffn_router_w"].T
    r["w_e1"] = v["L0_ffn_w1"].transpose(2, 0, 1)
    r["w_e2"] = v["L0_ffn_w2"].transpose(2, 0, 1)
    r["b_e2"] = v["L0_ffn_b2"]
    r["rows"] = np.broadcast_to(np.stack([v[n] for n in (
        "L0_attn_gamma", "L0_attn_beta", "L0_ffn_out_b", "L0_ffn_ln1_g", "L0_ffn_ln1_b", "L0_ffn_ln2_g",
        "L0_ffn_ln2_b")])[None, :, None, :], (P, 7, 2, D))
    r["router_b"] = np.broadcast_to(v["L0_ffn_router_b"][None, None, :], (P, 2, NE))
    bi = v["L0_ffn_in_proj_b"].reshape(3, D)
    blk = lambda t: t.reshape(HID, P).T
    cols = {"bq": bi[0][:, None], "bk": bi[1][:, None], "bv": bi[2][:, None], "b1": v["L0_ffn_b1"].T,
            "ln_g": v["L1_attn_ln_g"][:, None], "ln_b": v["L1_attn_ln_b"][:, None], "conv_w": v["L1_attn_conv_w"][:, 0, :],
            "conv_b": v["L1_attn_conv_b"][:, None], "dt_b": v["L1_attn_dt_b"][:, None],
            "log_A": v["L1_attn_log_A"][:, None], "D_param": v["L1_attn_D_param"][:, None],
            "w1_s": blk(v["L1_ffn_w1_s"]), "w2_s": blk(v["L1_ffn_w2_s"]), "h1_s": blk(v["L1_ffn_h1_s"]),
            "h2_s": blk(v["L1_ffn_h2_s"])}
    r["pp"] = np.concatenate([cols[n] for n in PP], 1)
    r["w_in"], r["w_dt"], r["w_b"], r["w_c"], r["w_out"] = (
        v["L1_attn_" + n] for n in ("W_in", "dt_w", "B_w", "C_w", "W_out"))
    r["w_bR"] = np.broadcast_to(v["L1_attn_B_w"][:, :, None], (D, DS, 16))
    r["w_cR"] = np.broadcast_to(v["L1_attn_C_w"][:, None, :], (D, 8, DS))
    r["w_m1"], r["w_m2"] = v["L1_ffn_w1_w"].T, v["L1_ffn_w2_w"].T
    for n, k in (("w_h1", "h1_w"), ("w_h2", "h2_w"), ("w_m3", "w3_w")):
        t = v["L1_ffn_" + k].T
        r[n] = t.reshape(HID, P, t.shape[1]).transpose(1, 0, 2)
    r["w3_s"] = np.broadcast_to(v["L1_ffn_w3_s"][None, None, :], (P, HID, D))
    r["c_ident"] = np.eye(P, dtype=f)
    r["c_headmask"] = (p[:, None] // HD % 4 == np.arange(4)[None, :]).astype(f)
    r["c_vmask"] = (p[:, None] // BLK == np.arange(BLK)[None, :] // HD).astype(f)
    r["c_rep"] = (p[:, None] % BLK == p[None, :] % BLK).astype(f)
    gap = np.arange(SPAN)[None, :] - (p % BLK)[:, None]
    r["c_band"] = np.tile(np.where((gap >= 1) & (gap <= WIN), 0.0, NEG).astype(f), (1, NBLK))
    own = (p % BLK)[:, None] // NB == np.arange(BLK)[None, :] // NB
    r["c_same"] = np.tile(np.where(own, 0.0, NEG).astype(f), (1, NBLK))
    e = np.arange(NE)
    r["c_negsel"] = np.where(e[:, None, None] == e[None, :, None], 0.0, NEG).astype(f) * np.ones((1, 1, P), f)
    r["c_iota"] = np.broadcast_to(e.astype(f), (P, NE))
    r["c_bmask"] = np.broadcast_to((p[:, None] // CH == np.arange(16)[None, :]).astype(f)[:, None, None, :], (P, 2, DS, 16))
    r["c_cmask"] = (p[:, None] // DS == np.arange(NT)[None, :] % 64 // CH).astype(f)
    r["c_first"] = np.broadcast_to((np.arange(NT) % CH != 0).astype(f), (P, NT))
    return {k: np.ascontiguousarray(t) for k, t in r.items()}


def kernel(**inputs):
    import concourse.bacc as _bacc
    from concourse import mybir as _mybir
    from concourse.bass_utils import run_bass_kernel_spmd as _run

    nc = _bacc.Bacc("TRN2", target_bir_lowering=False, num_devices=1)
    arrays, args = {}, {}
    for name, v in lay_out(inputs).items():
        arrays[f"in_{name}"] = v
        args[name] = nc.dram_tensor(f"in_{name}", v.shape, _mybir.dt.from_np(v.dtype), kind="ExternalInput").ap()
    out = nc.dram_tensor("out_x", (NB, NT, D), F32, kind="ExternalOutput").ap()
    build(nc, args, out)
    r = _run(nc, [arrays], core_ids=[0])
    return r.results[0]["out_x"]
```

```python
from contextlib import ExitStack

import concourse.bass as bass
from concourse import mybir

F32 = mybir.dt.float32
BF16 = mybir.dt.bfloat16
F32R = mybir.dt.float32r
U32 = mybir.dt.uint32
ALU = mybir.AluOpType
ACT = mybir.ActivationFunctionType
AX = mybir.AxisListType

P = 128
D = 128
NB, NT = 16, 256
HD = 8
G = 4
BLK = 32
WIN = 16
SPAN = BLK + WIN
NBLK = NT // BLK
NE = 8
DS = 16
CH = 8
NCH = NT // CH
HID = 4
EPS = 1e-5
NEG = -1e12
ATT_SCALE = float(HD) ** -0.5
LANES = (0, 1)
ITER = NB // 2
ITER_MLP = NB // 4

PP = {}
for _name, _n in (("bq", 1), ("bk", 1), ("bv", 1), ("b1", NE), ("ln_g", 1), ("ln_b", 1), ("conv_w", 4), ("conv_b", 1),
                  ("dt_b", 1), ("log_A", 1), ("D_param", 1), ("w1_s", HID), ("w2_s", HID), ("h1_s", HID), ("h2_s", HID)):
    PP[_name] = sum(n for n, _ in PP.values()), _n
    PP[_name] = (_n, sum(n for k, (n, _) in PP.items() if k != _name))
NPP = sum(n for n, _ in PP.values())

OFF = [sum(NCH * (CH - k) for k in range(j)) for j in range(CH + 1)]
PAIR_BANKS = ((0, 2), (2, 5), (5, 8))


class Chain:

    def __init__(self, eng, sem):
        self.eng, self.sem, self.count = eng, sem, 0

    def clear(self):
        self.eng.sem_clear(self.sem)
        self.count = 0

    def link(self, ins):
        self.count += 1
        ins.then_inc(self.sem, 1)
        self.eng.wait_ge(self.sem, self.count)


def pipelined(eng, step, ahead, behind, tiles, turn=2):
    def one(n):
        step(n, n % turn, lambda k: 0 <= n + k < tiles)

    lo, hi = behind, tiles - ahead
    turns = (hi - lo) // turn
    for n in range(-ahead, lo):
        one(n)
    with eng.Fori(0, turns) as i:
        for k in range(turn):
            step(i * turn + (lo + k), (lo + k) % turn, lambda d: True)
    for n in range(lo + turn * turns, tiles + behind):
        one(n)


class LayerNorm:

    def __init__(self, name, k, sb, sem):
        self.k = k
        self.st = [sb(f"{name}_st{l}", [P, k, 6]) for l in LANES]
        self.mv = [sb(f"{name}_mv{l}", [P, k, 2]) for l in LANES]
        self.ve = [sb(f"{name}_ve{l}", [P, k]) for l in LANES]
        self.rs = [sb(f"{name}_rs{l}", [P, k]) for l in LANES]
        self.mv_ready = sem(f"{name}_mv_ready")
        self.rstd_ready = sem(f"{name}_rstd_ready")

    def stats(self, dve, chain, src, l):
        for b in range(self.k):
            last = dve.bn_stats(self.st[l][:, b, :], src(b))
        chain.link(last)
        for b in range(self.k):
            last = dve.bn_aggr(self.mv[l][:, b, :], self.st[l][:, b, :])
        last.then_inc(self.mv_ready, 1)

    def rstd(self, pool, chain, eps, half, l, n):
        pool.wait_ge(self.mv_ready, n)
        chain.link(pool.tensor_tensor(self.ve[l][:, :], self.mv[l][:, :, 1], eps[:, 0:self.k], ALU.add))
        pool.tensor_tensor(self.rs[l][:, :], self.ve[l][:, :], half[:, 0:self.k], ALU.pow).then_inc(self.rstd_ready, 1)

    def apply(self, dve, out, src, l, n, scale=None):
        rs = self.rs if scale is None else scale
        dve.wait_ge(self.rstd_ready, n)
        for b in range(self.k):
            last = dve.tensor_scalar(out(b), src(b), self.mv[l][:, b, 0:1], rs[l][:, b:b + 1],
                                     ALU.subtract, ALU.mult)
        return last


def build(nc, a, out):
    with ExitStack() as ctx:
        def sb(name, shape, dt=F32):
            return ctx.enter_context(nc.sbuf_tensor(name, shape, dt))

        def sem(name):
            return ctx.enter_context(nc.semaphore(name))

        ps = ctx.enter_context(nc.psum_tensor("ps", [P, 8, 512], F32))

        x = sb("x", [P, 2 * NB, D])
        ident = sb("ident", [P, P])
        eps = sb("eps", [P, 4])
        half = sb("half", [P, 4])
        pp = sb("pp", [P, NPP])
        w_in = sb("w_in", [P, 2 * D])
        w_dt = sb("w_dt", [P, D])
        w_b = sb("w_b", [P, DS])
        w_c = sb("w_c", [P, DS])
        w_bR = sb("w_bR", [P, DS, 16])
        w_cR = sb("w_cR", [P, 8, DS])
        w_out = sb("w_out", [P, D])
        bmask = sb("bmask", [P, 2, DS, 16])
        cmask = sb("cmask", [P, NT])
        first = sb("first", [P, NT])
        ones = sb("ones", [P, P])
        expA = sb("expA", [P, 1])
        negA = sb("negA", [P, 1])
        w_m1 = sb("w_m1", [P, HID * D])
        w_m2 = sb("w_m2", [P, HID * D])
        w_h1 = sb("w_h1", [P, HID, HID * D])
        w_h2 = sb("w_h2", [P, HID, HID * D])
        w_m3 = sb("w_m3", [P, HID, D])
        w3_s = sb("w3_s", [P, HID, D])

        outer, ctx = ctx, ExitStack()
        headmask = sb("headmask", [P, G])
        vmask = sb("vmask", [P, BLK])
        rep = sb("rep", [P, P], BF16)
        wa = sb("wa", [P, 4, D])
        wf = sb("wf", [P, 4, D])
        w_router = sb("w_router", [P, NE])
        w_e1 = sb("w_e1", [P, NE, D])
        w_e2 = sb("w_e2", [P, NE, D])
        b_e2 = sb("b_e2", [NE, D])
        rows = sb("rows", [P, 7, 2, D])
        router_b = sb("router_b", [P, 2, NE])
        iota = sb("iota", [P, NE])
        negsel = sb("negsel", [NE, NE, P], BF16)
        band = sb("band", [P, NBLK * SPAN], BF16)
        same = sb("same", [P, NBLK * BLK], BF16)
        layer0, ctx = ctx, outer

        fill_done, cast_ready, expA_ready, negA_ready, zero_ready = (sem(n) for n in (
            "fill_done", "cast_ready", "expA_ready", "negA_ready", "zero_ready"))
        w_loaded = {k: sem("w_loaded_" + k) for k in "abcd"}
        x_loaded = [sem(f"x_loaded{l}") for l in LANES]
        pool_chain, dve_chain, act_chain = sem("pool_chain"), sem("dve_chain"), sem("act_chain")

        loads = {
            "a": [(ident[:, :], "c_ident"), (headmask[:, :], "c_headmask"), (vmask[:, :], "c_vmask"),
                  (wa[:, :, :], "wa"), (rows[:, :, :, :], "rows"), (pp[:, :], "pp")],
            "b": [(wf[:, :, :], "wf"), (w_router[:, :], "w_router"), (w_e1[:, :, :], "w_e1"), (w_e2[:, :, :], "w_e2"),
                  (b_e2[:, :], "b_e2"), (router_b[:, :, :], "router_b"), (iota[:, :], "c_iota")],
            "c": [(w_in[:, :], "w_in"), (w_dt[:, :], "w_dt"), (w_b[:, :], "w_b"), (w_c[:, :], "w_c"),
                  (w_bR[:, :, :], "w_bR"), (w_cR[:, :, :], "w_cR"), (w_out[:, :], "w_out"),
                  (bmask[:, :, :, :], "c_bmask"), (cmask[:, :], "c_cmask"), (first[:, :], "c_first")],
            "d": [(w_m1[:, :], "w_m1"), (w_m2[:, :], "w_m2"), (w_h1[:, :, :], "w_h1"), (w_h2[:, :, :], "w_h2"),
                  (w_m3[:, :, :], "w_m3"), (w3_s[:, :, :], "w3_s")],
        }
        W_ALL = {k: 16 * len(v) for k, v in loads.items()}
        W_ALL["a"] += 16 * 4

        def vec(name, c=0):
            return pp[:, PP[name][1] + c:PP[name][1] + c + 1]

        def tok(name, k=2):
            return [sb(f"{name}{l}", [P, k, D]) for l in LANES]

        def chan(name):
            return [sb(f"{name}{l}", [P, NT]) for l in LANES]

        def flat3(t):
            return t.rearrange("p a b -> p (a b)")

        ctx = layer0
        stage_f = [sb("stage_rep", [P, P]), sb("stage_band", [P, NBLK * SPAN]), sb("stage_same", [P, NBLK * BLK]),
                   sb("stage_negsel", [NE, NE, P])]
        xB = sb("xB", [P, 2 * NB, D])
        t_xn, t_xb, t_y, t_zn, t_zg, t_z, t_o, t_h, t_on, t_og, t_yo = (
            tok("t_" + n) for n in ("xn", "xb", "y", "zn", "zg", "z", "o", "h", "on", "og", "yo"))
        xh, xl = ([sb(f"{n}{l}", [P, NT], F32R) for l in LANES] for n in ("xh", "xl"))
        wa_h, wa_l, wf_h, wf_l = (sb(n, [P, 3, D], F32R) for n in ("wa_h", "wa_l", "wf_h", "wf_l"))
        msgT = chan("msgT")
        qk, rest = ([sb(f"{n}{l}", [P, 2, NT]) for l in LANES] for n in ("qk", "rest"))
        parts = [sb(f"parts{l}", [P, 3, 2, NT], BF16) for l in LANES]
        hbd = [sb(f"hbd{l}", [P, 3, NBLK, 4, BLK], BF16) for l in LANES]
        vT = [sb(f"vT{l}", [P, NT]) for l in LANES]
        vbd = [sb(f"vbd{l}", [P, NBLK, D]) for l in LANES]
        with ExitStack() as only_a:
            tau = [only_a.enter_context(nc.sbuf_tensor(f"tau{l}", [P, G, NBLK * SPAN], F32)) for l in LANES]
        sm = [sb(f"sm{l}", [P, G * NBLK, BLK]) for l in LANES]
        ex = [sb(f"ex{l}", [P, G * NBLK, BLK]) for l in LANES]
        pT = [sb(f"pT{l}", [P, G, NBLK * BLK]) for l in LANES]
        mx, den, rden = ([sb(f"{n}{l}", [P, G * NBLK]) for l in LANES] for n in ("mx", "den", "rden"))
        hT = chan("hT")
        lg, le = ([sb(f"{n}{l}", [P, 2, NE]) for l in LANES] for n in ("lg", "le"))
        lmx = [sb(f"lmx{l}", [P, 2]) for l in LANES]
        m8 = [sb(f"m8{l}", [P, 2, 8]) for l in LANES]
        ix = [sb(f"ix{l}", [P, 2, 8], U32) for l in LANES]
        pick = [sb(f"pick{l}", [P, 2]) for l in LANES]
        hot = [sb(f"hot{l}", [P, 2, NE]) for l in LANES]
        hotT = [sb(f"hotT{l}", [NE, NT]) for l in LANES]
        hotTb = [sb(f"hotTb{l}", [NE, NT], BF16) for l in LANES]
        he = [sb(f"he{c}", [P, NT]) for c in range(2)]
        a_ln1, a_ln2, a_ln3, b_ln0, b_ln1, b_ln2, b_ln3 = (
            LayerNorm(n, 2, sb, lambda m: outer.enter_context(nc.semaphore(m)))
            for n in ("a_ln1", "a_ln2", "a_ln3", "b_ln0", "b_ln1", "b_ln2", "b_ln3"))
        ctx.close()

        ctx = outer
        wm_h, wm_l = (sb(n, [P, 2, HID * D], F32R) for n in ("wm_h", "wm_l"))
        wh_h, wh_l = (sb(n, [P, 2, HID, HID * D], F32R) for n in ("wh_h", "wh_l"))
        ctx = ExitStack()
        c_xq, c_r, c_o = (tok("c_" + n) for n in ("xq", "r", "o"))
        c_xn = [sb(f"c_xn{k}", [P, 2, D]) for k in range(4)]
        zs = [sb(f"c_zs{k}", [P, NT]) for k in range(4)]
        c_xT, cv, xs, xd, zb, sp_, dt, cdt, ya, yi = (
            chan("c_" + n) for n in ("xT", "cv", "xs", "xd", "zb", "sp", "dt", "cdt", "ya", "yi"))
        xpad = [sb(f"xpad{l}", [P, 3 + NT]) for l in LANES]
        dec = [sb(f"dec{l}", [P, 2, NCH, CH]) for l in LANES]
        bcT = [sb(f"bcT{l}", [DS, 2, NCH, CH]) for l in LANES]
        prod = [sb(f"prod{l}", [DS, OFF[CH]]) for l in LANES]
        wall = [sb(f"wall{l}", [P, OFF[CH]]) for l in LANES]
        term = [sb(f"term{l}", [P, OFF[CH]]) for l in LANES]
        wend = [sb(f"wend{l}", [P, NCH, CH]) for l in LANES]
        wendT = [sb(f"wendT{l}", [P, 2, D]) for l in LANES]
        bbd = [sb(f"bbd{l}", [P, 2, DS * 16]) for l in LANES]
        cbd = [sb(f"cbd{l}", [P, NT]) for l in LANES]
        d0 = [sb(f"d0{l}", [P, DS, NCH]) for l in LANES]
        hs = [sb(f"hs{l}", [P, DS, NCH]) for l in LANES]
        hc = [sb(f"hc{l}", [P, NCH, DS]) for l in LANES]
        hcT = [sb(f"hcT{l}", [P, 4, D]) for l in LANES]
        c_v2, c_r2 = ([sb(f"{n}{l}", [P, 2]) for l in LANES] for n in ("c_v2", "c_r2"))
        new = lambda m: outer.enter_context(nc.semaphore(m))
        c_ln1, c_ln2 = (LayerNorm(n, 2, sb, new) for n in ("c_ln1", "c_ln2"))
        ctx.close()
        ctx = ExitStack()
        d_xn, d_y, d_o = (tok("d_" + n, 4) for n in ("xn", "y", "o"))
        d_xh, d_xl = ([sb(f"{n}{l}", [P, 4 * P], F32R) for l in LANES] for n in ("d_xh", "d_xl"))
        gate = [[sb(f"gate{l}{c}", [P, 4 * P]) for c in range(2)] for l in LANES]
        hid = [sb(f"hid{l}", [P, HID, 4 * P]) for l in LANES]
        h0_h, h0_l, h1_h, h1_l = ([sb(f"{n}{l}", [P, HID, 4 * P], F32R) for l in LANES]
                                  for n in ("h0_h", "h0_l", "h1_h", "h1_l"))
        d_ln1, d_ln2 = (LayerNorm(n, 4, sb, new) for n in ("d_ln1", "d_ln2"))
        ctx.close()
        ctx = outer
        last_weights = ((wm_h[:, 0, :], wm_l[:, 0, :], w_m1[:, :]), (wm_h[:, 1, :], wm_l[:, 1, :], w_m2[:, :]),
                        (wh_h[:, 0, :, :], wh_l[:, 0, :, :], w_h1[:, :, :]), (wh_h[:, 1, :, :], wh_l[:, 1, :, :], w_h2[:, :, :]))

        SEMS = """a_xn a_xb a_t_ps a_xh a_xl b_xh b_xl a_qk_ps a_v_ps a_qT a_hbd a_vbd a_s_ps a_tau a_m_ps a_msgT a_y_ps
            a_y a_zn a_z a_o a_x a_stored b_xn b_xb b_t_ps b_qk_ps b_v_ps b_kT b_hbd b_vbd b_s_ps b_sm b_ex b_rden
            b_p b_pT b_m_ps b_msgT b_y_ps b_zn b_h b_ht_ps b_hT b_l_ps b_lg b_le b_hot b_hott_ps b_hotT b_on b_z b_o
            b_x b_stored c_r2 c_xn_ c_t_ps c_xT_ c_in_ps c_xpad c_zs_ c_cv_ c_xs_ c_dt_ps c_b_ps c_c_ps c_zb_ c_sp_
            c_dt_ c_dec c_bcT c_prod c_g1_ps c_term c_ys c_xd c_cbd c_bbd c_wall c_wend c_wt_ps c_wendT c_st_ps c_d0
            c_hs c_hc c_hct_ps c_hcT c_yi_ps c_y c_out_ps c_o_ c_x d_xn_ d_t_ps d_xh d_xl d_y_ps d_o_ d_x d_stored""".split()
        S = {n: sem(n) for n in SEMS}
        he_ps, he_ready, e_done = (sem(n) for n in ("he_ps", "he_ready", "e_done"))
        STATE, IN, DT, BC, BR, PAIRS = 0, 1, 2, 3, 4, 5
        b_sum_read, split_done = sem("b_sum_read"), sem("split_done")
        LATE, HE, ACC = 4, 5, 7
        m_gu_ps, m_gate, m_raw, m_high, m_h0, m_h1_ps, m_h1_high, m_h1, m_h2_ps, m_h2, m_split = (
            sem(n) for n in ("m_gu_ps", "m_gate", "m_raw", "m_high", "m_h0", "m_h1_ps", "m_h1_high", "m_h1", "m_h2_ps",
                             "m_h2", "m_split"))

        def blocks_done(n, l, m):
            return n * (2 * HID) + (l * HID + m + 1)

        out_t = out.rearrange("b (h p) d -> (b h) p d", p=P)
        x1 = nc.dram_tensor("x1", (NB, NT, D), F32, kind="Internal").ap()
        x2 = nc.dram_tensor("x2", (NB, NT, D), F32, kind="Internal").ap()
        by_seq = lambda t: t.rearrange("b (h p) d -> (b h) p d", p=P)
        by_step = lambda t: t.rearrange("b (k s) d -> k s b d", s=8)

        def xblk(t, i, c):
            return t[:, bass.ds(i + c, 1), :].rearrange("p o d -> p (o d)")

        def heads(g):
            return slice(BLK * g, BLK * g + BLK)

        def bank(l, b, lo=0, hi=512):
            return ps[:, 4 * l + b, lo:hi]

        block = ctx.enter_context(nc.Block())

        @block.sync
        def _(sp):
            def load(per, first, issue):
                for l in LANES:
                    issue(0, l)
                with sp.Fori(1, ITER) as i:
                    for l in LANES:
                        sp.wait_ge(x_loaded[l], i * (16 * per) + first)
                        issue(i, l)

            def load_seq(src):
                def issue(i, l):
                    sp.dma_start(x[:, bass.ds(i * 4 + 2 * l, 2), :],
                                 by_seq(src)[bass.ds(i * 4 + 2 * l, 2)].rearrange("b p d -> p b d")
                                 ).then_inc(x_loaded[l], 16)
                return issue

            def load_step(src):
                def issue(i, l):
                    for b in range(2):
                        sp.dma_start(xblk(xB, i * 4, 2 * l + b),
                                     by_step(src)[bass.ds(i * 4 + 2 * l + b, 1)].rearrange("o s b d -> (o s) b d")
                                     ).then_inc(x_loaded[l], 16)
                return issue

            load(1, 0, load_seq(a["x"]))
            with sp.Fori(0, ITER) as i:
                for l in LANES:
                    sp.wait_ge(S["a_x"], i * 2 + l + 1)
                    sp.dma_start(by_seq(x1)[bass.ds(i * 4 + 2 * l, 2)].rearrange("b p d -> p b d"),
                                 x[:, bass.ds(i * 4 + 2 * l, 2), :]).then_inc(S["a_stored"], 16)
            sp.wait_ge(S["a_stored"], 16 * NB)
            load(2, 16 * ITER, load_step(x1))
            with sp.Fori(0, ITER) as i:
                for l in LANES:
                    sp.wait_ge(S["b_x"], i * 2 + l + 1)
                    for b in range(2):
                        sp.dma_start(by_step(x2)[bass.ds(i * 4 + 2 * l + b, 1)].rearrange("o s b d -> (o s) b d"),
                                     xB[:, bass.ds(i * 4 + 2 * l + b, 1), :].rearrange("p o d -> p (o d)")
                                     ).then_inc(S["b_stored"], 16)
            sp.wait_ge(S["b_stored"], 32 * NB)
            load(1, 48 * ITER, load_seq(x2))
            with sp.Fori(0, ITER_MLP) as i:
                for l in LANES:
                    sp.wait_ge(S["d_x"], i * 2 + l + 1)
                    sp.dma_start(out_t[bass.ds(i * 8 + 4 * l, 4)].rearrange("b p d -> p b d"),
                                 x[:, bass.ds(i * 8 + 4 * l, 4), :]).then_inc(S["d_stored"], 16)
            sp.wait_ge(S["d_stored"], 16 * 2 * ITER_MLP)

        @block.gpsimd
        def _(pool):
            chain = Chain(pool, pool_chain)
            pool.memset(eps[:, :], EPS).then_inc(fill_done, 1)
            pool.memset(half[:, :], -0.5).then_inc(fill_done, 1)
            pool.memset(ones[:, :], 1.0).then_inc(fill_done, 1)
            pool.wait_ge(fill_done, 3)
            pool.wait_ge(w_loaded["a"], W_ALL["a"])

            def scale_shift(l, n, ready, src, tmp, dst, g, b, done):
                pool.wait_ge(ready, n)
                chain.link(pool.tensor_tensor(tmp[l][:, :, :], src[l][:, :, :], rows[:, g, :, :], ALU.mult))
                pool.tensor_tensor(dst[l][:, :, :], tmp[l][:, :, :], rows[:, b, :, :], ALU.add).then_inc(done, 1)

            def copy(dst, src, one):
                return pool.tensor_tensor(dst, src, one, ALU.mult)

            def step_a(n, l, have):
                chain.clear()
                if have(-1):
                    a_ln2.rstd(pool, chain, eps, half, 1 - l, n)
                if have(2):
                    a_ln1.rstd(pool, chain, eps, half, l, n + 3)
                if have(1):
                    pool.wait_ge(S["a_xn"], n + 2)
                    if have(-1):
                        pool.wait_ge(S["a_y"], n)
                    copy(t_xb[1 - l][:, :, :], t_xn[1 - l][:, :, :], ones[:, :].unsqueeze(1).to_broadcast([P, 2, D])
                         ).then_inc(S["a_xb"], 1)
                if have(-1):
                    scale_shift(1 - l, n, S["a_zn"], t_zn, t_zg, t_z, 0, 1, S["a_z"])
                    a_ln3.rstd(pool, chain, eps, half, 1 - l, n)
                    pool.wait_ge(S["a_o"], n)
                    xt = x[:, bass.ds(n * 2 - 2, 2), :]
                    pool.tensor_tensor(xt, xt, t_o[1 - l][:, :, :], ALU.add).then_inc(S["a_x"], 1)

            pipelined(pool, step_a, 2, 1, NB)

            def step_b(n, l, have):
                chain.clear()
                o = 1 - l
                if have(-1):
                    b_ln2.rstd(pool, chain, eps, half, o, n)
                    scale_shift(o, n, S["b_on"], t_on, t_og, t_z, 5, 6, S["b_z"])
                if have(1):
                    b_ln1.rstd(pool, chain, eps, half, o, n + 2)
                    scale_shift(o, n + 2, S["b_zn"], t_zn, t_zg, t_h, 3, 4, S["b_h"])
                if have(4):
                    b_ln0.rstd(pool, chain, eps, half, l, n + 5)
                if have(3):
                    pool.wait_ge(S["b_xn"], n + 4)
                    pool.tensor_tensor(t_xb[o][:, :, :], t_xn[o][:, :, :], rows[:, 2, :, :], ALU.add).then_inc(S["b_xb"], 1)
                if have(-1):
                    b_ln3.rstd(pool, chain, eps, half, o, n)
                    pool.wait_ge(S["b_o"], n)
                    xt = xB[:, bass.ds(n * 2 - 2, 2), :]
                    pool.tensor_tensor(xt, xt, t_o[o][:, :, :], ALU.add).then_inc(S["b_x"], 1)
                if have(2):
                    pool.wait_ge(S["b_rden"], n + 3)
                    pool.tensor_tensor(sm[l][:, :, :], ex[l][:, :, :],
                                       rden[l][:, :].unsqueeze(2).to_broadcast([P, G * NBLK, BLK]),
                                       ALU.mult).then_inc(S["b_p"], 1)

            pool.wait_ge(S["a_x"], NB)
            pipelined(pool, step_b, 4, 1, NB)
            pool.wait_ge(S["b_stored"], 32 * NB)
            for l in LANES:
                pool.memset(xpad[l][:, 0:3], 0.0)
                pool.memset(d0[l][:, :, 0:1], 0.0)
                pool.memset(hc[l][:, 0:1, :], 0.0).then_inc(zero_ready, 1)
            def step_c(n, q, have):
                chain.clear()
                l, o = q % 2, 1 - q % 2
                if have(0):
                    pool.wait_ge(S["c_wall"], n + 1)
                    for j in range(CH):
                        w = wall[l][:, OFF[j]:OFF[j + 1]].rearrange("p (c t) -> p c t", t=CH - j)
                        last = copy(wend[l][:, :, CH - 1 - j], w[:, :, CH - 1 - j], ones[:, 0:NCH])
                    last.then_inc(S["c_wend"], 1)
                if have(1):
                    pool.wait_ge(S["c_bcT"], n + 2)
                    for j in range(CH):
                        last = pool.tensor_tensor(
                            prod[o][:, OFF[j]:OFF[j + 1]].rearrange("p (c t) -> p c t", t=CH - j),
                            bcT[o][:, 1, :, j:CH], bcT[o][:, 0, :, 0:CH - j], ALU.mult)
                    last.then_inc(S["c_prod"], 1)
                if have(3):
                    c_ln1.rstd(pool, chain, eps, half, o, n + 4)
                    pool.wait_ge(c_ln1.rstd_ready, n + 4)
                    chain.link(pool.tensor_tensor(c_v2[o][:, :], c_ln1.mv[o][:, :, 1], c_ln1.rs[o][:, :], ALU.mult))
                    chain.link(pool.tensor_tensor(c_v2[o][:, :], c_v2[o][:, :], c_ln1.rs[o][:, :], ALU.mult))
                    chain.link(pool.tensor_tensor(c_v2[o][:, :], c_v2[o][:, :], eps[:, 0:2], ALU.add))
                    chain.link(pool.tensor_tensor(c_v2[o][:, :], c_v2[o][:, :], half[:, 0:2], ALU.pow))
                    pool.tensor_tensor(c_r2[o][:, :], c_v2[o][:, :], c_ln1.rs[o][:, :], ALU.mult).then_inc(S["c_r2"], 1)
                if have(0):
                    pool.wait_ge(S["c_term"], n + 1)
                    y = term[l][:, 0:NT].rearrange("p (c t) -> p c t", t=CH)
                    for j in range(1, CH):
                        chain.link(pool.tensor_tensor(y[:, :, j:CH], y[:, :, j:CH],
                                                      term[l][:, OFF[j]:OFF[j + 1]].rearrange("p (c t) -> p c t", t=CH - j),
                                                      ALU.add))
                    pool.wait_ge(S["c_xd"], n + 1)
                    pool.tensor_tensor(term[l][:, 0:NT], term[l][:, 0:NT], xd[l][:, :], ALU.add).then_inc(S["c_ys"], 1)
                if have(-2):
                    pool.wait_ge(S["c_o_"], n - 1)
                    xt = x[:, bass.ds(n * 2 - 4, 2), :]
                    pool.tensor_tensor(xt, xt, c_o[l][:, :, :], ALU.add).then_inc(S["c_x"], 1)
                if have(-1):
                    c_ln2.rstd(pool, chain, eps, half, o, n)

            def step_c_split(n, q, have):
                step_c(n, q, have)
                if isinstance(n, int) and n < 0:
                    if n == -3:
                        pool.wait_ge(m_split, 4)
                    for hi, lo, w in {-3: last_weights[:2], -2: last_weights[2:3], -1: last_weights[3:]}[n]:
                        pool.tensor_tensor(lo, w, hi.bitcast(F32), ALU.subtract).then_inc(m_split, 1)

            pipelined(pool, step_c_split, 3, 2, NB, 4)
            def step_d(n, q, have):
                chain.clear()
                if have(-1):
                    for l in LANES:
                        d_ln2.rstd(pool, chain, eps, half, l, n * 2 + (l - 1))
                    for l in LANES:
                        pool.wait_ge(S["d_o_"], n * 2 + (l - 1))
                        xt = x[:, bass.ds(n * 8 + (4 * l - 8), 4), :]
                        pool.tensor_tensor(xt, xt, d_o[l][:, :, :], ALU.add).then_inc(S["d_x"], 1)
                if have(1):
                    for l in LANES:
                        d_ln1.rstd(pool, chain, eps, half, l, n * 2 + (l + 3))

            pipelined(pool, step_d, 1, 1, ITER_MLP, 1)

        @block.scalar
        def _(act):
            chain = Chain(act, act_chain)
            for t, name in zip(stage_f, ("c_rep", "c_band", "c_same", "c_negsel")):
                dst = t[:, :, :] if name == "c_negsel" else t[:, :]
                act.dma_start(dst, a[name]).then_inc(w_loaded["a"], 16)
            for part in "abcd":
                for dst, name in loads[part]:
                    act.dma_start(dst, a[name]).then_inc(w_loaded[part], 16)

            def transposed(l, b, n, t_ps, done):
                act.wait_ge(t_ps, n)
                act.activation(xh[l][:, :], ps[:, b, 0:NT], ACT.Copy).then_inc(done, 1)

            def step_a(n, l, have):
                if have(1):
                    act.wait_ge(S["a_qk_ps"], n + 2)
                    act.activation(qk[1 - l][:, :, :], ps[:, 4 * (1 - l):4 * (1 - l) + 2, 0:NT], ACT.Copy
                                   ).then_inc(S["a_qT"], 1)
                if have(0):
                    for k in range(2):
                        act.wait_ge(S["a_s_ps"], n * 2 + (k + 1))
                        act.activation(tau[l][:, 2 * k:2 * k + 2, :],
                                       ps[:, 4 * l + 2 * k:4 * l + 2 * k + 2, 0:NBLK * SPAN], ACT.Sigmoid,
                                       scale=ATT_SCALE).then_inc(S["a_tau"], 1)
                if have(2):
                    transposed(l, 4 * (1 - l) + 3, n + 3, S["a_t_ps"], S["a_xh"])
                if have(0):
                    act.wait_ge(S["a_m_ps"], n + 1)
                    act.activation(msgT[l][:, :], bank(l, 0, 0, NT), ACT.Copy).then_inc(S["a_msgT"], 1)

            pipelined(act, step_a, 2, 1, NB)

            def gelu(n, l, e):
                act.wait_ge(he_ps, n * NE + (e + 1))
                if e >= 2:
                    act.wait_ge(e_done, n * NE + (e - 1))
                act.activation(he[e % 2][:, :], ps[:, HE + e % 2, 0:NT], ACT.Gelu,
                               bias=vec("b1", e)).then_inc(he_ready, 1)

            def step_b(n, l, have):
                if have(0):
                    act.wait_ge(S["b_hott_ps"], n + 1)
                    act.activation(hotT[l][:, :], ps[0:NE, LATE, 0:NT], ACT.Copy)
                    act.activation(hotTb[l][:, :], ps[0:NE, LATE, 0:NT], ACT.Copy).then_inc(S["b_hotT"], 1)
                if have(1):
                    act.wait_ge(S["b_m_ps"], n + 2)
                    act.activation(msgT[1 - l][:, :], ps[:, LATE, 0:NT], ACT.Identity, bias=vec("bv")
                                   ).then_inc(S["b_msgT"], 1)
                if have(3):
                    transposed(1 - l, 3, n + 4, S["b_t_ps"], S["b_xh"])
                if have(3):
                    act.wait_ge(S["b_qk_ps"], n + 4)
                    act.activation(qk[1 - l][:, 0, :], ps[:, 0, 0:NT], ACT.Identity, bias=vec("bq"))
                    act.activation(qk[1 - l][:, 1, :], ps[:, 1, 0:NT], ACT.Identity, bias=vec("bk")
                                   ).then_inc(S["b_kT"], 1)
                if have(0):
                    for e in range(0, 4):
                        gelu(n, l, e)
                if have(1):
                    act.wait_ge(S["b_ht_ps"], n + 2)
                    act.activation(hT[1 - l][:, :], ps[:, LATE, 0:NT], ACT.Copy).then_inc(S["b_hT"], 1)
                if have(0):
                    for e in range(4, NE):
                        gelu(n, l, e)
                if have(2):
                    act.wait_ge(S["b_sm"], n + 3)
                    act.activation(ex[l][:, :, :], sm[l][:, :, :], ACT.Exp, scale=ATT_SCALE).then_inc(S["b_ex"], 1)
                if have(1):
                    act.wait_ge(S["b_lg"], n + 2)
                    act.activation(le[1 - l][:, :, :], lg[1 - l][:, :, :], ACT.Exp).then_inc(S["b_le"], 1)

            act.wait_ge(w_loaded["a"], W_ALL["a"])
            act.wait_ge(w_loaded["b"], W_ALL["b"])
            act.wait_ge(S["a_x"], NB)
            pipelined(act, step_b, 4, 1, NB)
            act.wait_ge(S["b_stored"], 32 * NB)
            act.wait_ge(w_loaded["c"], W_ALL["c"])
            act.wait_ge(zero_ready, 2)
            act.activation(expA[:, :], vec("log_A"), ACT.Exp).then_inc(expA_ready, 1)
            act.wait_ge(w_loaded["d"], W_ALL["d"])
            for hi, lo, w in last_weights:
                act.activation(hi, w, ACT.Copy).then_inc(m_split, 1)
            act.wait_ge(negA_ready, 1)
            def step_c(n, q, have):
                chain.clear()
                l, o = q % 2, 1 - q % 2
                if have(1):
                    act.wait_ge(S["c_zb_"], n + 2)
                    chain.link(act.activation(sp_[o][:, :], zb[o][:, :], ACT.Abs))
                    chain.link(act.activation(sp_[o][:, :], sp_[o][:, :], ACT.Exp, scale=-1.0))
                if have(2):
                    act.wait_ge(S["c_t_ps"], n + 3)
                    act.activation(c_xT[l][:, :], ps[:, IN, 0:NT], ACT.Identity, bias=vec("ln_b"),
                                   scale=vec("ln_g")).then_inc(S["c_xT_"], 1)
                if have(1):
                    act.wait_ge(S["c_b_ps"], n + 2)
                    act.activation(bcT[o][:, :, :, :].rearrange("p a c t -> p (a c t)"), ps[0:DS, BC, :],
                                   ACT.Copy).then_inc(S["c_bcT"], 1)
                    act.activation(sp_[o][:, :], sp_[o][:, :], ACT.Ln, bias=1.0).then_inc(S["c_sp_"], 1)
                if have(2):
                    act.wait_ge(S["c_in_ps"], n + 3)
                    act.activation(xpad[l][:, 3:3 + NT], ps[:, IN, 0:NT], ACT.Copy).then_inc(S["c_xpad"], 1)
                if have(0):
                    act.wait_ge(S["c_wt_ps"], n + 1)
                    act.activation(flat3(wendT[l][:, :, :]), ps[:, STATE, 0:NT], ACT.Copy).then_inc(S["c_wendT"], 1)
                    act.wait_ge(S["c_wall"], n + 1)
                    act.activation(d0[l][:, :, 1:NCH], dec[l][:, 1, 1:NCH, CH - 1].unsqueeze(1)
                                   .to_broadcast([P, DS, NCH - 1]), ACT.Copy).then_inc(S["c_d0"], 1)
                if have(1):
                    act.activation(xd[o][:, :], xs[o][:, :], ACT.Copy, scale=vec("D_param")).then_inc(S["c_xd"], 1)
                if have(2):
                    act.activation(zs[(q + 2) % 4][:, :], ps[:, IN, NT:2 * NT], ACT.Silu).then_inc(S["c_zs_"], 1)
                    act.wait_ge(S["c_cv_"], n + 3)
                    act.activation(xs[l][:, :], cv[l][:, :], ACT.Silu).then_inc(S["c_xs_"], 1)
                if have(0):
                    act.wait_ge(S["c_hs"], n + 1)
                    act.activation(hc[l][:, 1:NCH, :], hs[l][:, :, 0:NCH - 1].rearrange("p n c -> p c n"),
                                   ACT.Copy).then_inc(S["c_hc"], 1)
                if have(1):
                    act.wait_ge(S["c_dt_"], n + 2)
                    act.activation(dec[o][:, 0, :, :].rearrange("p c t -> p (c t)"), dt[o][:, :], ACT.Exp, scale=negA[:, :])
                    act.activation(dec[o][:, 1, :, :].rearrange("p c t -> p (c t)"), cdt[o][:, :], ACT.Exp,
                                   scale=negA[:, :]).then_inc(S["c_dec"], 1)
                if have(0):
                    act.wait_ge(S["c_hct_ps"], n + 1)
                    act.activation(flat3(hcT[l][:, :, :]), ps[:, STATE, :], ACT.Copy).then_inc(S["c_hcT"], 1)

            pipelined(act, step_c, 3, 2, NB, 4)
            def step_d(n, q, have):
                chain.clear()

                def high(dst, l, m, ready, done):
                    act.wait_ge(ready, blocks_done(n, l, m))
                    act.activation(dst[l][:, m, :], hid[l][:, m, :], ACT.Copy).then_inc(done, 1)

                if have(0):
                    for l in LANES:
                        for m in range(HID):
                            act.wait_ge(m_gu_ps, blocks_done(n, l, m))
                            if m >= 2:
                                act.wait_ge(m_raw, blocks_done(n, l, m - 2))
                            act.activation(gate[l][m % 2][:, :], bank(l, 2 * (1 - m % 2)), ACT.Silu,
                                           scale=vec("w1_s", m)).then_inc(m_gate, 1)
                            if m >= 1:
                                high(h0_h, l, m - 1, m_raw, m_high)
                        high(h0_h, l, HID - 1, m_raw, m_high)
                    for l in LANES:
                        for m in range(HID):
                            act.wait_ge(m_h1_ps, blocks_done(n, l, m))
                            chain.link(act.activation(hid[l][:, m, :], bank(l, m), ACT.Gelu, scale=vec("h1_s", m)))
                            act.activation(h1_h[l][:, m, :], hid[l][:, m, :], ACT.Copy).then_inc(m_h1_high, 1)
                    for l in LANES:
                        for m in range(HID):
                            act.wait_ge(m_h2_ps, blocks_done(n, l, m))
                            act.activation(hid[l][:, m, :], bank(l, m), ACT.Gelu, scale=vec("h2_s", m)).then_inc(m_h2, 1)
                if have(1):
                    for l in LANES:
                        act.wait_ge(S["d_t_ps"], n * 2 + (l + 3))
                        act.activation(d_xh[l][:, :], bank(l, 1), ACT.Copy).then_inc(S["d_xh"], 1)

            pipelined(act, step_d, 1, 1, ITER_MLP, 1)

        @block.vector
        def _(dve):
            chain = Chain(dve, dve_chain)
            dve.wait_ge(w_loaded["a"], W_ALL["a"])
            for dst, src in zip((rep[:, :], band[:, :], same[:, :], negsel[:, :, :]),
                                (stage_f[0][:, :], stage_f[1][:, :], stage_f[2][:, :], stage_f[3][:, :, :])):
                dve.tensor_copy(dst, src).then_inc(cast_ready, 1)

            def split(dst_h, dst_l, src, done, before):
                dve.tensor_copy(dst_h, src).then_inc(done, 1)
                dve.wait_ge(done, before + 1)
                dve.tensor_tensor(dst_l, src, dst_h.bitcast(F32), ALU.subtract).then_inc(done, 1)

            def low_part(l, b, n, high, done):
                dve.wait_ge(high, n)
                dve.tensor_tensor(xl[l][:, :], ps[:, b, 0:NT], xh[l][:, :].bitcast(F32), ALU.subtract).then_inc(done, 1)

            def in_parts(l):
                f, r, p = qk[l][:, :, :], rest[l][:, :, :], parts[l]
                chain.link(dve.tensor_copy(p[:, 0, :, :], f))
                chain.link(dve.tensor_tensor(r, f, p[:, 0, :, :], ALU.subtract))
                chain.link(dve.tensor_copy(p[:, 1, :, :], r))
                chain.link(dve.tensor_tensor(p[:, 2, :, :], r, p[:, 1, :, :], ALU.subtract))

            def four_heads(l, which, done):
                src = parts[l][:, :, which, :].rearrange("p k (j s) -> p k j s", s=BLK)
                for h in range(4):
                    last = dve.tensor_scalar(hbd[l][:, :, :, h, :], src, headmask[:, h:h + 1], None, ALU.mult)
                last.then_inc(done, 1)

            def values(l, b, done):
                chain.link(dve.transpose(vT[l][:, :], ps[:, b + 2, 0:NT]))
                dve.tensor_tensor(flat3(vbd[l][:, :, :]).rearrange("p (k h c) -> p k h c", h=4, c=HD),
                                  vT[l][:, :].rearrange("p (k c) -> p k c", c=HD).unsqueeze(2).to_broadcast([P, 4 * NBLK, 4, HD]),
                                  vmask[:, :].rearrange("p (h c) -> p h c", c=HD).unsqueeze(1).to_broadcast([P, 4 * NBLK, 4, HD]),
                                  ALU.mult).then_inc(done, 1)

            def blocks(t):
                return t.rearrange("p (b d) -> p b d", d=D)

            def step_a(n, l, have):
                chain.clear()
                o = 1 - l
                if have(-1):
                    dve.wait_ge(S["a_y_ps"], n)
                    dve.wait_ge(S["a_xb"], n)
                    dve.tensor_tensor(t_y[o][:, :, :], blocks(bank(o, 3, 0, NT)), t_xb[o][:, :, :], ALU.add
                                      ).then_inc(S["a_y"], 1)
                    dve.wait_ge(S["a_y"], n)
                    a_ln2.stats(dve, chain, lambda b: t_y[o][:, b, :], o)
                if have(2):
                    if isinstance(n, int):
                        dve.wait_ge(x_loaded[l], 16 * ((n + 2) // 2 + 1))
                    else:
                        dve.wait_ge(x_loaded[l], n * 8 + (32 - 8 * l))
                    a_ln1.stats(dve, chain, lambda b: xblk(x, n * 2, 4 + b), l)
                    if have(0):
                        dve.wait_ge(S["a_xb"], n + 1)
                    a_ln1.apply(dve, lambda b: t_xn[l][:, b, :], lambda b: xblk(x, n * 2, 4 + b), l,
                                n + 3).then_inc(S["a_xn"], 1)
                if have(-1):
                    a_ln2.apply(dve, lambda b: t_zn[o][:, b, :], lambda b: t_y[o][:, b, :], o, n).then_inc(S["a_zn"], 1)
                if have(1):
                    dve.wait_ge(S["a_qT"], n + 2)
                    in_parts(o)
                    four_heads(o, 1, S["a_hbd"])
                    dve.wait_ge(S["a_v_ps"], n + 2)
                    values(o, 4 * o, S["a_vbd"])
                if have(-1):
                    dve.wait_ge(S["a_z"], n)
                    a_ln3.stats(dve, chain, lambda b: t_z[o][:, b, :], o)
                    a_ln3.apply(dve, lambda b: t_o[o][:, b, :], lambda b: t_z[o][:, b, :], o, n).then_inc(S["a_o"], 1)
                if have(2):
                    low_part(l, 4 * o + 3, n + 3, S["a_xh"], S["a_xl"])

            split(wa_h[:, :, :], wa_l[:, :, :], wa[:, 0:3, :], split_done, 0)
            dve.wait_ge(w_loaded["b"], W_ALL["b"])
            split(wf_h[:, :, :], wf_l[:, :, :], wf[:, 0:3, :], split_done, 2)
            pipelined(dve, step_a, 2, 1, NB)

            def step_b(n, l, have):
                chain.clear()
                o = 1 - l
                if have(2):
                    dve.wait_ge(S["b_s_ps"], n + 3)
                    sc = ps[:, 0:4, 0:NT].rearrange("p g (j s) -> p g j s", s=BLK)
                    m4 = mx[l][:, :].rearrange("p (g j) -> p g j", j=NBLK)
                    chain.link(dve.tensor_reduce(m4, sc, AX.X, ALU.max))
                    dve.tensor_tensor(sm[l][:, :, :].rearrange("p (g j) s -> p g j s", j=NBLK), sc,
                                      m4.unsqueeze(3).to_broadcast([P, G, NBLK, BLK]), ALU.subtract).then_inc(S["b_sm"], 1)
                if have(-1):
                    dve.wait_ge(e_done, n * NE)
                    chain.link(dve.tensor_tensor(t_yo[o][:, :, :], blocks(ps[:, ACC, 0:NT]), t_h[o][:, :, :], ALU.add))
                    dve.sem_inc(b_sum_read, 1)
                    b_ln2.stats(dve, chain, lambda b: t_yo[o][:, b, :], o)
                if have(3):
                    low_part(o, 3, n + 4, S["b_xh"], S["b_xl"])
                if have(-1):
                    b_ln2.apply(dve, lambda b: t_on[o][:, b, :], lambda b: t_yo[o][:, b, :], o, n).then_inc(S["b_on"], 1)
                if have(1):
                    dve.wait_ge(S["b_y_ps"], n + 2)
                    chain.link(dve.tensor_tensor(t_y[o][:, :, :], blocks(ps[:, LATE, 0:NT]), t_xb[o][:, :, :], ALU.add))
                    b_ln1.stats(dve, chain, lambda b: t_y[o][:, b, :], o)
                if have(3):
                    dve.wait_ge(S["b_kT"], n + 4)
                    in_parts(o)
                if have(1):
                    b_ln1.apply(dve, lambda b: t_zn[o][:, b, :], lambda b: t_y[o][:, b, :], o, n + 2).then_inc(S["b_zn"], 1)
                if have(3):
                    four_heads(o, 0, S["b_hbd"])
                    dve.wait_ge(S["b_v_ps"], n + 4)
                    values(o, 0, S["b_vbd"])
                if have(4):
                    if isinstance(n, int):
                        dve.wait_ge(x_loaded[l], 16 * ITER + 32 * ((n + 4) // 2 + 1))
                    else:
                        dve.wait_ge(x_loaded[l], n * 16 + (16 * ITER + 96 - 16 * l))
                    b_ln0.stats(dve, chain, lambda b: xblk(xB, n * 2, 8 + b), l)
                if have(-1):
                    dve.wait_ge(S["b_z"], n)
                    b_ln3.stats(dve, chain, lambda b: t_z[o][:, b, :], o)
                if have(4):
                    if have(2):
                        dve.wait_ge(S["b_xb"], n + 3)
                    b_ln0.apply(dve, lambda b: t_xn[l][:, b, :], lambda b: xblk(xB, n * 2, 8 + b), l,
                                n + 5).then_inc(S["b_xn"], 1)
                if have(-1):
                    b_ln3.apply(dve, lambda b: t_o[o][:, b, :], lambda b: t_z[o][:, b, :], o, n).then_inc(S["b_o"], 1)
                if have(1):
                    dve.wait_ge(S["b_l_ps"], n + 2)
                    chain.link(dve.tensor_tensor(lg[o][:, :, :], ps[:, LATE, 0:2 * NE].rearrange("p (b e) -> p b e", e=NE),
                                                 router_b[:, :, :], ALU.add))
                    chain.link(dve.tensor_reduce(lmx[o][:, :], lg[o][:, :, :], AX.X, ALU.max))
                    dve.tensor_tensor(lg[o][:, :, :], lg[o][:, :, :], lmx[o][:, :].unsqueeze(2).to_broadcast([P, 2, NE]),
                                      ALU.subtract).then_inc(S["b_lg"], 1)
                if have(2):
                    dve.wait_ge(S["b_ex"], n + 3)
                    chain.link(dve.tensor_reduce(den[l][:, :], ex[l][:, :, :], AX.X, ALU.add))
                    dve.reciprocal(rden[l][:, :], den[l][:, :]).then_inc(S["b_rden"], 1)
                if have(1):
                    dve.wait_ge(S["b_le"], n + 2)
                    dve.tensor_copy(lg[o][:, :, :], le[o][:, :, :])
                    for b in range(2):
                        last = dve.max(m8[o][:, b, :], le[o][:, b, :])
                    chain.link(last)
                    for b in range(2):
                        last = dve.max_index(ix[o][:, b, :], m8[o][:, b, :], le[o][:, b, :])
                    chain.link(last)
                    chain.link(dve.tensor_tensor(pick[o][:, :], ix[o][:, :, 0], ix[o][:, :, 1], ALU.max))
                    for b in range(2):
                        last = dve.tensor_scalar(hot[o][:, b, :], iota[:, :], pick[o][:, b:b + 1], None, ALU.is_equal)
                    last.then_inc(S["b_hot"], 1)
                if have(2):
                    dve.wait_ge(S["b_p"], n + 3)
                    dve.transpose(flat3(pT[l][:, :, :]), flat3(sm[l][:, :, :])).then_inc(S["b_pT"], 1)

            dve.wait_ge(S["a_x"], NB)
            pipelined(dve, step_b, 4, 1, NB)
            dve.wait_ge(S["b_stored"], 32 * NB)
            dve.wait_ge(w_loaded["c"], W_ALL["c"])
            dve.wait_ge(zero_ready, 2)
            dve.wait_ge(expA_ready, 1)
            dve.tensor_scalar(negA[:, :], expA[:, :], -1.0, None, ALU.mult).then_inc(negA_ready, 1)
            def step_c(n, q, have):
                chain.clear()
                l, o = q % 2, 1 - q % 2
                if have(0):
                    dve.wait_ge(S["c_dec"], n + 1)
                    flat = dec[l][:, :, :, :].rearrange("p a c t -> p (a c t)")
                    chain.link(dve.tensor_scalar(flat, flat, 1.0, None, ALU.min))
                    for j in range(1, CH):
                        w0 = wall[l][:, OFF[j - 1]:OFF[j]].rearrange("p (c t) -> p c t", t=CH - j + 1)
                        w1 = wall[l][:, OFF[j]:OFF[j + 1]].rearrange("p (c t) -> p c t", t=CH - j)
                        ins = dve.tensor_tensor(w1, dec[l][:, 0, :, j:CH], w0[:, :, 0:CH - j], ALU.mult)
                        if j < CH - 1:
                            chain.link(ins)
                    ins.then_inc(S["c_wall"], 1)
                if have(1):
                    dve.wait_ge(S["c_dt_ps"], n + 2)
                    dve.tensor_scalar(zb[o][:, :], ps[:, DT, 0:NT], vec("dt_b"), None, ALU.add).then_inc(S["c_zb_"], 1)
                if have(2):
                    dve.wait_ge(S["c_r2"], n + 3)
                    c_ln1.apply(dve, lambda b: c_xq[l][:, b, :], lambda b: xblk(x, n * 2, 4 + b), l, n + 3,
                                scale=c_r2).then_inc(S["c_xn_"], 1)
                if have(-1):
                    dve.wait_ge(S["c_yi_ps"], n)
                    chain.link(dve.tensor_tensor(yi[o][:, :], ps[:, STATE, 0:NT],
                                                 dec[o][:, 1, :, :].rearrange("p c t -> p (c t)"), ALU.mult))
                    dve.wait_ge(S["c_ys"], n)
                    chain.link(dve.tensor_tensor(yi[o][:, :], yi[o][:, :], term[o][:, 0:NT], ALU.add))
                    dve.wait_ge(S["c_zs_"], n)
                    dve.tensor_tensor(ya[o][:, :], yi[o][:, :], zs[(q - 1) % 4][:, :], ALU.mult).then_inc(S["c_y"], 1)
                if have(0):
                    dve.wait_ge(S["c_wall"], n + 1)
                    dve.wait_ge(S["c_g1_ps"], n + 1)
                    for b, (j0, j1) in enumerate(PAIR_BANKS):
                        ins = dve.tensor_tensor(term[l][:, OFF[j0]:OFF[j1]], wall[l][:, OFF[j0]:OFF[j1]],
                                                ps[:, PAIRS + b, 0:OFF[j1] - OFF[j0]], ALU.mult)
                    ins.then_inc(S["c_term"], 1)
                if have(1):
                    dve.wait_ge(S["c_c_ps"], n + 2)
                    dve.tensor_tensor(flat3(bbd[o][:, :, :]), ps[:, BR, :], bmask[:, :, :, :].rearrange("p k n c -> p (k n c)"),
                                      ALU.mult).then_inc(S["c_bbd"], 1)
                    dve.tensor_tensor(cbd[o][:, :], ps[:, DT, NT:2 * NT], cmask[:, :], ALU.mult).then_inc(S["c_cbd"], 1)
                if have(3):
                    if isinstance(n, int):
                        dve.wait_ge(x_loaded[o], 48 * ITER + 16 * ((n + 3) // 2 + 1))
                    else:
                        dve.wait_ge(x_loaded[o], n * 8 + (48 * ITER + (40 if o == 0 else 32)))
                    c_ln1.stats(dve, chain, lambda b: xblk(x, n * 2, 6 + b), o)
                if have(-2):
                    c_ln2.apply(dve, lambda b: c_o[l][:, b, :], lambda b: c_r[l][:, b, :], l, n - 1).then_inc(S["c_o_"], 1)
                if have(2):
                    dve.wait_ge(S["c_xpad"], n + 3)
                    chain.link(dve.tensor_scalar(cv[l][:, :], xpad[l][:, 3:3 + NT], vec("conv_w", 3), vec("conv_b"),
                                                 ALU.mult, ALU.add))
                    for k in (2, 1, 0):
                        ins = dve.scalar_tensor_tensor(out=cv[l][:, :], in0=xpad[l][:, k:k + NT], scalar=vec("conv_w", k),
                                                       in1=cv[l][:, :], op0=ALU.mult, op1=ALU.add)
                        if k:
                            chain.link(ins)
                    ins.then_inc(S["c_cv_"], 1)
                if have(0):
                    dve.wait_ge(S["c_d0"], n + 1)
                    dve.wait_ge(S["c_st_ps"], n + 1)
                    dve.tensor_tensor_scan(flat3(hs[l][:, :, :]), flat3(d0[l][:, :, :]), ps[:, STATE, :], 0.0,
                                           ALU.mult, ALU.add).then_inc(S["c_hs"], 1)
                if have(1):
                    dve.wait_ge(S["c_sp_"], n + 2)
                    chain.link(dve.scalar_tensor_tensor(out=dt[o][:, :], in0=zb[o][:, :], scalar=0.0, in1=sp_[o][:, :],
                                                        op0=ALU.max, op1=ALU.add))
                    dve.tensor_tensor_scan(cdt[o][:, :], first[:, :], dt[o][:, :], 0.0, ALU.mult, ALU.add
                                           ).then_inc(S["c_dt_"], 1)
                    dve.tensor_tensor(wall[o][:, 0:NT], dt[o][:, :], xs[o][:, :], ALU.mult)
                if have(-1):
                    dve.wait_ge(S["c_out_ps"], n)
                    chain.link(dve.tensor_tensor(c_r[o][:, :, :], blocks(ps[:, DT, 0:NT]), c_xn[(q - 1) % 4][:, :, :],
                                                 ALU.add))
                    c_ln2.stats(dve, chain, lambda b: c_r[o][:, b, :], o)
                if have(3):
                    c_ln1.apply(dve, lambda b: c_xn[(q + 3) % 4][:, b, :], lambda b: xblk(x, n * 2, 6 + b), o, n + 4)

            pipelined(dve, step_c, 3, 2, NB, 4)
            dve.wait_ge(w_loaded["d"], W_ALL["d"])
            dve.wait_ge(S["c_x"], NB)
            def step_d(n, q, have):
                chain.clear()

                def low(dst, high_part, l, m, high, done):
                    dve.wait_ge(high, blocks_done(n, l, m))
                    dve.tensor_tensor(dst[l][:, m, :], hid[l][:, m, :], high_part[l][:, m, :].bitcast(F32), ALU.subtract
                                      ).then_inc(done, 1)

                for l in LANES:
                    if have(0):
                        for m in range(HID):
                            dve.wait_ge(m_gate, blocks_done(n, l, m))
                            dve.scalar_tensor_tensor(out=hid[l][:, m, :], in0=bank(l, 2 * (1 - m % 2) + 1),
                                                     scalar=vec("w2_s", m), in1=gate[l][m % 2][:, :], op0=ALU.mult,
                                                     op1=ALU.mult).then_inc(m_raw, 1)
                            if m >= 1:
                                low(h0_l, h0_h, l, m - 1, m_high, m_h0)
                        low(h0_l, h0_h, l, HID - 1, m_high, m_h0)
                if have(-1):
                    for l in LANES:
                        d_ln2.stats(dve, chain, lambda b: d_y[l][:, b, :], l)
                    for l in LANES:
                        d_ln2.apply(dve, lambda b: d_o[l][:, b, :], lambda b: d_y[l][:, b, :], l,
                                    n * 2 + (l - 1)).then_inc(S["d_o_"], 1)
                if have(1):
                    for l in LANES:
                        d_ln1.stats(dve, chain, lambda b: xblk(x, n * 8, 8 + 4 * l + b), l)
                    for l in LANES:
                        d_ln1.apply(dve, lambda b: d_xn[l][:, b, :], lambda b: xblk(x, n * 8, 8 + 4 * l + b), l,
                                    n * 2 + (l + 3)).then_inc(S["d_xn_"], 1)
                if have(0):
                    for l in LANES:
                        for m in range(HID):
                            low(h1_l, h1_h, l, m, m_h1_high, m_h1)
                for l in LANES:
                    if have(0):
                        dve.wait_ge(S["d_y_ps"], n * 2 + (l + 1))
                        chain.link(dve.tensor_tensor(flat3(d_y[l][:, :, :]), bank(l, 0), flat3(w3_s[:, :, :]), ALU.mult))
                    if have(1):
                        dve.wait_ge(S["d_xh"], n * 2 + (l + 3))
                        dve.tensor_tensor(d_xl[l][:, :], bank(l, 1), d_xh[l][:, :].bitcast(F32), ALU.subtract
                                          ).then_inc(S["d_xl"], 1)

            pipelined(dve, step_d, 1, 1, ITER_MLP, 1)

        @block.tensor
        def _(pe):
            pe.wait_ge(w_loaded["a"], W_ALL["a"])
            pe.wait_ge(cast_ready, 4)

            def turn(b, src, k, ready, n, done):
                pe.wait_ge(ready, n)
                for c in range(k):
                    last = pe.transpose(ps[:, b, P * c:P * c + P], src[:, c, :], ident[:, :])
                last.then_inc(done, 1)

            def product(dst, a_h, a_l, b_h, b_l, start):
                pe.matmul(dst, a_h, b_h, start=start, stop=True, skip_group_check=True)
                pe.matmul(dst, a_l, b_h, start=False, stop=True, skip_group_check=True)
                return pe.matmul(dst, a_h, b_l, start=False, stop=True, skip_group_check=True)

            def project(l, b, w_h, w_l, qk_ps, v_ps):
                for k, done in ((0, None), (1, qk_ps), (2, v_ps)):
                    last = product(ps[:, b + k, 0:NT], w_h[:, k, :], w_l[:, k, :], xh[l][:, :], xl[l][:, :], True)
                    if done is not None:
                        last.then_inc(done, 1)

            def score(l, dst, g, j, w, moving):
                for k, m in ((0, 0), (0, 1), (1, 0), (1, 1), (0, 2), (2, 0)):
                    last = pe.matmul(dst, hbd[l][heads(g), k, j, :, :].rearrange("p h s -> p (h s)"),
                                     parts[l][heads(g), m, moving, BLK * j:BLK * j + w], start=False, stop=True,
                                     skip_group_check=True)
                return last

            def out_tokens(b, src, w, done):
                for c in range(2):
                    last = pe.matmul(ps[:, b, P * c:P * c + P], src[:, P * c:P * c + P], w, start=True, stop=True)
                last.then_inc(done, 1)

            def step_a(n, l, have):
                o = 1 - l
                if have(1):
                    pe.wait_ge(S["a_xl"], n + 2)
                    project(o, 4 * o, wa_h, wa_l, S["a_qk_ps"], S["a_v_ps"])
                if have(0):
                    pe.wait_ge(S["a_qT"], n + 1)
                    pe.wait_ge(S["a_hbd"], n + 1)
                    pe.wait_ge(S["a_vbd"], n + 1)
                    for g in range(G):
                        pe.matmul(bank(l, g, 0, NBLK * SPAN), rep[heads(g), :], band[heads(g), :], start=True, stop=True)
                    for g in range(G):
                        for j in range(NBLK):
                            w = SPAN if j < NBLK - 1 else BLK
                            last = score(l, bank(l, g, SPAN * j, SPAN * j + w), g, j, w, 0)
                        if g % 2 == 1:
                            last.then_inc(S["a_s_ps"], 1)
                if have(2):
                    if have(-1):
                        pe.wait_ge(S["a_y"], n)
                    turn(4 * o + 3, t_xn[l], 2, S["a_xn"], n + 3, S["a_t_ps"])
                if have(0):
                    for g in range(G):
                        if g % 2 == 0:
                            pe.wait_ge(S["a_tau"], n * 2 + (g // 2 + 1))
                        for j in range(NBLK):
                            w = SPAN if j < NBLK - 1 else BLK
                            last = pe.matmul(ps[heads(g), 4 * l, BLK * j:BLK * j + w], vbd[l][:, j, heads(g)],
                                             tau[l][:, g, SPAN * j:SPAN * j + w], start=(j == 0),
                                             stop=True, skip_group_check=True)
                    last.then_inc(S["a_m_ps"], 1)
                    pe.wait_ge(S["a_msgT"], n + 1)
                    out_tokens(4 * l + 3, msgT[l], wa[:, 3, :], S["a_y_ps"])

            pe.wait_ge(split_done, 4)
            pipelined(pe, step_a, 2, 1, NB)

            def expert(n, l, e):
                if e < NE:
                    if e >= 2:
                        pe.wait_ge(he_ready, n * NE + (e - 1))
                    bk = ps[:, HE + e % 2, 0:NT]
                    pe.matmul(bk, negsel[:, e, :], hotTb[l][:, :], start=True, stop=False)
                    pe.matmul(bk, w_e1[:, e, :], hT[l][:, :], start=False, stop=True).then_inc(he_ps, 1)
                if e > 0:
                    pe.wait_ge(he_ready, n * NE + e)
                    for c in range(2):
                        last = pe.matmul(ps[:, ACC, P * c:P * c + P], he[(e - 1) % 2][:, P * c:P * c + P],
                                         w_e2[:, e - 1, :], start=False, stop=True, skip_group_check=True)
                    last.then_inc(e_done, 1)

            def step_b(n, l, have):
                o = 1 - l
                if have(0):
                    pe.wait_ge(S["b_hot"], n + 1)
                    for c in range(2):
                        last = pe.transpose(ps[0:NE, LATE, P * c:P * c + P], hot[l][:, c, :], ident[:, :])
                    last.then_inc(S["b_hott_ps"], 1)
                if have(1):
                    pe.wait_ge(S["b_pT"], n + 2)
                    if have(0):
                        pe.wait_ge(S["b_hotT"], n + 1)
                    for j in range(NBLK):
                        for g in range(G):
                            last = pe.matmul(ps[heads(g), LATE, BLK * j:BLK * j + BLK], vbd[o][:, j, heads(g)],
                                             pT[o][:, g, BLK * j:BLK * j + BLK], start=True, stop=True)
                    last.then_inc(S["b_m_ps"], 1)
                if have(3):
                    if have(2):
                        pe.wait_ge(S["b_sm"], n + 3)
                    turn(3, t_xn[o], 2, S["b_xn"], n + 4, S["b_t_ps"])
                if have(1):
                    pe.wait_ge(S["b_msgT"], n + 2)
                    out_tokens(LATE, msgT[o], wf[:, 3, :], S["b_y_ps"])
                if have(3):
                    pe.wait_ge(S["b_xl"], n + 4)
                    project(o, 0, wf_h, wf_l, S["b_qk_ps"], S["b_v_ps"])
                if have(0):
                    pe.wait_ge(S["b_hotT"], n + 1)
                    if have(-1):
                        pe.wait_ge(b_sum_read, n)
                    for c in range(2):
                        pe.matmul(ps[:, ACC, P * c:P * c + P], hotT[l][:, P * c:P * c + P], b_e2[:, :],
                                  start=(c == 0), stop=True, skip_group_check=True)
                    for e in range(0, 4):
                        expert(n, l, e)
                if have(1):
                    turn(LATE, t_h[o], 2, S["b_h"], n + 2, S["b_ht_ps"])
                if have(0):
                    expert(n, l, 4)
                    expert(n, l, 5)
                if have(1):
                    pe.wait_ge(S["b_hT"], n + 2)
                    for c in range(2):
                        last = pe.matmul(ps[:, LATE, NE * c:NE * c + NE], hT[o][:, P * c:P * c + P], w_router[:, :],
                                         start=True, stop=True)
                    last.then_inc(S["b_l_ps"], 1)
                if have(0):
                    for e in (6, 7, 8):
                        expert(n, l, e)
                if have(3):
                    pe.wait_ge(S["b_kT"], n + 4)
                    pe.wait_ge(S["b_hbd"], n + 4)
                    pe.wait_ge(S["b_vbd"], n + 4)
                    for g in range(G):
                        pe.matmul(ps[:, g, 0:NT], rep[heads(g), :], same[heads(g), :], start=True, stop=True)
                    for j in range(NBLK):
                        for g in range(G):
                            last = score(o, ps[:, g, BLK * j:BLK * j + BLK], g, j, BLK, 1)
                    last.then_inc(S["b_s_ps"], 1)

            pe.wait_ge(w_loaded["b"], W_ALL["b"])
            pe.wait_ge(S["a_x"], NB)
            pipelined(pe, step_b, 4, 1, NB)
            pe.wait_ge(w_loaded["c"], W_ALL["c"])
            def step_c(n, q, have):
                l, o = q % 2, 1 - q % 2
                if have(1):
                    pe.wait_ge(S["c_xs_"], n + 2)
                    if have(-2):
                        pe.wait_ge(c_ln2.mv_ready, n - 1)
                    pe.matmul(ps[:, DT, 0:NT], w_dt[:, :], xs[o][:, :], start=True, stop=True).then_inc(S["c_dt_ps"], 1)
                    pe.matmul(ps[0:DS, BC, 0:NT], w_b[:, :], xs[o][:, :], start=True, stop=True)
                    pe.matmul(ps[0:DS, BC, NT:2 * NT], w_c[:, :], xs[o][:, :], start=True, stop=True
                              ).then_inc(S["c_b_ps"], 1)
                if have(-1):
                    pe.wait_ge(S["c_hcT"], n)
                    pe.wait_ge(S["c_cbd"], n)
                    for c in range(4):
                        last = pe.matmul(ps[:, STATE, 64 * c:64 * c + 64], hcT[o][:, c, :], cbd[o][:, 64 * c:64 * c + 64],
                                         start=True, stop=True)
                    last.then_inc(S["c_yi_ps"], 1)
                if have(2):
                    if have(1):
                        pe.wait_ge(S["c_zs_"], n + 2)
                    turn(IN, c_xq[l], 2, S["c_xn_"], n + 3, S["c_t_ps"])
                if have(1):
                    for c in range(2):
                        pe.matmul(ps[:, BR, NT * c:NT * c + NT], xs[o][:, P * c:P * c + P], flat3(w_bR[:, :, :]),
                                  start=True, stop=True)
                    pe.wait_ge(S["c_zb_"], n + 2)
                    pe.matmul(ps[:, DT, NT:2 * NT], flat3(w_cR[:, :, :]), xs[o][:, :], start=True, stop=True
                              ).then_inc(S["c_c_ps"], 1)
                if have(2):
                    pe.wait_ge(S["c_xT_"], n + 3)
                    pe.matmul(ps[:, IN, 0:NT], w_in[:, 0:D], c_xT[l][:, :], start=True, stop=True)
                    pe.matmul(ps[:, IN, NT:2 * NT], w_in[:, D:2 * D], c_xT[l][:, :], start=True, stop=True
                              ).then_inc(S["c_in_ps"], 1)
                if have(0):
                    pe.wait_ge(S["c_wend"], n + 1)
                    if have(-1):
                        pe.wait_ge(S["c_y"], n)
                    for c in range(2):
                        last = pe.transpose(ps[:, STATE, P * c:P * c + P],
                                            wend[l][:, 16 * c:16 * c + 16, :].rearrange("p c t -> p (c t)"), ident[:, :])
                    last.then_inc(S["c_wt_ps"], 1)
                if have(-1):
                    pe.wait_ge(S["c_y"], n)
                    if have(1):
                        pe.wait_ge(S["c_cbd"], n + 2)
                    out_tokens(DT, ya[o], w_out[:, :], S["c_out_ps"])
                if have(0):
                    pe.wait_ge(S["c_wendT"], n + 1)
                    for c in range(2):
                        dst = ps[:, STATE, :].rearrange("p (n c) -> p n c", c=NCH)[:, :, 16 * c:16 * c + 16]
                        last = pe.matmul(dst, wendT[l][:, c, :], bbd[l][:, c, :].rearrange("p (n c) -> p n c", c=16),
                                         start=True, stop=True)
                    last.then_inc(S["c_st_ps"], 1)
                if have(1):
                    pe.wait_ge(S["c_prod"], n + 2)
                    if have(0):
                        pe.wait_ge(S["c_term"], n + 1)
                    for b, (j0, j1) in enumerate(PAIR_BANKS):
                        last = pe.matmul(ps[:, PAIRS + b, 0:OFF[j1] - OFF[j0]], ones[0:DS, :], prod[o][:, OFF[j0]:OFF[j1]],
                                         start=True, stop=True)
                    last.then_inc(S["c_g1_ps"], 1)
                if have(0):
                    pe.wait_ge(S["c_hc"], n + 1)
                    for c in range(4):
                        last = pe.transpose(ps[:, STATE, P * c:P * c + P],
                                            hc[l][:, 8 * c:8 * c + 8, :].rearrange("p c n -> p (c n)"), ident[:, :])
                    last.then_inc(S["c_hct_ps"], 1)

            pipelined(pe, step_c, 3, 2, NB, 4)
            pe.wait_ge(w_loaded["d"], W_ALL["d"])
            pe.wait_ge(m_split, 8)

            def step_d(n, q, have):
                if have(0):
                    for l in LANES:
                        pe.wait_ge(S["d_xl"], n * 2 + (l + 1))
                        for m in range(HID):
                            if m >= 2:
                                pe.wait_ge(m_raw, blocks_done(n, l, m - 2))
                            cols = slice(P * m, P * m + P)
                            for w in range(2):
                                last = product(bank(l, 2 * (1 - m % 2) + w), wm_h[:, w, cols], wm_l[:, w, cols],
                                               d_xh[l][:, :], d_xl[l][:, :], True)
                            last.then_inc(m_gu_ps, 1)
                    for w, src_h, src_l, ready, done in ((0, h0_h, h0_l, m_h0, m_h1_ps), (1, h1_h, h1_l, m_h1, m_h2_ps)):
                        for l in LANES:
                            pe.wait_ge(ready, blocks_done(n, l, HID - 1))
                            for m in range(HID):
                                for k in range(HID):
                                    last = product(bank(l, m), wh_h[:, w, k, P * m:P * m + P],
                                                   wh_l[:, w, k, P * m:P * m + P], src_h[l][:, k, :], src_l[l][:, k, :],
                                                   k == 0)
                                last.then_inc(done, 1)
                for l in LANES:
                    if have(0):
                        pe.wait_ge(m_h2, blocks_done(n, l, HID - 1))
                        for c in range(4):
                            for k in range(HID):
                                last = pe.matmul(bank(l, 0, P * c, P * c + P), hid[l][:, k, P * c:P * c + P],
                                                 w_m3[:, k, :], start=(k == 0), stop=(k == HID - 1))
                        last.then_inc(S["d_y_ps"], 1)
                    if have(1):
                        turn(4 * l + 1, d_xn[l], 4, S["d_xn_"], n * 2 + (l + 3), S["d_t_ps"])

            pipelined(pe, step_d, 1, 1, ITER_MLP, 1)



def lay_out(inp):
    import numpy as np
    f = np.float32
    v = {k: np.asarray(t) for k, t in inp.items()}
    p = np.arange(P)
    r = {"x": v["L0_attn_x"]}
    wkv = v["L0_attn_wkv"].reshape(16, 2, HD, D)
    by_head = lambda t: t.reshape(D, G, 4, HD).transpose(0, 2, 1, 3).reshape(D, D)
    r["wa"] = np.stack([v["L0_attn_wq"].T, wkv[:, 0].reshape(D, D).T, by_head(wkv[:, 1].reshape(D, D).T),
                        v["L0_attn_wo"].T], 1)
    wi = v["L0_ffn_in_proj_w"]
    r["wf"] = np.stack([wi[0:D].T, wi[D:2 * D].T, by_head(wi[2 * D:].T), v["L0_ffn_out_w"].T], 1)
    r["w_router"] = v["L0_ffn_router_w"].T
    r["w_e1"] = v["L0_ffn_w1"].transpose(2, 0, 1)
    r["w_e2"] = v["L0_ffn_w2"].transpose(2, 0, 1)
    r["b_e2"] = v["L0_ffn_b2"]
    r["rows"] = np.broadcast_to(np.stack([v[n] for n in (
        "L0_attn_gamma", "L0_attn_beta", "L0_ffn_out_b", "L0_ffn_ln1_g", "L0_ffn_ln1_b", "L0_ffn_ln2_g",
        "L0_ffn_ln2_b")])[None, :, None, :], (P, 7, 2, D))
    r["router_b"] = np.broadcast_to(v["L0_ffn_router_b"][None, None, :], (P, 2, NE))
    bi = v["L0_ffn_in_proj_b"].reshape(3, D)
    blk = lambda t: t.reshape(HID, P).T
    cols = {"bq": bi[0][:, None], "bk": bi[1][:, None], "bv": bi[2][:, None], "b1": v["L0_ffn_b1"].T,
            "ln_g": v["L1_attn_ln_g"][:, None], "ln_b": v["L1_attn_ln_b"][:, None], "conv_w": v["L1_attn_conv_w"][:, 0, :],
            "conv_b": v["L1_attn_conv_b"][:, None], "dt_b": v["L1_attn_dt_b"][:, None],
            "log_A": v["L1_attn_log_A"][:, None], "D_param": v["L1_attn_D_param"][:, None],
            "w1_s": blk(v["L1_ffn_w1_s"]), "w2_s": blk(v["L1_ffn_w2_s"]), "h1_s": blk(v["L1_ffn_h1_s"]),
            "h2_s": blk(v["L1_ffn_h2_s"])}
    r["pp"] = np.concatenate([cols[n] for n in PP], 1)
    r["w_in"], r["w_dt"], r["w_b"], r["w_c"], r["w_out"] = (
        v["L1_attn_" + n] for n in ("W_in", "dt_w", "B_w", "C_w", "W_out"))
    r["w_bR"] = np.broadcast_to(v["L1_attn_B_w"][:, :, None], (D, DS, 16))
    r["w_cR"] = np.broadcast_to(v["L1_attn_C_w"][:, None, :], (D, 8, DS))
    r["w_m1"], r["w_m2"] = v["L1_ffn_w1_w"].T, v["L1_ffn_w2_w"].T
    for n, k in (("w_h1", "h1_w"), ("w_h2", "h2_w"), ("w_m3", "w3_w")):
        t = v["L1_ffn_" + k].T
        r[n] = t.reshape(HID, P, t.shape[1]).transpose(1, 0, 2)
    r["w3_s"] = np.broadcast_to(v["L1_ffn_w3_s"][None, None, :], (P, HID, D))
    r["c_ident"] = np.eye(P, dtype=f)
    r["c_headmask"] = (p[:, None] // HD % 4 == np.arange(4)[None, :]).astype(f)
    r["c_vmask"] = (p[:, None] // BLK == np.arange(BLK)[None, :] // HD).astype(f)
    r["c_rep"] = (p[:, None] % BLK == p[None, :] % BLK).astype(f)
    gap = np.arange(SPAN)[None, :] - (p % BLK)[:, None]
    r["c_band"] = np.tile(np.where((gap >= 1) & (gap <= WIN), 0.0, NEG).astype(f), (1, NBLK))
    own = (p % BLK)[:, None] // NB == np.arange(BLK)[None, :] // NB
    r["c_same"] = np.tile(np.where(own, 0.0, NEG).astype(f), (1, NBLK))
    e = np.arange(NE)
    r["c_negsel"] = np.where(e[:, None, None] == e[None, :, None], 0.0, NEG).astype(f) * np.ones((1, 1, P), f)
    r["c_iota"] = np.broadcast_to(e.astype(f), (P, NE))
    r["c_bmask"] = np.broadcast_to((p[:, None] // CH == np.arange(16)[None, :]).astype(f)[:, None, None, :], (P, 2, DS, 16))
    r["c_cmask"] = (p[:, None] // DS == np.arange(NT)[None, :] % 64 // CH).astype(f)
    r["c_first"] = np.broadcast_to((np.arange(NT) % CH != 0).astype(f), (P, NT))
    return {k: np.ascontiguousarray(t) for k, t in r.items()}


def kernel(**inputs):
    import concourse.bacc as _bacc
    from concourse import mybir as _mybir
    from concourse.bass_utils import run_bass_kernel_spmd as _run

    nc = _bacc.Bacc("TRN2", target_bir_lowering=False, num_devices=1)
    arrays, args = {}, {}
    for name, v in lay_out(inputs).items():
        arrays[f"in_{name}"] = v
        args[name] = nc.dram_tensor(f"in_{name}", v.shape, _mybir.dt.from_np(v.dtype), kind="ExternalInput").ap()
    out = nc.dram_tensor("out_x", (NB, NT, D), F32, kind="ExternalOutput").ap()
    build(nc, args, out)
    r = _run(nc, [arrays], core_ids=[0])
    return r.results[0]["out_x"]
```
